# Optimizing a Trainium2 kernel written in Bass

```python
import numpy as np
import jax
import jax.numpy as jnp

def _softmax(x, axis=-1):
    return jax.nn.softmax(x, axis=axis)

def _gelu(x):
    return jax.nn.gelu(x, approximate=True)

def _silu(x):
    return jax.nn.silu(x)

def _sigmoid(x):
    return jax.nn.sigmoid(x)

def _layernorm(x, axis=-1, eps=1e-05):
    m = jnp.mean(x, axis=axis, keepdims=True)
    v = jnp.var(x, axis=axis, keepdims=True)
    return (x - m) / jnp.sqrt(v + eps)

def _scatter_add(tgt, idx, src, axis=0):
    return tgt.at[idx].add(src)

def _segment_sum(src, seg, n):
    return jax.ops.segment_sum(src, seg, n)
kernel_name = 'mk_decoder_postln_d2_seqx_r4_e10501'

def setup_inputs(seed: int=0):
    np.random.seed(seed)
    _w = jnp.asarray

    def _rec_inputs():
        import jax
        import jax.numpy as jnp
        _rk = jax.random.key(seed)
        x = -0.0002928 + 1 * jax.random.normal(jax.random.fold_in(_rk, 1), (4, 1024, 256), jnp.float32)
        _lenS = 1024 - jax.random.randint(jax.random.fold_in(_rk, 7), (4,), 0, max(1, 1024 // 4) + 1, jnp.int32)
        _lenS2 = 77 - jax.random.randint(jax.random.fold_in(_rk, 8), (4,), 0, max(1, 77 // 4) + 1, jnp.int32)
        _ctx_1024P = jax.random.normal(jax.random.fold_in(_rk, 11), (4, 16, 256), jnp.float32)
        _ctx_1024c = jax.random.dirichlet(jax.random.fold_in(_rk, 511), 0.3 * jnp.ones((16,), jnp.float32), (4, 77))
        _ctx_1024t = jnp.einsum('bsk,bkd->bsd', _ctx_1024c, _ctx_1024P)
        _ctx_1024t = _ctx_1024t * jax.lax.rsqrt(jnp.mean(jnp.square(_ctx_1024t)) + 1e-12) * 0.953939
        ctx_1024 = -1.39393e-06 + 0.999914 * (_ctx_1024t + 0.3 * jax.random.normal(jax.random.fold_in(_rk, 611), (4, 77, 256), jnp.float32))
        _validS = jnp.arange(1024)[None, :] < _lenS[:, None]
        _validS2 = jnp.arange(77)[None, :] < _lenS2[:, None]
        _causal = jnp.tril(jnp.ones((1024, 1024), dtype=bool))
        mask_BxS2_bk0 = jnp.logical_not(jnp.broadcast_to(_validS2[:, :], (4, 77)))
        return (x, ctx_1024, mask_BxS2_bk0)
    x, ctx_1024, mask_BxS2_bk0 = _rec_inputs()

    def _L0_attn_setup():
        import jax, jax.numpy as jnp
        import numpy as np
        N_HEADS = 16
        HIDDEN = 256
        HEAD_DIM = 64
        BSZ = 4
        SEQ = 256
        SCALE = HEAD_DIM ** (-0.5)
        key = jax.random.key(seed)
        k_x, k_q, k_k, k_v, k_o = jax.random.split(key, 5)
        s = HIDDEN ** (-0.5)
        return {'x': jax.random.normal(k_x, (BSZ, SEQ, HIDDEN), dtype=jnp.float32), 'wq': jax.random.normal(k_q, (N_HEADS * HEAD_DIM, HIDDEN), dtype=jnp.float32) * s, 'wk': jax.random.normal(k_k, (N_HEADS * HEAD_DIM, HIDDEN), dtype=jnp.float32) * s, 'wv': jax.random.normal(k_v, (N_HEADS * HEAD_DIM, HIDDEN), dtype=jnp.float32) * s, 'wo': jax.random.normal(k_o, (HIDDEN, N_HEADS * HEAD_DIM), dtype=jnp.float32) * s}
    _L0_attn_all = _L0_attn_setup()
    _L0_attn_in = {k: v for k, v in _L0_attn_all.items() if k in ('wq', 'wk', 'wv', 'wo')}
    del _L0_attn_all

    def _L0_xattn_setup():
        import jax, jax.numpy as jnp
        import numpy as np
        B, TQ, TK, D, H = (2, 512, 512, 256, 16)
        HD = D // H
        NUM_PAD = 64
        key = jax.random.key(seed)
        ks = jax.random.split(key, 8)
        s = 0.02
        q = jax.random.normal(ks[0], (B, TQ, D), dtype=jnp.float32)
        kv = jax.random.normal(ks[1], (B, TK, D), dtype=jnp.float32)
        key_padding_mask = jnp.broadcast_to(jnp.arange(TK) >= TK - NUM_PAD, (B, TK))
        Wq = jax.random.normal(ks[2], (D, D), dtype=jnp.float32) * s
        bq = jax.random.normal(ks[3], (D,), dtype=jnp.float32) * s
        Wkv = jax.random.normal(ks[4], (D, 2 * D), dtype=jnp.float32) * s
        bkv = jax.random.normal(ks[5], (2 * D,), dtype=jnp.float32) * s
        Wo = jax.random.normal(ks[6], (D, D), dtype=jnp.float32) * s
        bo = jax.random.normal(ks[7], (D,), dtype=jnp.float32) * s
        return {'q': q, 'kv': kv, 'key_padding_mask': key_padding_mask, 'Wq': Wq, 'bq': bq, 'Wkv': Wkv, 'bkv': bkv, 'Wo': Wo, 'bo': bo}
    _L0_xattn_all = _L0_xattn_setup()
    _L0_xattn_in = {k: v for k, v in _L0_xattn_all.items() if k in ('Wq', 'bq', 'Wkv', 'bkv', 'Wo', 'bo')}
    del _L0_xattn_all

    def _L0_ffn_setup():
        import jax, jax.numpy as jnp
        import numpy as np
        B, T, E, C, H, G = (2, 512, 8, 256, 512, 16)
        key = jax.random.key(seed)
        ks = jax.random.split(key, 7)
        return {'hidden_states': jax.random.normal(ks[0], (B, T, C), jnp.float32), 'w_red': jax.random.normal(ks[1], (C, G), jnp.float32) * 0.02, 'wg': jax.random.normal(ks[2], (E, G), jnp.float32), 'W1': jax.random.normal(ks[3], (E, C, H), jnp.float32) * 0.02, 'b1': jax.random.normal(ks[4], (E, H), jnp.float32) * 0.02, 'W2': jax.random.normal(ks[5], (E, H, C), jnp.float32) * 0.02, 'b2': jax.random.normal(ks[6], (E, C), jnp.float32) * 0.02}
    _L0_ffn_all = _L0_ffn_setup()
    _L0_ffn_in = {k: v for k, v in _L0_ffn_all.items() if k in ('w_red', 'wg', 'W1', 'b1', 'W2', 'b2')}
    del _L0_ffn_all

    def _L1_attn_setup():
        import jax, jax.numpy as jnp
        import numpy as np
        EMB = 256
        HEAD = 64
        key = jax.random.key(seed)
        k1, k2, k3, k4, k5 = jax.random.split(key, 5)
        x = jax.random.normal(k1, (4, 1024, EMB), dtype=jnp.float32)
        W_qkv = jax.random.normal(k2, (EMB, 3 * HEAD), dtype=jnp.float32) * (1.0 / np.sqrt(EMB))
        b_qkv = jax.random.normal(k3, (3 * HEAD,), dtype=jnp.float32) * 0.01
        W_out = jax.random.normal(k4, (HEAD, EMB), dtype=jnp.float32) * (1.0 / np.sqrt(HEAD))
        b_out = jax.random.normal(k5, (EMB,), dtype=jnp.float32) * 0.01
        return {'x': x, 'W_qkv': W_qkv, 'b_qkv': b_qkv, 'W_out': W_out, 'b_out': b_out}
    _L1_attn_all = _L1_attn_setup()
    _L1_attn_in = {k: v for k, v in _L1_attn_all.items() if k in ('W_qkv', 'b_qkv', 'W_out', 'b_out')}
    del _L1_attn_all

    def _L1_xattn_setup():
        import jax, jax.numpy as jnp
        import numpy as np
        B, S, D, H = (2, 512, 256, 16)
        key = jax.random.key(seed)
        ks = jax.random.split(key, 7)
        scale_in = (6.0 / (D + 3 * D)) ** 0.5
        scale_out = (6.0 / (D + D)) ** 0.5
        return {'query': jax.random.normal(ks[0], (B, S, D), jnp.float32), 'key': jax.random.normal(ks[1], (B, S, D), jnp.float32), 'value': jax.random.normal(ks[2], (B, S, D), jnp.float32), 'in_proj_weight': jax.random.uniform(ks[3], (D, 3 * D), jnp.float32, -scale_in, scale_in), 'in_proj_bias': jnp.zeros((3 * D,), jnp.float32), 'out_proj_weight': jax.random.uniform(ks[4], (D, D), jnp.float32, -scale_out, scale_out), 'out_proj_bias': jnp.zeros((D,), jnp.float32), 'num_heads': H}
    _L1_xattn_all = _L1_xattn_setup()
    _L1_xattn_in = {k: v for k, v in _L1_xattn_all.items() if k in ('in_proj_weight', 'in_proj_bias', 'out_proj_weight', 'out_proj_bias')}
    del _L1_xattn_all

    def _L1_ffn_setup():
        import jax, jax.numpy as jnp
        import numpy as np
        CAPACITY = 0.5
        key = jax.random.key(seed)
        ks = jax.random.split(key, 7)
        b, s, d, h = (4, 2048, 256, 1024)
        sc_r = 1.0 / np.sqrt(d)
        sc_1 = 1.0 / np.sqrt(d)
        sc_2 = 1.0 / np.sqrt(h)
        return {'x': jax.random.normal(ks[0], (b, s, d), dtype=jnp.float32), 'w_r': jax.random.uniform(ks[1], (d, 1), jnp.float32, -sc_r, sc_r), 'b_r': jax.random.uniform(ks[2], (1,), jnp.float32, -sc_r, sc_r), 'W1': jax.random.uniform(ks[3], (d, h), jnp.float32, -sc_1, sc_1), 'b1': jax.random.uniform(ks[4], (h,), jnp.float32, -sc_1, sc_1), 'W2': jax.random.uniform(ks[5], (h, d), jnp.float32, -sc_2, sc_2), 'b2': jax.random.uniform(ks[6], (d,), jnp.float32, -sc_2, sc_2)}
    _L1_ffn_all = _L1_ffn_setup()
    _L1_ffn_in = {k: v for k, v in _L1_ffn_all.items() if k in ('w_r', 'b_r', 'W1', 'b1', 'W2', 'b2')}
    del _L1_ffn_all
    return {'x': x, 'ctx_1024': ctx_1024, 'mask_BxS2_bk0': mask_BxS2_bk0, 'L0_attn_wq': _L0_attn_in['wq'], 'L0_attn_wk': _L0_attn_in['wk'], 'L0_attn_wv': _L0_attn_in['wv'], 'L0_attn_wo': _L0_attn_in['wo'], 'L0_xattn_Wq': _L0_xattn_in['Wq'], 'L0_xattn_bq': _L0_xattn_in['bq'], 'L0_xattn_Wkv': _L0_xattn_in['Wkv'], 'L0_xattn_bkv': _L0_xattn_in['bkv'], 'L0_xattn_Wo': _L0_xattn_in['Wo'], 'L0_xattn_bo': _L0_xattn_in['bo'], 'L0_ffn_w_red': _L0_ffn_in['w_red'], 'L0_ffn_wg': _L0_ffn_in['wg'], 'L0_ffn_W1': _L0_ffn_in['W1'], 'L0_ffn_b1': _L0_ffn_in['b1'], 'L0_ffn_W2': _L0_ffn_in['W2'], 'L0_ffn_b2': _L0_ffn_in['b2'], 'L1_attn_W_qkv': _L1_attn_in['W_qkv'], 'L1_attn_b_qkv': _L1_attn_in['b_qkv'], 'L1_attn_W_out': _L1_attn_in['W_out'], 'L1_attn_b_out': _L1_attn_in['b_out'], 'L1_xattn_in_proj_weight': _L1_xattn_in['in_proj_weight'], 'L1_xattn_in_proj_bias': _L1_xattn_in['in_proj_bias'], 'L1_xattn_out_proj_weight': _L1_xattn_in['out_proj_weight'], 'L1_xattn_out_proj_bias': _L1_xattn_in['out_proj_bias'], 'L1_ffn_w_r': _L1_ffn_in['w_r'], 'L1_ffn_b_r': _L1_ffn_in['b_r'], 'L1_ffn_W1': _L1_ffn_in['W1'], 'L1_ffn_b1': _L1_ffn_in['b1'], 'L1_ffn_W2': _L1_ffn_in['W2'], 'L1_ffn_b2': _L1_ffn_in['b2']}

def reference(x, ctx_1024, mask_BxS2_bk0, L0_attn_wq, L0_attn_wk, L0_attn_wv, L0_attn_wo, L0_xattn_Wq, L0_xattn_bq, L0_xattn_Wkv, L0_xattn_bkv, L0_xattn_Wo, L0_xattn_bo, L0_ffn_w_red, L0_ffn_wg, L0_ffn_W1, L0_ffn_b1, L0_ffn_W2, L0_ffn_b2, L1_attn_W_qkv, L1_attn_b_qkv, L1_attn_W_out, L1_attn_b_out, L1_xattn_in_proj_weight, L1_xattn_in_proj_bias, L1_xattn_out_proj_weight, L1_xattn_out_proj_bias, L1_ffn_w_r, L1_ffn_b_r, L1_ffn_W1, L1_ffn_b1, L1_ffn_W2, L1_ffn_b2):
    import jax
    import jax.numpy as jnp

    def _L0_attn_ref(x, wq, wk, wv, wo):
        import jax, jax.numpy as jnp
        import numpy as np
        N_HEADS = 16
        HIDDEN = 256
        HEAD_DIM = 64
        BSZ = 4
        SEQ = 256
        SCALE = HEAD_DIM ** (-0.5)
        bsz, seqlen, _ = x.shape
        xq = jnp.einsum('bsh,oh->bso', x, wq)
        xk = jnp.einsum('bsh,oh->bso', x, wk)
        xv = jnp.einsum('bsh,oh->bso', x, wv)
        xq = xq.reshape(bsz, N_HEADS, seqlen, HEAD_DIM)
        xk = xk.reshape(bsz, N_HEADS, seqlen, HEAD_DIM)
        xv = xv.reshape(bsz, N_HEADS, seqlen, HEAD_DIM)
        scores = jnp.einsum('bhid,bhjd->bhij', xq, xk) * SCALE
        scores = jax.nn.softmax(scores, axis=-1)
        out = jnp.einsum('bhij,bhjd->bhid', scores, xv)
        out = out.reshape(bsz, seqlen, N_HEADS * HEAD_DIM)
        return jnp.einsum('bso,ho->bsh', out, wo)

    def _L0_xattn_ref(q, kv, key_padding_mask, Wq, bq, Wkv, bkv, Wo, bo):
        import jax, jax.numpy as jnp
        import numpy as np
        B, TQ, TK, D, H = (2, 512, 512, 256, 16)
        HD = D // H
        NUM_PAD = 64
        Bc, Tq, Dm = q.shape
        Tk = kv.shape[1]
        scale = HD ** (-0.5)
        Q = (q @ Wq + bq).reshape(Bc, Tq, H, HD).transpose(0, 2, 1, 3)
        KV = (kv @ Wkv + bkv).reshape(Bc, Tk, 2, H, HD).transpose(2, 0, 3, 1, 4)
        K, V = (KV[0], KV[1])
        attn = jnp.einsum('bhqd,bhkd->bhqk', Q, K) * scale
        attn = jnp.where(key_padding_mask[:, None, None, :], -jnp.inf, attn)
        attn = jax.nn.softmax(attn, axis=-1)
        out = jnp.einsum('bhqk,bhkd->bhqd', attn, V)
        out = out.transpose(0, 2, 1, 3).reshape(Bc, Tq, Dm)
        return out @ Wo + bo

    def _L0_ffn_ref(hidden_states, w_red, wg, W1, b1, W2, b2):
        import jax, jax.numpy as jnp
        import numpy as np
        B, T, E, C, H, G = (2, 512, 8, 256, 512, 16)
        b, t, c = hidden_states.shape
        x = hidden_states.reshape(-1, c)
        x_red = x @ w_red
        wg_n = wg / jnp.maximum(jnp.linalg.norm(wg, axis=1, keepdims=True), 0.0001)
        logits = x_red @ wg_n.T
        gates = jax.nn.softmax(logits, axis=1)
        scores = jnp.max(gates, axis=1)
        idx = jnp.argmax(gates, axis=1)
        h = jnp.einsum('nc,ech->neh', x, W1) + b1[None]
        h = jnp.take_along_axis(h, idx[:, None, None], axis=1)[:, 0, :]
        h = jax.nn.gelu(h, approximate=False)
        o = jnp.einsum('nh,ehc->nec', h, W2) + b2[None]
        o = jnp.take_along_axis(o, idx[:, None, None], axis=1)[:, 0, :]
        o = o * scores[:, None]
        return o.reshape(b, t, c)

    def _L1_attn_ref(x, W_qkv, b_qkv, W_out, b_out):
        import jax, jax.numpy as jnp
        import numpy as np
        EMB = 256
        HEAD = 64
        qkv = jnp.einsum('bse,ed->bsd', x, W_qkv) + b_qkv
        q, k, v = jnp.split(qkv, 3, axis=-1)
        scale = 1.0 / jnp.sqrt(jnp.asarray(q.shape[-1], q.dtype))
        scores = jnp.einsum('bqh,bkh->bqk', q, k) * scale
        attn = jax.nn.softmax(scores, axis=-1)
        ctx = jnp.einsum('bqk,bkh->bqh', attn, v)
        return jnp.einsum('bqh,he->bqe', ctx, W_out) + b_out

    def _L1_xattn_ref(query, key, value, in_proj_weight, in_proj_bias, out_proj_weight, out_proj_bias, num_heads):
        import jax, jax.numpy as jnp
        import numpy as np
        B, S, D, H = (2, 512, 256, 16)
        qbs, qss, qds = query.shape
        b, s, d = value.shape
        qw, kw, vw = jnp.split(in_proj_weight, 3, axis=-1)
        qb, kb, vb = jnp.split(in_proj_bias, 3, axis=-1)
        q = (query @ qw + qb).reshape(qbs, qss, num_heads, -1)
        k = (key @ kw + kb).reshape(b, s, num_heads, -1)
        v = (value @ vw + vb).reshape(b, s, num_heads, -1)
        scale = q.shape[-1] ** (-0.5)
        scores = jnp.einsum('bqhd,bkhd->bhqk', q * scale, k)
        attn = jax.nn.softmax(scores, axis=-1)
        out = jnp.einsum('bhqk,bkhd->bqhd', attn, v)
        return out.reshape(qbs, qss, qds) @ out_proj_weight + out_proj_bias

    def _L1_ffn_ref(x, w_r, b_r, W1, b1, W2, b2):
        import jax, jax.numpy as jnp
        import numpy as np
        CAPACITY = 0.5
        b, s, d = x.shape
        k = int(CAPACITY * s)
        weights = (jnp.einsum('bsd,do->bso', x, w_r) + b_r).squeeze(-1)
        top_vals, _ = jax.lax.top_k(weights, k)
        threshold = top_vals[:, -1]
        selected = weights > threshold[:, None]
        hidden = jax.nn.gelu(jnp.einsum('bsd,dh->bsh', x, W1) + b1, approximate=False)
        blk = jnp.einsum('bsh,hd->bsd', hidden, W2) + b2
        m = selected[..., None]
        return jnp.where(m, blk, x)
    x = _layernorm(x + _L0_attn_ref(x, L0_attn_wq, L0_attn_wk, L0_attn_wv, L0_attn_wo), axis=-1)
    x = _layernorm(x + _L0_xattn_ref(x, ctx_1024, mask_BxS2_bk0, L0_xattn_Wq, L0_xattn_bq, L0_xattn_Wkv, L0_xattn_bkv, L0_xattn_Wo, L0_xattn_bo), axis=-1)
    x = _layernorm(x + _L0_ffn_ref(x, L0_ffn_w_red, L0_ffn_wg, L0_ffn_W1, L0_ffn_b1, L0_ffn_W2, L0_ffn_b2), axis=-1)
    x = _layernorm(x + _L1_attn_ref(x, L1_attn_W_qkv, L1_attn_b_qkv, L1_attn_W_out, L1_attn_b_out), axis=-1)
    x = _layernorm(x + _L1_xattn_ref(x, ctx_1024, ctx_1024, L1_xattn_in_proj_weight, L1_xattn_in_proj_bias, L1_xattn_out_proj_weight, L1_xattn_out_proj_bias, 16), axis=-1)
    x = _layernorm(x + _L1_ffn_ref(x, L1_ffn_w_r, L1_ffn_b_r, L1_ffn_W1, L1_ffn_b1, L1_ffn_W2, L1_ffn_b2), axis=-1)
    return x

_drawn_inputs = setup_inputs


def setup_inputs(seed=0):
    import zlib

    import numpy as np

    out = dict(_drawn_inputs(seed))
    spreads = {'L1_xattn_in_proj_bias': (0.0, 0.1), 'L1_xattn_out_proj_bias': (0.0, 0.1)}
    factors = {'L0_xattn_Wq': 8.0,
     'L0_xattn_bq': 52.018,
     'L0_xattn_bkv': 5.665,
     'L0_ffn_w_red': 3.391,
     'L0_ffn_wg': 3.389,
     'L0_ffn_W1': 3.298,
     'L0_ffn_b1': 8.0,
     'L0_ffn_W2': 3.183,
     'L0_ffn_b2': 8.0,
     'L1_attn_b_qkv': 5.49,
     'L1_attn_b_out': 5.981,
     'L1_ffn_b1': 6.709,
     'L1_ffn_b2': 4.401}
    for name, (base, spread) in spreads.items():
        noise = np.random.default_rng([zlib.crc32(name.encode()), seed]).standard_normal(out[name].shape)
        drawn = base * np.exp(spread * noise) if base else spread * noise
        out[name] = jnp.asarray(drawn.astype(out[name].dtype))
    for name, factor in factors.items():
        out[name] = (out[name] * factor).astype(out[name].dtype)
    return out
```

```python
from contextlib import ExitStack

import concourse.bass as bass
from concourse import mybir

F32 = mybir.dt.float32
F32R = mybir.dt.float32r
ALU = mybir.AluOpType
ACT = mybir.ActivationFunctionType
AX = mybir.AxisListType
P = 128
D = 256
EPS = 1e-5


class Tally:

    def __init__(self, sems):
        self.sems = sems
        self.count = {}
        self.per = None
        self.reg = None
        self.mute = False

    def inc(self, name, n=1):
        self.count[name] = self.count.get(name, 0) + n

    def at(self, name, back=0):
        value = self.count.get(name, 0) - back
        if self.reg is not None and self.per.get(name, 0):
            return self.reg * self.per[name] + value
        return value

    def loop(self, eng, trips, body):
        start = dict(self.count)
        self.mute = True
        body(0)
        self.mute = False
        per = {k: v - start.get(k, 0) for k, v in self.count.items()}
        self.count = dict(start)
        with eng.Fori(0, trips) as reg:
            self.per, self.reg = per, reg
            body(reg)
        self.per = self.reg = None
        self.count = {k: start.get(k, 0) + trips * n for k, n in per.items()}


class Writer(Tally):

    def __init__(self, nc, eng, role, sems, weights=0):
        super().__init__(sems)
        self.nc, self.eng, self.role = nc, eng, role
        self.weights = weights

    def on(self, role):
        return self.role == role and not self.mute

    def wait(self, name, value):
        if isinstance(value, int) and value <= 0:
            return
        self.eng.wait_ge(self.sems[name], value)

    def waits(self, *pairs):
        pairs = [(name, value if isinstance(value, int) else self.eng.to_reg(value)) for name, value in pairs]
        if not all(isinstance(value, int) for _, value in pairs):
            self.eng.wait_ge(self.sems["w"], self.weights)
        for name, value in pairs:
            self.wait(name, value)

    def fixed(self, value):
        return value if isinstance(value, int) else self.eng.snap(value)

    def link(self, ins, name):
        if ins is not None:
            ins.then_inc(self.sems[name], 1)
        self.inc(name)
        if ins is not None:
            self.wait(name, self.at(name))


class Room:

    def __init__(self, nc, ctx, tag):
        self.nc, self.ctx, self.tag = nc, ctx, tag
        self.sems = []
        ctx.callback(self.clear)

    def clear(self):
        self.nc.clear_and_free_semaphores(self.sems)
        self.nc.all_engine_barrier()

    def sb(self, name, shape, dt=F32):
        return self.ctx.enter_context(self.nc.sbuf_tensor(f"{self.tag}_{name}", shape, dt))

    def ps(self, name, shape, dt=F32):
        return self.ctx.enter_context(self.nc.psum_tensor(f"{self.tag}_{name}", shape, dt))

    def sem(self, name):
        self.sems.append(self.nc.alloc_semaphore(name=f"{self.tag}_{name}"))
        return self.sems[-1]


def make_identity(pool, tile, sem):
    pool.memset(tile[:, :], 0.0).then_inc(sem, 1)
    pool.wait_ge(sem, 1)
    pool.affine_select(out=tile[:, :], in_=tile[:, :], compare_op=ALU.not_equal, fill=1.0, base=0,
                       pattern=[[-1, P]], channel_multiplier=1).then_inc(sem, 1)


def layer0_self_attention(nc, x, wqT, wkT, wvT, woT, y):
    TOK = x.shape[0]
    HD = 64
    SEG = wqT.shape[1] // HD
    ROWS = SEG * HD
    GH = 4
    GT = GH * HD
    NG = TOK // GT
    KC = ROWS // P
    SCALE = HD ** -0.5
    RING = 4
    XB = 3

    with ExitStack() as ctx:
        m = Room(nc, ctx, "a")
        wq = m.sb("wq", [P, 2, SEG * HD])
        wk = m.sb("wk", [P, 2, SEG * HD])
        wv = m.sb("wv", [P, 2, SEG * HD])
        wo = m.sb("wo", [P, KC, D])
        ident = m.sb("ident", [P, P])
        rowmask = m.sb("rowmask", [16, KC, P], mybir.dt.bfloat16)
        xs = m.sb("xs", [P, 2, D])
        xg = m.sb("xg", [P, XB, 2, D])
        xT = m.sb("xT", [P, 2, GT])
        qhi, qlo, khi, klo = (m.sb(n, [P, 2, GH, 512], F32R) for n in ("qhi", "qlo", "khi", "klo"))
        vghi, vglo = (m.sb(n, [P, 2, 2 * 512], F32R) for n in ("vghi", "vglo"))
        qA = m.sb("qA", [P, 2, ROWS], F32R)
        qB = m.sb("qB", [P, 2, ROWS], F32R)
        kA = m.sb("kA", [P, 2, ROWS], F32R)
        kB = m.sb("kB", [P, 2, ROWS], F32R)
        vhi = m.sb("vhi", [P, 2, KC, 2 * HD], F32R)
        vlo = m.sb("vlo", [P, 2, KC, HD], F32R)
        pr = m.sb("pr", [P, 2, 512])
        plo = m.sb("plo", [P, RING, 512], F32R)
        phi = m.sb("phi", [P, RING, 512], F32R)
        mxs = m.sb("mxs", [P, KC, 2])
        mall = m.sb("mall", [P, KC])
        m16 = m.sb("m16", [P, 2 * KC], F32R)
        oU = m.sb("oU", [P, 2, 512])
        rec = m.sb("rec", [HD, 2, 512])
        inv = m.sb("inv", [HD, ROWS // 32])
        oT = m.sb("oT", [P, 2, KC, P])
        res = m.sb("res", [P, 2, D])
        bst = m.sb("bst", [P, 2, 6])
        mv = m.sb("mv", [P, 2, 2])
        rstd = m.sb("rstd", [P, 2, 2])
        mhalf = m.sb("mhalf", [P, 1])
        eps = m.sb("eps", [P, 1])
        idle = m.sb("idle", [1, 1])
        psS = m.ps("psS", [P, 2, 512])
        psO = m.ps("psO", [P, 2, 512])
        psX = m.ps("psX", [P, 2, 512])
        psM = m.ps("psM", [P, 512])

        names = ("cst", "cstv", "w", "x", "mi", "md", "ch", "ba0", "ba1", "bb0", "bb1", "bv", "mx", "mxr", "m16", "s", "e", "ph", "lo",
                 "pv", "nm", "ot", "var", "pl", "rstd", "y", "yo", "dv")
        sems = {n: m.sem(n) for n in names}
        block = ctx.enter_context(nc.Block())

        def task_list():
            todo = [("T",)] + [("Q", c) for c in range(KC)] + [("K", c) for c in range(KC)] + \
                   [("V", tt, c2) for tt in range(2) for c2 in range(2)]
            slots = {}
            for j in range(GH):
                for kc in range(KC):
                    if kc == 6:
                        slots[j, kc] = ("M",)
                    elif kc == 3 and j % 2 == 0:
                        slots[j, kc] = ("O",)
                    elif (j, kc) >= (0, 1) and todo:
                        slots[j, kc] = todo.pop(0)
            assert not todo
            return slots

        SLOTS = task_list()
        XPLAN = {1: 3, 2: 3, 3: 3, 4: 3, 5: 4}

        def load_x(w, g):
            if w.on("sync"):
                row, slot = w.fixed(g % NG * GT), w.fixed(g % XB)
                w.waits(("var", w.at("var")), ("mi", w.at("mi")))
                w.eng.dma_start(xg[:, bass.ds(slot, 1), :, :],
                                x[bass.ds(row, GT), :].rearrange("(t p) c -> p t c", p=P)).then_inc(sems["x"], 16)
                w.eng.dma_start(xs[:, :, :], x[bass.ds(row, GT), :].rearrange("(t p) c -> p t c", p=P))\
                    .then_inc(sems["x"], 16)
            w.inc("x", 32)

        def misc(w, what, G, buf):
            kind = what[0]
            if w.on("tensor"):
                w.wait("md", w.at("md"))
                if kind == "T":
                    w.wait("x", w.at("x"))
                    for cc in range(2):
                        for tt in range(2):
                            last = w.eng.transpose(psM[:, (2 * cc + tt) * P:(2 * cc + tt + 1) * P],
                                                   xs[:, tt, cc * P:(cc + 1) * P], ident[:, :])
                elif kind in "QK":
                    wt = wq if kind == "Q" else wk
                    c = what[1]
                    for cc in range(2):
                        last = w.eng.matmul(psM[:, 0:GT], wt[:, cc, c * P:(c + 1) * P], xT[:, cc, :],
                                            start=cc == 0, stop=cc == 1)
                elif kind == "V":
                    _, tt, c2 = what
                    for cc in range(2):
                        last = w.eng.matmul(psM[:, :], xT[:, cc, tt * P:(tt + 1) * P],
                                            wv[:, cc, c2 * 512:(c2 + 1) * 512], start=cc == 0, stop=cc == 1)
                elif kind == "M":
                    w.wait("m16", w.at("m16"))
                    last = w.eng.transpose(psM[0:16, 0:P], m16[:, :].bitcast(F32), ident[:, :])
                elif kind == "O":
                    w.wait("ot", w.at("ot"))
                    for c in range(KC):
                        last = w.eng.matmul(psM[:, 0:D], oT[:, buf, c, :], wo[:, c, :], start=c == 0, stop=c == KC - 1)
                last.then_inc(sems["mi"], 1)
            w.inc("mi")
            if kind == "T":
                if w.on("scalar"):
                    w.wait("mi", w.at("mi"))
                    w.eng.activation(xT[:, :, :].rearrange("p a b -> p (a b)"), psM[:, :], ACT.Copy).then_inc(sems["md"], 1)
            elif kind in "QK":
                hi, lo = (qhi, qlo) if kind == "Q" else (khi, klo)
                c = what[1]
                src = psM[:, 0:GT].rearrange("p (h t) -> p h t", t=HD)

                def dst(t):
                    v = t[:, bass.ds(buf, 1), :, c * HD:(c + 1) * HD]
                    return v.rearrange("p b h t -> p (b h) t")
                if w.on("scalar"):
                    if what == ("Q", 0):
                        for n in ("ba0", "ba1", "bb0", "bb1"):
                            w.wait(n, w.at(n))
                    w.wait("mi", w.at("mi"))
                    w.eng.activation(dst(hi), src, ACT.Copy).then_inc(sems["ch"], 1)
                w.inc("ch")
                if w.on("vector"):
                    if what == ("Q", 0):
                        for n in ("ba0", "ba1", "bb0", "bb1"):
                            w.wait(n, w.at(n))
                    w.wait("ch", w.at("ch"))
                    w.eng.tensor_tensor(dst(lo), src, dst(hi).bitcast(F32), ALU.subtract).then_inc(sems["md"], 1)
            elif kind == "V":
                _, tt, c2 = what
                part = slice(c2 * 512, (c2 + 1) * 512)
                if w.on("scalar"):
                    w.wait("bv", w.at("bv"))
                    w.wait("mi", w.at("mi"))
                    w.eng.activation(vghi[:, tt, part], psM[:, :], ACT.Copy).then_inc(sems["ch"], 1)
                w.inc("ch")
                if w.on("vector"):
                    w.wait("bv", w.at("bv"))
                    w.wait("ch", w.at("ch"))
                    w.eng.tensor_tensor(vglo[:, tt, part], psM[:, :], vghi[:, tt, part].bitcast(F32), ALU.subtract)\
                        .then_inc(sems["md"], 1)
            elif kind == "M":
                if w.on("vector"):
                    w.wait("mi", w.at("mi"))
                    w.eng.tensor_tensor(qB[HD:HD + 16, buf, :].rearrange("p (b t) -> p b t", t=P),
                                        psM[0:16, 0:P].unsqueeze(1).to_broadcast([16, KC, P]),
                                        rowmask[:, :, :], ALU.mult).then_inc(sems["md"], 1)
            elif kind == "O":
                if w.on("vector"):
                    w.wait("mi", w.at("mi"))
                    w.wait("yo", w.at("yo", 16))
                    xr = xg[:, bass.ds(G % XB, 1), buf, :].rearrange("p a c -> p (a c)")
                    w.eng.tensor_tensor(res[:, buf, :], psM[:, 0:D], xr, ALU.add).then_inc(sems["md"], 1)
                    w.wait("md", w.at("md", -1))
                if w.on("vector"):
                    w.link(w.eng.bn_stats(bst[:, buf, :], res[:, buf, :]), "dv")
                    w.eng.memset(idle[:, :], 0.0)
                    w.eng.bn_aggr(mv[:, buf, :], bst[:, buf, :]).then_inc(sems["var"], 1)
                else:
                    w.inc("dv")
                w.inc("var")
                if w.on("gpsimd"):
                    w.wait("var", w.at("var"))
                    w.link(w.eng.tensor_tensor(rstd[:, buf, 0:1], mv[:, buf, 1:2], eps[:, :], ALU.add), "pl")
                    w.eng.tensor_tensor(rstd[:, buf, 1:2], rstd[:, buf, 0:1], mhalf[:, :], ALU.pow).then_inc(sems["rstd"], 1)
                else:
                    w.inc("pl")
                w.inc("rstd")
            w.inc("md")

        def norm_out(w, G, buf):
            if w.on("vector"):
                w.wait("rstd", w.at("rstd"))
                w.eng.tensor_scalar(res[:, buf, :], res[:, buf, :], mv[:, buf, 0:1], rstd[:, buf, 1:2],
                                    ALU.subtract, ALU.mult).then_inc(sems["y"], 1)
            w.inc("y")
            if w.on("sync"):
                row = w.fixed(G * GT + buf * P)
                w.waits(("y", w.at("y")))
                w.eng.dma_start(y[bass.ds(row, P), :], res[:, buf, :]).then_inc(sems["yo"], 16)
            w.inc("yo", 16)

        def build(w, gbuf, j, b):
            if w.on("sync"):
                gbuf = w.fixed(gbuf)
                w.waits(("md", w.at("md")), ("s", w.at("s")))
                for t, rows, src in ((qA, 0, qhi), (qA, HD, qhi), (kA, 0, khi), (kA, HD, klo)):
                    for par in range(2):
                        w.eng.dma_start(t[rows:rows + HD, b, par * 512:(par + 1) * 512].bitcast(F32),
                                        src[par * HD:(par + 1) * HD, bass.ds(gbuf, 1), j, :].bitcast(F32)).then_inc(sems[f"ba{b}"], 16)
                for t, src in ((qB, qlo), (kB, khi)):
                    for par in range(2):
                        w.eng.dma_start(t[0:HD, b, par * 512:(par + 1) * 512].bitcast(F32),
                                        src[par * HD:(par + 1) * HD, bass.ds(gbuf, 1), j, :].bitcast(F32)).then_inc(sems[f"bb{b}"], 16)
            w.inc(f"ba{b}", 8 * 16)
            w.inc(f"bb{b}", 4 * 16)

        def build_v(w, j, b):
            if w.on("sync"):
                w.waits(("md", w.at("md")), ("pv", w.at("pv")))
                tt, half = j // 2, j % 2
                for to, src in ((vhi, vghi), (vlo, vglo)):
                    for c2 in range(2):
                        w.eng.dma_start(to[c2 * HD:(c2 + 1) * HD, b, :, 0:HD].bitcast(F32),
                                        src[half * HD:(half + 1) * HD, tt, c2 * 512:(c2 + 1) * 512]
                                        .rearrange("p (k d) -> p k d", d=HD).bitcast(F32)).then_inc(sems["bv"], 16)
            w.inc("bv", 4 * 16)

        def max_tile(w, u, b):
            if w.on("tensor"):
                if u == 0:
                    w.wait(f"ba{b}", w.at(f"ba{b}"))
                w.wait("mxr", w.at("mxr", 1))
                w.eng.matmul(psX[:, u % 2, :], qA[:, b, (u // 2) * P:(u // 2 + 1) * P], kA[:, b, (u % 2) * 512:(u % 2 + 1) * 512],
                             start=True, stop=True).then_inc(sems["mx"], 1)
            w.inc("mx")
            if w.on("vector"):
                w.wait("mx", w.at("mx"))
                w.eng.tensor_reduce(mxs[:, u // 2, u % 2:u % 2 + 1], psX[:, u % 2, :], AX.X, ALU.max).then_inc(sems["mxr"], 1)
            w.inc("mxr")

        def max_rows(w):
            if w.on("vector"):
                w.wait("mxr", w.at("mxr"))
                w.link(w.eng.tensor_reduce(mall[:, :], mxs[:, :, :], AX.X, ALU.max), "dv")
                w.link(w.eng.tensor_scalar(m16[:, 0:KC], mall[:, :], -1.0, None, ALU.mult), "dv")
                w.eng.scalar_tensor_tensor(out=m16[:, KC:2 * KC], in0=mall[:, :], scalar=-1.0,
                                           in1=m16[:, 0:KC].bitcast(F32), op0=ALU.mult, op1=ALU.subtract)\
                    .then_inc(sems["m16"], 1)
            else:
                w.inc("dv", 2)
            w.inc("m16")

        def scores(w, kc, b):
            if w.on("tensor"):
                if kc == 0:
                    w.wait(f"bb{b}", w.at(f"bb{b}"))
                    w.wait("md", w.at("md"))
                w.wait("e", w.at("e"))
                for a, q in ((0, 0), (0, 1), (1, 0), (1, 1)):
                    kt, qt = (kB, qB) if a else (kA, qA)
                    last = w.eng.matmul(psS[:, q, :], kt[:, b, kc * P:(kc + 1) * P], qt[:, b, q * 512:(q + 1) * 512],
                                        start=a == 0, stop=a == 1)
                    if a:
                        last.then_inc(sems["s"], 1)
            n = self_ring(w)
            for q in range(2):
                w.inc("s")
                if w.on("scalar"):
                    w.wait("s", w.at("s"))
                    w.wait("lo", w.at("e", 1))
                    w.eng.activation(pr[:, q, :], psS[:, q, :], ACT.Exp, scale=SCALE).then_inc(sems["e"], 1)
                    w.wait("e", w.at("e", -1))
                    w.wait("pv", w.at("e", RING - 1))
                    w.eng.activation(phi[:, n + q, :], pr[:, q, :], ACT.Copy).then_inc(sems["ph"], 1)
                w.inc("e")
                w.inc("ph")

        def low_parts(w):
            for q in range(2):
                n = (w.count["ph"] - 2 + q) % RING
                if w.on("gpsimd"):
                    w.wait("ph", w.at("ph", 1 - q))
                    w.eng.tensor_tensor(plo[:, n, :], pr[:, q, :], phi[:, n, :].bitcast(F32),
                                        ALU.subtract).then_inc(sems["lo"], 1)
                w.inc("lo")

        def self_ring(w):
            return w.count.get("e", 0) % RING

        def values_high(w, kc, b):
            if w.on("tensor"):
                if kc == 0:
                    w.wait("bv", w.at("bv"))
                    w.wait("nm", w.at("nm"))
                for q in range(2):
                    n = (w.count.get("pv", 0) + q) % RING
                    w.wait("ph", w.at("pv", -1 - q))
                    w.eng.matmul(psO[:, q, :], vhi[:, b, kc, :], phi[:, n, :], start=kc == 0, stop=False)
                    w.eng.matmul(psO[0:HD, q, :], vlo[:, b, kc, :], phi[:, n, :], start=False, stop=False)

        def values_low(w, kc, b):
            for q in range(2):
                n = w.count.get("pv", 0) % RING
                if w.on("tensor"):
                    w.wait("lo", w.at("pv", -1))
                    w.eng.matmul(psO[:, q, :], vhi[:, b, kc, :], plo[:, n, :],
                                 start=False, stop=kc == KC - 1).then_inc(sems["pv"], 1)
                w.inc("pv")

        def divide(w, j):
            if w.on("scalar"):
                w.wait("pv", w.at("pv"))
                w.wait("ot", w.at("ot"))
                w.eng.activation(oU[:, :, :], psO[:, :, :], ACT.Copy).then_inc(sems["nm"], 1)
            w.inc("nm")
            if w.on("vector"):
                w.wait("nm", w.at("nm"))
                w.link(w.eng.transpose(rec[:, :, :].rearrange("p a b -> p (a b)"), oU[HD:P, :, :].rearrange("p a b -> p (a b)")), "dv")
                w.link(w.eng.reciprocal(inv[:, :], rec[:, :, :].rearrange("p a b -> p (a b)")[:, 0:ROWS:32]), "dv")
                w.link(w.eng.transpose(rec[:, :, :].rearrange("p a b -> p (a b)"),
                                       inv[:, :].unsqueeze(2).to_broadcast([HD, 32, 32]).rearrange("p a b -> p a b")), "dv")
                for q in range(2):
                    w.eng.tensor_tensor(oT[q * HD:(q + 1) * HD, j // 2, :, (j % 2) * HD:(j % 2 + 1) * HD],
                                        oU[0:HD, q, :].rearrange("p (c t) -> p c t", t=HD),
                                        rec[:, q, :].rearrange("p (c t) -> p c t", t=HD), ALU.mult)\
                        .then_inc(sems["ot"], 1)
            else:
                w.inc("dv", 3)
            w.inc("ot", 2)

        def group(w, G, first=False, last=False):
            for j in range(GH):
                more = not (last and j == GH - 1)
                b, nb = j % 2, (j + 1) % 2
                for kc in range(KC):
                    n = XPLAN.get(kc, 0) if more else 0
                    u = sum(XPLAN.get(i, 0) for i in range(kc))

                    def max_tiles(first, last):
                        for i in range(first, min(last, n)):
                            max_tile(w, u + i, nb)
                    if kc < KC - 1:
                        scores(w, kc + 1, b)
                    elif more:
                        scores(w, 0, nb)
                    if kc == KC - 2 and not (last and j >= 2):
                        build(w, (G + (j + 2) // GH) % 2, (j + 2) % GH, b)
                    max_tiles(0, 1)
                    values_high(w, kc, b)
                    max_tiles(1, 2)
                    task = SLOTS.get((j, kc))
                    if task:
                        if task[0] == "M":
                            if more:
                                misc(w, task, G, nb)
                        elif task[0] == "O":
                            if not (first and j == 0):
                                misc(w, task, G - (j == 0), 1 if j == 0 else 0)
                        elif not last:
                            misc(w, task, G + 1, (G + 1) % 2)
                    max_tiles(2, n)
                    values_low(w, kc, b)
                    if more or kc < KC - 1:
                        low_parts(w)
                    if more and kc == 5:
                        max_rows(w)
                    if kc == KC - 1:
                        divide(w, j)
                    if kc == 4 and j % 2 == 0 and not (first and j == 0):
                        norm_out(w, G - (j == 0), 1 if j == 0 else 0)
                    if kc == 1 and more:
                        build_v(w, (j + 1) % GH, nb)
                    if kc == 7 and j == 1 and not last:
                        load_x(w, G + 2)

        def walk(w):
            load_x(w, 0)
            misc(w, ("T",), 0, 0)
            load_x(w, 1)
            for kind in "QK":
                for c in range(KC):
                    misc(w, (kind, c), 0, 0)
            build(w, 0, 0, 0)
            build(w, 0, 1, 1)
            for tt in range(2):
                for c2 in range(2):
                    misc(w, ("V", tt, c2), 0, 0)
            build_v(w, 0, 0)
            for u in range(2 * KC):
                max_tile(w, u, 0)
            max_rows(w)
            misc(w, ("M",), 0, 0)
            scores(w, 0, 0)
            low_parts(w)
            group(w, 0, first=True)
            w.loop(w.eng, NG - 2, lambda i: group(w, i + 1))
            group(w, NG - 1, last=True)
            misc(w, ("O",), NG - 1, 1)
            norm_out(w, NG - 1, 1)
            return w

        @block.sync
        def _(eng):
            for t, src in ((wq, wqT), (wk, wkT), (wv, wvT)):
                eng.dma_start(t[:, :, :], src.rearrange("(a p) o -> p a o", p=P)).then_inc(sems["w"], 16)
            eng.dma_start(wo[:, :, :], woT.rearrange("(c p) e -> p c e", p=P)).then_inc(sems["w"], 16)
            w = walk(Writer(nc, eng, "sync", sems, weights=64))
            w.wait("yo", w.at("yo"))

        @block.gpsimd
        def _(eng):
            make_identity(eng, ident, sems["cst"])
            eng.memset(rowmask[:, :, :], 0.0).then_inc(sems["cst"], 1)
            eng.wait_ge(sems["cst"], 3)
            for off in (0, KC):
                eng.affine_select(out=rowmask[:, :, :], in_=rowmask[:, :, :], compare_op=ALU.not_equal, fill=1.0,
                                  base=-off, pattern=[[-1, KC], [0, P]], channel_multiplier=1).then_inc(sems["cst"], 1)
                eng.wait_ge(sems["cst"], 4 if off == 0 else 5)
            eng.memset(mhalf[:, :], -0.5).then_inc(sems["cst"], 1)
            eng.memset(eps[:, :], EPS).then_inc(sems["cst"], 1)
            eng.wait_ge(sems["cst"], 7)
            walk(Writer(nc, eng, "gpsimd", sems))

        @block.vector
        def _(eng):
            eng.memset(vhi[:, :, :, HD:2 * HD].bitcast(F32), 1.0).then_inc(sems["cstv"], 1)
            eng.memset(qB[HD:P, :, :].bitcast(F32), 0.0).then_inc(sems["cstv"], 1)
            eng.memset(kB[HD:P, :, :].bitcast(F32), 0.0).then_inc(sems["cstv"], 1)
            eng.wait_ge(sems["cstv"], 3)
            eng.memset(kB[HD:HD + 16, :, :].bitcast(F32), 1.0).then_inc(sems["cstv"], 1)
            eng.wait_ge(sems["cst"], 6)
            walk(Writer(nc, eng, "vector", sems))

        @block.scalar
        def _(eng):
            eng.preload_act_table(ACT.Exp)
            walk(Writer(nc, eng, "scalar", sems))

        @block.tensor
        def _(eng):
            eng.wait_ge(sems["w"], 64)
            eng.wait_ge(sems["cst"], 6)
            eng.wait_ge(sems["cstv"], 4)
            walk(Writer(nc, eng, "tensor", sems))


def load_tokens(nc, y, X, tag):
    with ExitStack() as ctx:
        m = Room(nc, ctx, tag)
        came = m.sem("came")
        block = ctx.enter_context(nc.Block())

        @block.sync
        def _(eng):
            src = y.rearrange("(t p) c -> p t c", p=P)
            n = X.shape[1] // 4
            for i in range(4):
                eng.dma_start(X[:, i * n:(i + 1) * n, :], src[:, i * n:(i + 1) * n, :]).then_inc(came, 16)
            eng.wait_ge(came, 64)


def cross_attention(nc, tag, X, kv, w_q, b_q, w_k, b_k, w_v, b_v, w_o, b_o, mask):
    B, TK, _ = kv.shape
    NT = X.shape[1]
    TB = NT // B
    H, HD = 16, 16
    KP = 80
    NCH = H * KP // P
    HALF = H // 2
    SCALE = HD ** -0.5
    FAR = -1e30
    NW = 16 * (9 if mask is not None else 8)

    with ExitStack() as ctx:
        m = Room(nc, ctx, tag)
        wq, wk, wv, wo = (m.sb(n, [P, 2, D]) for n in ("wq", "wk", "wv", "wo"))
        bq, bk = (m.sb(n, [P, 2]) for n in ("bq", "bk"))
        bqs = m.sb("bqs", [P, 2])
        bv = m.sb("bv", [P, D])
        bo = m.sb("bo", [P, D])
        ident = m.sb("ident", [P, P])
        hmask = m.sb("hmask", [P, HALF])
        cx = m.sb("cx", [KP, D])
        cxT = m.sb("cxT", [P, 2, HALF, KP])
        vmask = m.sb("vmask", [P, NCH // 2, HALF])
        kt = m.sb("kt", [P, 2, KP])
        vt = m.sb("vt", [P, NCH // 2, D])
        kblk = m.sb("kblk", [P, B, 2, HALF, KP])
        vall = m.sb("vall", [P, B, NCH, P])
        vs = m.sb("vs", [P, NCH, P])
        mraw = m.sb("mraw", [P, B * TK // 4], mybir.dt.int32)
        mbias = m.sb("mbias", [P, B, KP])
        xs = m.sb("xs", [P, D])
        xb = m.sb("xb", [P, D])
        xT = m.sb("xT", [P, 2, P])
        qT = m.sb("qT", [P, 2, P])
        E = m.sb("E", [P, 2, H, KP])
        mx = m.sb("mx", [P, H])
        sm = m.sb("sm", [P, H])
        inv = m.sb("inv", [P, 2, H])
        pT = m.sb("pT", [P, NCH, P])
        oT = m.sb("oT", [P, 2, P])
        res = m.sb("res", [P, 2, D])
        bst = m.sb("bst", [P, 2, 6])
        mv = m.sb("mv", [P, 2, 2])
        rstd = m.sb("rstd", [P, 2, 2])
        mhalf = m.sb("mhalf", [P, 1])
        eps = m.sb("eps", [P, 1])
        idle = m.sb("idle", [1, 1])
        psQ = m.ps("psQ", [P, 2, 2, P])
        psS = m.ps("psS", [P, 4, 512])
        psP = m.ps("psP", [P, 2, 4, P])
        psO = m.ps("psO", [P, 2, D])
        names = ("cst", "cstv", "w", "cx", "ct", "cte", "kv", "kve", "vd", "dv", "xs", "tr", "xt", "q", "qe", "s",
                 "sa", "sb", "ex", "sm", "pn", "pt", "pe", "pv", "pve", "xb", "o", "var", "pl", "rstd", "y", "ph")
        sems = {n: m.sem(n) for n in names}
        block = ctx.enter_context(nc.Block())

        def prepare(w, b):
            if w.on("gpsimd"):
                w.waits(("ct", w.at("ct")))
                w.eng.dma_start(cx[0:TK, :], kv[bass.ds(b, 1), :, :].rearrange("b k c -> (b k) c")).then_inc(sems["cx"], 16)
            w.inc("cx", 16)
            if w.on("tensor"):
                w.wait("cx", w.at("cx"))
                w.wait("kve", w.at("kve"))
                for cc in range(2):
                    last = w.eng.transpose(psQ[:, 0, cc, 0:KP], cx[:, cc * P:(cc + 1) * P], ident[0:KP, 0:KP])
                last.then_inc(sems["ct"], 1)
            w.inc("ct")
            if w.on("scalar"):
                w.wait("ct", w.at("ct"))
                w.wait("kv", w.at("kv"))
                w.eng.activation(cxT[:, :, :, :], psQ[:, 0, :, 0:KP].unsqueeze(2).to_broadcast([P, 2, HALF, KP]), ACT.Copy).then_inc(sems["cte"], 1)
            w.inc("cte")
            if w.on("tensor"):
                w.wait("cte", w.at("cte"))
                for hh in range(2):
                    for cc in range(2):
                        w.eng.matmul(psQ[:, 1, hh, 0:KP], wk[:, cc, hh * P:(hh + 1) * P], cxT[:, cc, 0, :],
                                     start=cc == 0, stop=cc == 1)
                for i in range(NCH // 2):
                    for cc in range(2):
                        rows = cxT[:, cc, :, :].rearrange("p h k -> p (h k)")[:, i * P:(i + 1) * P]
                        last = w.eng.matmul(psS[:, i // 2, (i % 2) * D:(i % 2 + 1) * D], rows, wv[:, cc, :],
                                            start=cc == 0, stop=cc == 1)
                last.then_inc(sems["kv"], 1)
            w.inc("kv")
            if w.on("vector"):
                w.wait("kv", w.at("kv"))
                w.wait("dv", w.at("dv"))
                w.wait("vd", w.at("vd"))
                w.link(w.eng.tensor_tensor(kt[:, :, :], psQ[:, 1, :, 0:KP], bk[:, :].unsqueeze(2).to_broadcast([P, 2, KP]),
                                           ALU.add), "dv")
                w.link(w.eng.tensor_tensor(vt[:, 0:4, :], psS[:, 0:2, :].rearrange("p a (i c) -> p (a i) c", i=2),
                                           bv[:, :].unsqueeze(1).to_broadcast([P, 4, D]), ALU.add), "dv")
                w.eng.tensor_tensor(vt[:, 4, :], psS[:, 2, 0:D], bv[:, :], ALU.add).then_inc(sems["kve"], 1)
                w.wait("kve", w.at("kve", -1))
                for hh in range(2):
                    w.link(w.eng.tensor_tensor(kblk[:, bass.ds(b, 1), hh, :, :].rearrange("p b h k -> p (b h) k"),
                                               kt[:, hh:hh + 1, :].to_broadcast([P, HALF, KP]),
                                               hmask[:, :].unsqueeze(2).to_broadcast([P, HALF, KP]), ALU.mult), "dv")
                    for i in range(NCH // 2):
                        w.eng.tensor_tensor(vall[:, bass.ds(b, 1), hh * 5 + i, :].rearrange("p b (h d) -> p (b h) d", d=HD),
                                            vt[:, i, hh * P:(hh + 1) * P].rearrange("p (h d) -> p h d", d=HD),
                                            vmask[:, i, :].unsqueeze(2).to_broadcast([P, HALF, HD]), ALU.mult)\
                            .then_inc(sems["vd"], 1)
            else:
                w.inc("dv", 4)
            w.inc("kve")
            w.inc("vd", NCH)

        def copy_x(w, t):
            if w.on("gpsimd"):
                w.wait("tr", w.at("tr"))
                w.eng.tensor_copy(xs[:, :], X[:, bass.ds(t, 1), :].rearrange("p a c -> p (a c)")).then_inc(sems["xs"], 1)
            w.inc("xs")

        def turn_x(w):
            if w.on("tensor"):
                w.wait("xs", w.at("xs"))
                w.wait("xt", w.at("xt"))
                w.wait("qe", w.at("qe"))
                for cc in range(2):
                    last = w.eng.transpose(psQ[:, 0, cc, :], xs[:, cc * P:(cc + 1) * P], ident[:, :])
                last.then_inc(sems["tr"], 1)
            w.inc("tr")
            if w.on("scalar"):
                w.wait("tr", w.at("tr"))
                w.wait("q", w.at("q"))
                w.eng.activation(xT[:, :, :], psQ[:, 0, :, :], ACT.Copy).then_inc(sems["xt"], 1)
            w.inc("xt")

        def queries(w):
            if w.on("tensor"):
                w.wait("xt", w.at("xt"))
                w.wait("qe", w.at("qe"))
                for hh in range(2):
                    for cc in range(2):
                        last = w.eng.matmul(psQ[:, 1, hh, :], wq[:, cc, hh * P:(hh + 1) * P], xT[:, cc, :],
                                            start=cc == 0, stop=cc == 1)
                last.then_inc(sems["q"], 1)
            w.inc("q")
            if w.on("scalar"):
                w.wait("q", w.at("q"))
                w.wait("s", w.at("s"))
                for hh in range(2):
                    last = w.eng.activation(qT[:, hh, :], psQ[:, 1, hh, :], ACT.Identity, bias=bqs[:, hh:hh + 1], scale=SCALE)
                last.then_inc(sems["qe"], 1)
            w.inc("qe")

        def scores(w, t):
            b = t // TB
            if w.on("tensor"):
                w.wait("qe", w.at("qe"))
                w.wait("sa", w.at("sa"))
                for hh in range(2):
                    for g in range(2):
                        last = w.eng.matmul(psS[:, 2 * hh + g, 0:4 * KP], qT[:, hh, :],
                                            kblk[:, bass.ds(b, 1), hh, 4 * g:4 * g + 4, :].rearrange("p b h k -> p (b h k)"),
                                            start=True, stop=True)
                last.then_inc(sems["s"], 1)
            w.inc("s")

        def less_max(w, t, par):
            b = t // TB
            if w.on("vector"):
                w.wait("s", w.at("s"))
                w.wait("pt", w.at("pt"))
                e4 = E[:, par, :, :].rearrange("p (g h) k -> p g h k", g=4)
                s4 = psS[:, :, 0:4 * KP].rearrange("p g (h k) -> p g h k", k=KP)
                for g in range(4):
                    last = w.eng.tensor_tensor(e4[:, g, :, :], s4[:, g, :, :],
                                               mbias[:, bass.ds(b, 1), :].to_broadcast([P, 4, KP]), ALU.add)
                last.then_inc(sems["sa"], 1)
                w.wait("sa", w.at("sa", -1))
                w.link(w.eng.tensor_reduce(mx[:, :], E[:, par, :, :], AX.X, ALU.max), "dv")
                w.eng.tensor_tensor(E[:, par, :, :], E[:, par, :, :], mx[:, :].unsqueeze(2).to_broadcast([P, H, KP]),
                                    ALU.subtract).then_inc(sems["sb"], 1)
            else:
                w.inc("dv")
            w.inc("sa")
            w.inc("sb")

        def exponentials(w, par):
            if w.on("scalar"):
                w.wait("sb", w.at("sb"))
                w.eng.activation(E[:, par, :, :], E[:, par, :, :], ACT.Exp).then_inc(sems["ex"], 1)
            w.inc("ex")

        def sums(w, par):
            if w.on("vector"):
                w.wait("ex", w.at("ex"))
                w.link(w.eng.tensor_reduce(sm[:, :], E[:, par, :, :], AX.X, ALU.add), "dv")
                w.eng.reciprocal(inv[:, par, :], sm[:, :]).then_inc(sems["sm"], 1)
            else:
                w.inc("dv")
            w.inc("sm")
            if w.on("gpsimd"):
                w.wait("sm", w.at("sm"))
                w.eng.tensor_tensor(E[:, par, :, :], E[:, par, :, :], inv[:, par, :].unsqueeze(2).to_broadcast([P, H, KP]),
                                    ALU.mult).then_inc(sems["pn"], 1)
            w.inc("pn")

        def fetch_values(w, t):
            b = t // TB
            if w.on("scalar"):
                w.wait("pv", w.at("pv"))
                w.eng.activation(vs[:, :, :], vall[:, bass.ds(b, 1), :, :].rearrange("p b n c -> p (b n) c"), ACT.Copy)\
                    .then_inc(sems["pe"], 1)
            w.inc("pe")

        def turn_p(w, i, par, later=1):
            c0, c1 = 4 * i, min(4 * i + 4, NCH)
            e = E[:, par, :, :].rearrange("p h k -> p (h k)")
            if w.on("tensor"):
                if i == 0:
                    w.wait("pn", w.at("pn", later))
                w.wait("pe", w.at("pe", 1))
                for c in range(c0, c1):
                    last = w.eng.transpose(psP[:, i % 2, c - c0, :], e[:, c * P:(c + 1) * P], ident[:, :])
                if i == 2:
                    last.then_inc(sems["pt"], 1)
                else:
                    last.then_inc(sems["ph"], 1)
            if i == 2:
                w.inc("pt")
            else:
                w.inc("ph")
            if w.on("scalar"):
                w.wait("pt" if i == 2 else "ph", w.at("pt" if i == 2 else "ph"))
                w.eng.activation(pT[:, c0:c1, :], psP[:, i % 2, 0:c1 - c0, :], ACT.Copy).then_inc(sems["pe"], 1)
            w.inc("pe")

        def outputs(w, t):
            if w.on("tensor"):
                w.wait("pe", w.at("pe"))
                w.wait("var", w.at("var"))
                for hh in range(2):
                    for i in range(5):
                        last = w.eng.matmul(psO[:, 0, hh * P:(hh + 1) * P], vs[:, 5 * hh + i, :], pT[:, 5 * hh + i, :],
                                            start=i == 0, stop=i == 4)
                last.then_inc(sems["pv"], 1)
            w.inc("pv")
            if w.on("vector"):
                w.wait("pv", w.at("pv"))
                w.wait("o", w.at("o"))
                w.eng.tensor_copy(oT[:, :, :].rearrange("p a b -> p (a b)"), psO[:, 0, :]).then_inc(sems["pve"], 1)
            w.inc("pve")
            if w.on("gpsimd"):
                w.wait("var", w.at("var"))
                w.eng.tensor_tensor(xb[:, :], X[:, bass.ds(t, 1), :].rearrange("p a c -> p (a c)"), bo[:, :], ALU.add)\
                    .then_inc(sems["xb"], 1)
            w.inc("xb")

        def project(w, par):
            if w.on("tensor"):
                w.wait("pve", w.at("pve"))
                for hh in range(2):
                    last = w.eng.matmul(psO[:, 1, :], oT[:, hh, :], wo[:, hh, :], start=hh == 0, stop=hh == 1)
                last.then_inc(sems["o"], 1)
            w.inc("o")
            if w.on("vector"):
                w.wait("o", w.at("o"))
                w.wait("xb", w.at("xb"))
                w.link(w.eng.tensor_tensor(res[:, par, :], psO[:, 1, :], xb[:, :], ALU.add), "dv")
                w.link(w.eng.bn_stats(bst[:, par, :], res[:, par, :]), "dv")
                w.eng.memset(idle[:, :], 0.0)
                w.eng.bn_aggr(mv[:, par, :], bst[:, par, :]).then_inc(sems["var"], 1)
            else:
                w.inc("dv", 2)
            w.inc("var")
            if w.on("gpsimd"):
                w.wait("var", w.at("var"))
                w.link(w.eng.tensor_tensor(rstd[:, par, 0:1], mv[:, par, 1:2], eps[:, :], ALU.add), "pl")
                w.eng.tensor_tensor(rstd[:, par, 1:2], rstd[:, par, 0:1], mhalf[:, :], ALU.pow).then_inc(sems["rstd"], 1)
            else:
                w.inc("pl")
            w.inc("rstd")

        def normed(w, t, par):
            if w.on("vector"):
                w.wait("rstd", w.at("rstd"))
                w.eng.tensor_scalar(X[:, bass.ds(t, 1), :].rearrange("p a c -> p (a c)"), res[:, par, :],
                                    mv[:, par, 0:1], rstd[:, par, 1:2], ALU.subtract, ALU.mult).then_inc(sems["y"], 1)
            w.inc("y")

        def tile(w, t, par, left=3, first=False):
            if left >= 2:
                scores(w, t + 2)
            if left >= 3:
                copy_x(w, t + 3)
            if left >= 1:
                sums(w, 1 - par)
            fetch_values(w, t)
            turn_p(w, 0, par, 1 if left else 0)
            if not first:
                project(w, 1 - par)
            turn_p(w, 1, par)
            if left >= 3:
                turn_x(w)
            turn_p(w, 2, par)
            if left >= 2:
                less_max(w, t + 2, par)
            if not first:
                normed(w, t - 1, 1 - par)
            if left >= 3:
                queries(w)
            outputs(w, t)
            if left >= 2:
                exponentials(w, par)

        def walk(w):
            w.loop(w.eng, B, lambda b: prepare(w, b))
            if w.role == "tensor":
                w.wait("dv", w.at("dv"))
                w.wait("kve", w.at("kve"))
            if w.role == "scalar":
                w.wait("vd", w.at("vd"))
            for t in range(3):
                copy_x(w, t)
                turn_x(w)
                queries(w)
                if t < 2:
                    scores(w, t)
                    less_max(w, t, t)
                    exponentials(w, t)
                if t == 0:
                    sums(w, 0)
            tile(w, 0, 0, first=True)
            tile(w, 1, 1)
            w.loop(w.eng, NT // 2 - 3, lambda i: (tile(w, 2 * i + 2, 0), tile(w, 2 * i + 3, 1)))
            for t in range(NT - 4, NT):
                tile(w, t, t % 2, left=min(3, NT - 1 - t))
            project(w, 1)
            normed(w, NT - 1, 1)

        @block.sync
        def _(eng):
            for t, src in ((wq, w_q), (wk, w_k), (wv, w_v), (wo, w_o)):
                eng.dma_start(t[:, :, :], src.rearrange("(a p) o -> p a o", p=P)).then_inc(sems["w"], 16)
            for t, src in ((bq, b_q), (bk, b_k)):
                eng.dma_start(t[:, :], src.rearrange("(a p) -> p a", p=P), allow_slow_non_contiguous=True).then_inc(sems["w"], 16)
            for t, src in ((bv, b_v), (bo, b_o)):
                eng.dma_start(t[:, :], src.partition_broadcast(P)).then_inc(sems["w"], 16)
            if mask is not None:
                eng.dma_start(mraw[:, :], mask.partition_broadcast(P)).then_inc(sems["w"], 16)

        @block.gpsimd
        def _(eng):
            make_identity(eng, ident, sems["cst"])
            eng.memset(hmask[:, :], 1.0).then_inc(sems["cst"], 1)
            eng.memset(mhalf[:, :], -0.5).then_inc(sems["cst"], 1)
            eng.memset(eps[:, :], EPS).then_inc(sems["cst"], 1)
            eng.wait_ge(sems["cst"], 5)
            eng.affine_select(out=hmask[:, :], in_=hmask[:, :], compare_op=ALU.is_ge, fill=0.0, base=0,
                              pattern=[[-HD, HALF]], channel_multiplier=1).then_inc(sems["cst"], 1)
            eng.wait_ge(sems["cst"], 6)
            eng.affine_select(out=hmask[:, :], in_=hmask[:, :], compare_op=ALU.is_ge, fill=0.0, base=HD - 1,
                              pattern=[[HD, HALF]], channel_multiplier=-1).then_inc(sems["cst"], 1)
            eng.memset(vmask[:, :, :], 1.0).then_inc(sems["cst"], 1)
            eng.wait_ge(sems["cst"], 8)
            eng.affine_select(out=vmask[:, :, :], in_=vmask[:, :, :], compare_op=ALU.is_ge, fill=0.0, base=0,
                              pattern=[[P, NCH // 2], [-KP, HALF]], channel_multiplier=1).then_inc(sems["cst"], 1)
            eng.wait_ge(sems["cst"], 9)
            eng.affine_select(out=vmask[:, :, :], in_=vmask[:, :, :], compare_op=ALU.is_ge, fill=0.0, base=KP - 1,
                              pattern=[[-P, NCH // 2], [KP, HALF]], channel_multiplier=-1).then_inc(sems["cst"], 1)
            eng.wait_ge(sems["w"], NW)
            eng.wait_ge(sems["cstv"], 2)
            walk(Writer(nc, eng, "gpsimd", sems, weights=NW))

        @block.vector
        def _(eng):
            eng.memset(cx[:, :], 0.0).then_inc(sems["cstv"], 1)
            eng.memset(mbias[:, :, :], FAR).then_inc(sems["cstv"], 1)
            eng.wait_ge(sems["cstv"], 2)
            eng.wait_ge(sems["w"], NW)
            if mask is not None:
                eng.tensor_scalar(mbias[:, :, 0:TK], mraw[:, :].bitcast(mybir.dt.uint8).rearrange("p (b k) -> p b k", k=TK), FAR, None, ALU.mult).then_inc(sems["cstv"], 1)
            else:
                eng.memset(mbias[:, :, 0:TK], 0.0).then_inc(sems["cstv"], 1)
            eng.tensor_scalar(bqs[:, :], bq[:, :], SCALE, None, ALU.mult).then_inc(sems["cstv"], 1)
            eng.wait_ge(sems["cstv"], 4)
            eng.wait_ge(sems["cst"], 10)
            walk(Writer(nc, eng, "vector", sems))

        @block.scalar
        def _(eng):
            eng.preload_act_table(ACT.Exp)
            eng.wait_ge(sems["cstv"], 4)
            walk(Writer(nc, eng, "scalar", sems, weights=NW))

        @block.tensor
        def _(eng):
            eng.wait_ge(sems["w"], NW)
            eng.wait_ge(sems["cst"], 7)
            walk(Writer(nc, eng, "tensor", sems))

GELU = ACT.Gelu


def turn_tokens(nc, tag, X, xT):
    NT = X.shape[1]
    with ExitStack() as ctx:
        m = Room(nc, ctx, tag)
        ident = m.sb("ident", [P, P])
        xs = m.sb("xs", [P, 2, D])
        psT = m.ps("psT", [P, 2, 2, 256])
        sems = {n: m.sem(n) for n in ("cst", "xs", "tr", "xt")}
        block = ctx.enter_context(nc.Block())

        def tile(w, t, par):
            if w.on("gpsimd"):
                w.wait("tr", w.at("tr", 1))
                w.eng.tensor_copy(xs[:, par, :], X[:, bass.ds(t, 1), :].rearrange("p a c -> p (a c)")).then_inc(sems["xs"], 1)
            w.inc("xs")
            if w.on("tensor"):
                w.wait("xs", w.at("xs"))
                w.wait("xt", w.at("xt", 1))
                for cc in range(2):
                    last = w.eng.transpose(psT[:, par, cc, 0:P], xs[:, par, cc * P:(cc + 1) * P], ident[:, :])
                last.then_inc(sems["tr"], 1)
            w.inc("tr")
            if w.on("vector"):
                w.wait("tr", w.at("tr"))
                w.eng.tensor_copy(xT[:, :, bass.ds(t * P, P)], psT[:, par, :, 0:P]).then_inc(sems["xt"], 1)
            w.inc("xt")

        def walk(w):
            tile(w, 0, 0)
            tile(w, 1, 1)
            w.loop(w.eng, NT // 2 - 1, lambda i: (tile(w, 2 * i + 2, 0), tile(w, 2 * i + 3, 1)))

        @block.gpsimd
        def _(eng):
            make_identity(eng, ident, sems["cst"])
            walk(Writer(nc, eng, "gpsimd", sems))

        @block.vector
        def _(eng):
            walk(Writer(nc, eng, "vector", sems))

        @block.tensor
        def _(eng):
            eng.wait_ge(sems["cst"], 2)
            walk(Writer(nc, eng, "tensor", sems))


def expert_gates(nc, xT, w_red, wg, gates):
    NT = gates.shape[1]
    E, G = wg.shape
    TILES = 4
    with ExitStack() as ctx:
        m = Room(nc, ctx, "g")
        ident = m.sb("ident", [P, P])
        wr = m.sb("wr", [P, 2, G])
        wgt = m.sb("wgt", [E, G])
        sq = m.sb("sq", [E, G])
        nrm = m.sb("nrm", [E, 4])
        half = m.sb("half", [E, 1])
        wn = m.sb("wn", [E, G])
        wnT = m.sb("wnT", [G, E])
        xr = m.sb("xr", [G, 512])
        lg = m.sb("lg", [P, NT, E])
        mx = m.sb("mx", [P, NT])
        ex = m.sb("ex", [P, NT, E])
        sm = m.sb("sm", [P, NT])
        sc = m.sb("sc", [P, NT])
        first = m.sb("first", [P, E])
        hit = m.sb("hit", [P, NT, E])
        hm = m.sb("hm", [P, NT])
        psR = m.ps("psR", [P, 512])
        psL = m.ps("psL", [P, 512])
        sems = {n: m.sem(n) for n in ("cst", "w", "nv", "np", "nt", "nte", "r", "re", "l", "le", "dv", "ex")}
        block = ctx.enter_context(nc.Block())

        def group(w, g):
            if w.on("tensor"):
                w.wait("re", w.at("re"))
                for cc in range(2):
                    last = w.eng.matmul(psR[0:G, :], wr[:, cc, :], xT[:, cc, bass.ds(g * 512, 512)],
                                        start=cc == 0, stop=cc == 1)
                last.then_inc(sems["r"], 1)
            w.inc("r")
            if w.on("scalar"):
                w.wait("r", w.at("r"))
                w.wait("l", w.at("l"))
                w.eng.activation(xr[:, :], psR[0:G, :], ACT.Copy).then_inc(sems["re"], 1)
            w.inc("re")
            if w.on("tensor"):
                w.wait("re", w.at("re"))
                w.wait("le", w.at("le"))
                for i in range(TILES):
                    last = w.eng.matmul(psL[:, i * E:(i + 1) * E], xr[:, i * P:(i + 1) * P], wnT[:, :], start=True, stop=True)
                last.then_inc(sems["l"], 1)
            w.inc("l")
            if w.on("vector"):
                w.wait("l", w.at("l"))
                w.eng.tensor_copy(lg[:, bass.ds(g * TILES, TILES), :],
                                  psL[:, 0:TILES * E].rearrange("p (t e) -> p t e", e=E)).then_inc(sems["le"], 1)
            w.inc("le")

        def walk(w):
            group(w, 0)
            w.loop(w.eng, NT // TILES - 1, lambda i: group(w, i + 1))
            return w

        def spread(t):
            return t[:, :].unsqueeze(2).to_broadcast([P, NT, E])

        @block.sync
        def _(eng):
            eng.dma_start(wr[:, :, :], w_red.rearrange("(a p) g -> p a g", p=P)).then_inc(sems["w"], 16)
            eng.dma_start(wgt[:, :], wg).then_inc(sems["w"], 16)

        @block.gpsimd
        def _(eng):
            make_identity(eng, ident, sems["cst"])
            eng.memset(half[:, :], 0.5).then_inc(sems["cst"], 1)
            for e in range(E):
                eng.memset(first[:, e:e + 1], float(E - e)).then_inc(sems["cst"], 1)
            eng.wait_ge(sems["cst"], 3 + E)
            eng.wait_ge(sems["nv"], 2)
            eng.tensor_tensor(nrm[:, 1:2], nrm[:, 0:1], half[:, :], ALU.pow).then_inc(sems["np"], 1)

        @block.scalar
        def _(eng):
            eng.preload_act_table(ACT.Exp)
            eng.wait_ge(sems["nt"], 1)
            eng.activation(wnT[:, :], psL[0:G, 0:E], ACT.Copy).then_inc(sems["nte"], 1)
            walk(Writer(nc, eng, "scalar", sems))
            eng.wait_ge(sems["dv"], 2)
            eng.activation(ex[:, :, :], lg[:, :, :], ACT.Exp).then_inc(sems["ex"], 1)

        @block.tensor
        def _(eng):
            eng.wait_ge(sems["cst"], 2)
            eng.wait_ge(sems["nv"], 5)
            eng.transpose(psL[0:G, 0:E], wn[:, :], ident[0:E, 0:E]).then_inc(sems["nt"], 1)
            eng.wait_ge(sems["nte"], 1)
            walk(Writer(nc, eng, "tensor", sems))

        @block.vector
        def _(eng):
            eng.wait_ge(sems["w"], 32)
            w = Writer(nc, eng, "vector", sems)
            w.link(eng.tensor_tensor(sq[:, :], wgt[:, :], wgt[:, :], ALU.mult), "nv")
            w.link(eng.tensor_reduce(nrm[:, 0:1], sq[:, :], AX.X, ALU.add), "nv")
            eng.wait_ge(sems["np"], 1)
            w.link(eng.tensor_scalar(nrm[:, 2:3], nrm[:, 1:2], 1e-4, None, ALU.max), "nv")
            w.link(eng.reciprocal(nrm[:, 3:4], nrm[:, 2:3]), "nv")
            w.link(eng.tensor_scalar(wn[:, :], wgt[:, :], nrm[:, 3:4], None, ALU.mult), "nv")
            walk(w)
            eng.wait_ge(sems["le"], NT // TILES)
            w.link(eng.tensor_reduce(mx[:, :], lg[:, :, :], AX.X, ALU.max), "dv")
            eng.wait_ge(sems["cst"], 3 + E)
            w.link(eng.tensor_tensor(lg[:, :, :], lg[:, :, :], spread(mx), ALU.subtract), "dv")
            eng.wait_ge(sems["ex"], 1)
            w.link(eng.tensor_reduce(sm[:, :], ex[:, :, :], AX.X, ALU.add), "dv")
            w.link(eng.reciprocal(sc[:, :], sm[:, :]), "dv")
            w.link(eng.tensor_scalar(hit[:, :, :], lg[:, :, :], 0.0, None, ALU.is_equal), "dv")
            w.link(eng.tensor_tensor(hit[:, :, :], hit[:, :, :], first[:, :].unsqueeze(1).to_broadcast([P, NT, E]), ALU.mult), "dv")
            w.link(eng.tensor_reduce(hm[:, :], hit[:, :, :], AX.X, ALU.max), "dv")
            w.link(eng.tensor_tensor(hit[:, :, :], hit[:, :, :], spread(hm), ALU.is_equal), "dv")
            w.link(eng.tensor_tensor(gates[:, :, :], hit[:, :, :], spread(sc), ALU.mult), "dv")


def choose_tokens(nc, xT, w_r, b_r, scratch, keep, gates):
    NT = gates.shape[1]
    B = scratch.shape[0]
    S = scratch.shape[1]
    TB = NT // B
    with ExitStack() as ctx:
        m = Room(nc, ctx, "t")
        wr = m.sb("wr", [P, 2, 1])
        br = m.sb("br", [1, 1])
        row = m.sb("row", [1, B * S])
        col = m.sb("col", [P, NT])
        rows = m.sb("rows", [P, B, S])
        ge = m.sb("ge", [P, S])
        cnt = m.sb("cnt", [P, NT])
        psW = m.ps("psW", [P, 2, 512])
        sems = {n: m.sem(n) for n in ("w", "r", "re", "out", "back", "cnt")}
        block = ctx.enter_context(nc.Block())
        N = B * S // 512

        @block.sync
        def _(eng):
            eng.dma_start(wr[:, :, :], w_r.rearrange("(a p) g -> p a g", p=P), allow_slow_non_contiguous=True).then_inc(sems["w"], 16)
            eng.dma_start(br[:, :], b_r.rearrange("(a b) -> a b", a=1)).then_inc(sems["w"], 16)
            eng.wait_ge(sems["re"], N)
            eng.dma_start(scratch.rearrange("b s -> (b s)").unsqueeze(0), row[:, :]).then_inc(sems["out"], 16)
            eng.wait_ge(sems["out"], 16)
            eng.dma_start(rows[:, :, :], scratch.partition_broadcast(P)).then_inc(sems["back"], 16)
            eng.dma_start(col[:, :], scratch.rearrange("b (t p) -> p (b t)", p=P), allow_slow_non_contiguous=True)\
                .then_inc(sems["back"], 16)

        @block.tensor
        def _(eng):
            eng.wait_ge(sems["w"], 32)
            for n in range(N):
                if n >= 2:
                    eng.wait_ge(sems["re"], n - 1)
                for cc in range(2):
                    last = eng.matmul(psW[0:1, n % 2, :], wr[:, cc, :], xT[:, cc, n * 512:(n + 1) * 512],
                                      start=cc == 0, stop=cc == 1)
                last.then_inc(sems["r"], 1)

        @block.vector
        def _(eng):
            eng.wait_ge(sems["w"], 32)
            for n in range(N):
                eng.wait_ge(sems["r"], n + 1)
                eng.tensor_scalar(row[:, n * 512:(n + 1) * 512], psW[0:1, n % 2, :], br[:, :], None, ALU.add)\
                    .then_inc(sems["re"], 1)
            eng.wait_ge(sems["back"], 32)
            for t in range(NT):
                eng.tensor_scalar(ge[:, :], rows[:, t // TB, :], col[:, t:t + 1], None, ALU.is_ge, ALU.add,
                                  accum_out=cnt[:, t:t + 1]).then_inc(sems["cnt"], 1)
                eng.wait_ge(sems["cnt"], t + 1)
            eng.tensor_scalar(gates[:, :, :].rearrange("p t e -> p (t e)"), cnt[:, :], float(keep), None, ALU.is_lt)\
                .then_inc(sems["cnt"], 1)
            eng.wait_ge(sems["cnt"], NT + 1)


def gated_mlps(nc, tag, X, xT, gates, W1, b1, W2, b2, skip_unchosen, out=None):
    E, _, H = W1.shape
    NT = X.shape[1]
    HC = H // P
    NG = NT // 4
    UN = 2 if E > 1 else 1
    with ExitStack() as ctx:
        m = Room(nc, ctx, tag)
        w1 = m.sb("w1", [P, UN, 2, H])
        w2 = m.sb("w2", [P, UN, HC, D])
        b1s = m.sb("b1s", [P, UN, HC])
        b2s = m.sb("b2s", [P, E, D])
        acc = m.sb("acc", [P, NT, D])
        hT = m.sb("hT", [P, 2, HC, 512])
        tmp = m.sb("tmp", [P, 2, D])
        f = m.sb("f", [P, NT])
        res = m.sb("res", [P, 2, D])
        bst = m.sb("bst", [P, 2, 6])
        mv = m.sb("mv", [P, 2, 2])
        rstd = m.sb("rstd", [P, 2, 2])
        mhalf = m.sb("mhalf", [P, 1])
        eps = m.sb("eps", [P, 1])
        idle = m.sb("idle", [1, 1])
        psH = m.ps("psH", [P, 4, 512])
        psO = m.ps("psO", [P, 4, 512])
        names = ("cst", "cstv", "b", "w0", "w1", "h", "he", "o", "oe", "dv", "var", "pl", "rstd", "y", "st")
        sems = {n: m.sem(n) for n in names}
        block = ctx.enter_context(nc.Block())

        def load(w, e, buf):
            if w.on("sync"):
                w.waits(("o", w.at("o")))
                w.eng.dma_start(w1[:, buf, :, :], W1[bass.ds(e, 1), :, :].rearrange("e (a p) h -> p (e a) h", p=P))\
                    .then_inc(sems[f"w{buf}"], 16)
                w.eng.dma_start(w2[:, buf, :, :], W2[bass.ds(e, 1), :, :].rearrange("e (a p) c -> p (e a) c", p=P))\
                    .then_inc(sems[f"w{buf}"], 16)
                w.eng.dma_start(b1s[:, buf, :], b1[bass.ds(e, 1), :].rearrange("e (a p) -> p (e a)", p=P),
                                allow_slow_non_contiguous=True).then_inc(sems[f"w{buf}"], 16)
            w.inc(f"w{buf}", 48)

        def up(w, e, g, buf, par):
            for hc in range(HC):
                bank = hc % 4
                if w.on("tensor"):
                    if hc == 0:
                        w.wait(f"w{buf}", w.at(f"w{buf}"))
                    w.wait("he", w.at("he", 3))
                    for cc in range(2):
                        last = w.eng.matmul(psH[:, bank, :], w1[:, buf, cc, hc * P:(hc + 1) * P],
                                            xT[:, cc, bass.ds(g * 512, 512)], start=cc == 0, stop=cc == 1)
                    last.then_inc(sems["h"], 1)
                w.inc("h")
                if w.on("scalar"):
                    w.wait("h", w.at("h"))
                    w.wait("o", w.at("o"))
                    if hc == 0:
                        w.wait(f"w{buf}", w.at(f"w{buf}"))
                    w.eng.activation(hT[:, par, hc, :], psH[:, bank, :], GELU,
                                     bias=b1s[:, buf, hc:hc + 1]).then_inc(sems["he"], 1)
                w.inc("he")

        def down(w, e, g, buf, par, later):
            for i in range(4):
                if w.on("tensor"):
                    w.wait("he", w.at("he", later))
                    w.wait("oe", w.at("oe", 3))
                    for hc in range(HC):
                        last = w.eng.matmul(psO[:, i, 0:D], hT[:, par, hc, i * P:(i + 1) * P], w2[:, buf, hc, :],
                                            start=hc == 0, stop=hc == HC - 1)
                    last.then_inc(sems["o"], 1)
                w.inc("o")
                if w.on("vector"):
                    t = g * 4 + i
                    w.wait("o", w.at("o"))
                    w.eng.tensor_tensor(tmp[:, i % 2, :], psO[:, i, 0:D],
                                        b2s[:, bass.ds(e, 1), :].rearrange("p e c -> p (e c)"), ALU.add).then_inc(sems["oe"], 1)
                    w.wait("oe", w.at("oe", -1))
                    a = acc[:, bass.ds(t, 1), :].rearrange("p t c -> p (t c)")
                    w.link(w.eng.scalar_tensor_tensor(out=a, in0=tmp[:, i % 2, :],
                                                      scalar=gates[:, bass.ds(t, 1), bass.ds(e, 1)].rearrange("p t e -> p (t e)"),
                                                      in1=a, op0=ALU.mult, op1=ALU.add), "dv")
                else:
                    w.inc("dv")
                w.inc("oe")

        def finish(w, t, par):
            if w.on("vector"):
                w.wait("y", w.at("y"))
                w.link(w.eng.scalar_tensor_tensor(out=res[:, par, :], in0=X[:, bass.ds(t, 1), :].rearrange("p t c -> p (t c)"),
                                                  scalar=f[:, bass.ds(t, 1)], in1=acc[:, bass.ds(t, 1), :].rearrange("p t c -> p (t c)"),
                                                  op0=ALU.mult, op1=ALU.add), "dv")
                w.link(w.eng.bn_stats(bst[:, par, :], res[:, par, :]), "dv")
                w.eng.memset(idle[:, :], 0.0)
                w.eng.bn_aggr(mv[:, par, :], bst[:, par, :]).then_inc(sems["var"], 1)
            else:
                w.inc("dv", 2)
            w.inc("var")
            if w.on("gpsimd"):
                w.wait("var", w.at("var"))
                w.link(w.eng.tensor_tensor(rstd[:, par, 0:1], mv[:, par, 1:2], eps[:, :], ALU.add), "pl")
                w.eng.tensor_tensor(rstd[:, par, 1:2], rstd[:, par, 0:1], mhalf[:, :], ALU.pow).then_inc(sems["rstd"], 1)
            else:
                w.inc("pl")
            w.inc("rstd")

        def normed(w, t, par, later=0):
            if w.on("vector"):
                w.wait("rstd", w.at("rstd", later))
                w.eng.tensor_scalar(X[:, bass.ds(t, 1), :].rearrange("p t c -> p (t c)"), res[:, par, :],
                                    mv[:, par, 0:1], rstd[:, par, 1:2], ALU.subtract, ALU.mult).then_inc(sems["y"], 1)
            w.inc("y")
            if out is not None:
                if w.on("sync"):
                    row = w.fixed(t * P)
                    tt = w.fixed(t)
                    w.waits(("y", w.at("y")))
                    w.eng.dma_start(out[bass.ds(row, P), :], X[:, bass.ds(tt, 1), :].rearrange("p t c -> p (t c)"))\
                        .then_inc(sems["st"], 16)
                w.inc("st", 16)

        def expert(w, e, buf):
            for g in range(NG):
                up(w, e, g, buf, g % 2)
                if g:
                    down(w, e, g - 1, buf, (g - 1) % 2, HC)
            down(w, e, NG - 1, buf, (NG - 1) % 2, 0)

        def walk(w):
            load(w, 0, 0)
            if E > 1:
                load(w, 1, 1)

                def pair(e):
                    expert(w, e, 0)
                    load(w, (e + 2) % E, 0)
                    expert(w, e + 1, 1)
                    load(w, (e + 3) % E, 1)
                pair(0)
                w.loop(w.eng, E // 2 - 1, lambda i: pair(2 * i + 2))
                if w.role == "sync":
                    for n in ("w0", "w1"):
                        w.wait(n, w.at(n))
            else:
                up(w, 0, 0, 0, 0)
                up(w, 0, 1, 0, 1)
                down(w, 0, 0, 0, 0, HC)

                def two(i):
                    up(w, 0, 2 * i + 2, 0, 0)
                    down(w, 0, 2 * i + 1, 0, 1, HC)
                    up(w, 0, 2 * i + 3, 0, 1)
                    down(w, 0, 2 * i + 2, 0, 0, HC)
                w.loop(w.eng, NG // 2 - 1, two)
                down(w, 0, NG - 1, 0, 1, 0)
            finish(w, 0, 0)
            finish(w, 1, 1)
            normed(w, 0, 0, 1)

            def last(i):
                finish(w, 2 * i + 2, 0)
                normed(w, 2 * i + 1, 1, 1)
                finish(w, 2 * i + 3, 1)
                normed(w, 2 * i + 2, 0, 1)
            w.loop(w.eng, NT // 2 - 1, last)
            normed(w, NT - 1, 1)
            return w

        @block.sync
        def _(eng):
            eng.dma_start(b2s[:, :, :], b2.partition_broadcast(P)).then_inc(sems["b"], 16)
            w = Writer(nc, eng, "sync", {**sems, "w": sems["b"]}, weights=16)
            w = walk(w)
            if out is not None:
                w.wait("st", w.at("st"))

        @block.gpsimd
        def _(eng):
            eng.memset(mhalf[:, :], -0.5).then_inc(sems["cst"], 1)
            eng.memset(eps[:, :], EPS).then_inc(sems["cst"], 1)
            eng.memset(acc[:, :, :], 0.0).then_inc(sems["cst"], 1)
            eng.wait_ge(sems["cst"], 3)
            walk(Writer(nc, eng, "gpsimd", sems))

        @block.vector
        def _(eng):
            if skip_unchosen:
                eng.tensor_scalar(f[:, :], gates[:, :, 0], -1.0, 2.0, ALU.mult, ALU.add).then_inc(sems["cstv"], 1)
            else:
                eng.memset(f[:, :], 1.0).then_inc(sems["cstv"], 1)
            eng.wait_ge(sems["cstv"], 1)
            eng.wait_ge(sems["b"], 16)
            eng.wait_ge(sems["cst"], 3)
            walk(Writer(nc, eng, "vector", sems))

        @block.scalar
        def _(eng):
            eng.preload_act_table(GELU)
            walk(Writer(nc, eng, "scalar", sems))

        @block.tensor
        def _(eng):
            walk(Writer(nc, eng, "tensor", sems))


def layer1_self_attention(nc, X, xT, w_qkv, b_qkv, w_out, b_out, B):
    NT = X.shape[1]
    TB = NT // B
    S = TB * P
    HD = w_out.shape[0]
    KC = S // P
    SCALE = HD ** -0.5
    RING = 4
    NW = 16 * 12
    with ExitStack() as ctx:
        m = Room(nc, ctx, "s")
        wq = m.sb("wq", [P, 2, 2 * HD])
        wk = m.sb("wk", [P, 2, 2 * HD])
        wv = m.sb("wv", [P, 2, HD])
        wo = m.sb("wo", [HD, D])
        bq = m.sb("bq", [P, 1])
        bk = m.sb("bk", [P, 1])
        bv = m.sb("bv", [P, HD])
        bo = m.sb("bo", [P, D])
        ident = m.sb("ident", [P, P])
        rowmask = m.sb("rowmask", [16, KC, P])
        xb = m.sb("xb", [P, 2, S])
        qA = m.sb("qA", [P, S], F32R)
        qB = m.sb("qB", [P, S], F32R)
        kA = m.sb("kA", [P, S], F32R)
        kB = m.sb("kB", [P, S], F32R)
        vd = m.sb("vd", [P, KC, 2 * HD])
        pr = m.sb("pr", [P, RING, 512])
        mxs = m.sb("mxs", [P, KC, 2])
        mall = m.sb("mall", [P, KC])
        m16 = m.sb("m16", [P, 2 * KC], F32R)
        oU = m.sb("oU", [P, 2, 512])
        turned = m.sb("turned", [HD, S])
        inv = m.sb("inv", [HD, S // 32])
        rec = m.sb("rec", [HD, S])
        oT = m.sb("oT", [HD, S])
        xo = m.sb("xo", [P, 2, D])
        res = m.sb("res", [P, 2, D])
        bst = m.sb("bst", [P, 2, 6])
        mv = m.sb("mv", [P, 2, 2])
        rstd = m.sb("rstd", [P, 2, 2])
        mhalf = m.sb("mhalf", [P, 1])
        eps = m.sb("eps", [P, 1])
        idle = m.sb("idle", [1, 1])
        psS = m.ps("psS", [P, RING, 512])
        psO = m.ps("psO", [P, 2, 512])
        psX = m.ps("psX", [P, 2, 512])
        names = ("cst", "cstv", "w", "xb", "ch", "px", "pxr", "m16", "s", "e", "pv", "nm", "ot", "xo", "var", "pl",
                 "rstd", "y", "dv")
        sems = {n: m.sem(n) for n in names}
        block = ctx.enter_context(nc.Block())

        def bank(w):
            return w.count.get("px", 0) % 2

        def fetch(w, b):
            if w.on("gpsimd"):
                w.wait("px", w.at("px"))
                w.eng.tensor_copy(xb[:, :, :], xT[:, :, bass.ds(b * S, S)]).then_inc(sems["xb"], 1)
            w.inc("xb")

        def project(w, wt, bias, hi, hi2, lo, lo_from, n):
            k = bank(w)
            cols = slice(n * 512, (n + 1) * 512)
            if w.on("tensor"):
                w.wait("xb", w.at("xb"))
                w.wait("pxr", w.at("pxr", 1))
                for cc in range(2):
                    last = w.eng.matmul(psX[:, k, :], wt[:, cc, :], xb[:, cc, cols], start=cc == 0, stop=cc == 1)
                last.then_inc(sems["px"], 1)
            w.inc("px")
            if w.on("scalar"):
                w.wait("px", w.at("px"))
                w.wait("s", w.at("s"))
                w.eng.activation(hi[:, cols], psX[:, k, :], ACT.Identity, bias=bias[:, :]).then_inc(sems["ch"], 1)
                if hi2 is not None:
                    w.eng.activation(hi2[0:HD, cols], psX[0:HD, k, :], ACT.Identity, bias=bias[0:HD, :]).then_inc(sems["ch"], 1)
            w.inc("ch", 1 if hi2 is None else 2)
            if w.on("vector"):
                r = slice(lo_from, lo_from + HD)
                w.wait("ch", w.at("ch"))
                w.wait("px", w.at("px"))
                w.eng.scalar_tensor_tensor(out=lo[r, cols], in0=psX[r, k, :], scalar=bias[r, :],
                                           in1=hi[r, cols].bitcast(F32), op0=ALU.add, op1=ALU.subtract)\
                    .then_inc(sems["pxr"], 1)
            w.inc("pxr")

        def values_in(w):
            k = bank(w)
            if w.on("tensor"):
                w.wait("pxr", w.at("pxr", 1))
                for t in range(KC):
                    for cc in range(2):
                        last = w.eng.matmul(psX[:, k, t * HD:(t + 1) * HD], xb[:, cc, t * P:(t + 1) * P], wv[:, cc, :],
                                            start=cc == 0, stop=cc == 1)
                last.then_inc(sems["px"], 1)
            w.inc("px")
            if w.on("vector"):
                w.wait("px", w.at("px"))
                w.wait("pv", w.at("pv"))
                w.eng.tensor_tensor(vd[:, :, 0:HD], psX[:, k, :].rearrange("p (t d) -> p t d", d=HD),
                                    bv[:, :].unsqueeze(1).to_broadcast([P, KC, HD]), ALU.add).then_inc(sems["pxr"], 1)
            w.inc("pxr")

        def max_tile(w, u):
            k = bank(w)
            if w.on("tensor"):
                w.wait("pxr", w.at("pxr", 1 if u else 0))
                w.eng.matmul(psX[:, k, :], qA[:, (u // 2) * P:(u // 2 + 1) * P], kA[:, (u % 2) * 512:(u % 2 + 1) * 512],
                             start=True, stop=True).then_inc(sems["px"], 1)
            w.inc("px")
            if w.on("vector"):
                w.wait("px", w.at("px"))
                w.eng.tensor_reduce(mxs[:, u // 2, u % 2:u % 2 + 1], psX[:, k, :], AX.X, ALU.max).then_inc(sems["pxr"], 1)
            w.inc("pxr")

        def max_rows(w):
            if w.on("vector"):
                w.wait("pxr", w.at("pxr"))
                w.link(w.eng.tensor_reduce(mall[:, :], mxs[:, :, :], AX.X, ALU.max), "dv")
                w.link(w.eng.tensor_scalar(m16[:, 0:KC], mall[:, :], -1.0, None, ALU.mult), "dv")
                w.eng.scalar_tensor_tensor(out=m16[:, KC:2 * KC], in0=mall[:, :], scalar=-1.0,
                                           in1=m16[:, 0:KC].bitcast(F32), op0=ALU.mult, op1=ALU.subtract)\
                    .then_inc(sems["m16"], 1)
            else:
                w.inc("dv", 2)
            w.inc("m16")
            k = bank(w)
            if w.on("tensor"):
                w.wait("m16", w.at("m16"))
                w.wait("pxr", w.at("pxr", 1))
                w.eng.transpose(psX[0:16, k, 0:P], m16[:, :].bitcast(F32), ident[:, :]).then_inc(sems["px"], 1)
            w.inc("px")
            if w.on("vector"):
                w.wait("px", w.at("px"))
                w.eng.tensor_tensor(qB[HD:HD + 16, :].rearrange("p (b t) -> p b t", t=P),
                                    psX[0:16, k, 0:P].unsqueeze(1).to_broadcast([16, KC, P]),
                                    rowmask[:, :, :], ALU.mult).then_inc(sems["pxr"], 1)
            w.inc("pxr")

        def scores(w, kc):
            n = w.count.get("e", 0) % RING
            if w.on("tensor"):
                w.wait("pxr", w.at("pxr"))
                w.wait("e", w.at("e", RING - 2))
                for a, q in ((0, 0), (0, 1), (1, 0), (1, 1)):
                    kt, qt = (kB, qB) if a else (kA, qA)
                    last = w.eng.matmul(psS[:, n + q, :], kt[:, kc * P:(kc + 1) * P], qt[:, q * 512:(q + 1) * 512],
                                        start=a == 0, stop=a == 1)
                    if a:
                        last.then_inc(sems["s"], 1)
            for q in range(2):
                w.inc("s")
                if w.on("scalar"):
                    w.wait("s", w.at("s"))
                    w.wait("pv", w.at("e", RING - 1))
                    w.eng.activation(pr[:, n + q, :], psS[:, n + q, :], ACT.Exp, scale=SCALE).then_inc(sems["e"], 1)
                w.inc("e")

        def values(w, kc):
            for q in range(2):
                n = w.count.get("pv", 0) % RING
                if w.on("tensor"):
                    w.wait("nm", w.at("nm"))
                    w.wait("e", w.at("pv", -1))
                    w.eng.matmul(psO[:, q, :], vd[:, kc, :], pr[:, n, :],
                                 start=kc == 0, stop=kc == KC - 1).then_inc(sems["pv"], 1)
                w.inc("pv")

        def divide(w):
            if w.on("scalar"):
                w.wait("pv", w.at("pv"))
                w.wait("ot", w.at("ot"))
                w.eng.activation(oU[:, :, :], psO[:, :, :], ACT.Copy).then_inc(sems["nm"], 1)
            w.inc("nm")
            if w.on("vector"):
                w.wait("nm", w.at("nm"))
                w.link(w.eng.transpose(turned[:, :], oU[HD:P, :, :].rearrange("p a b -> p (a b)")), "dv")
                w.link(w.eng.reciprocal(inv[:, :], turned[:, 0:S:32]), "dv")
                w.link(w.eng.transpose(rec[:, :], inv[:, :].unsqueeze(2).to_broadcast([HD, 32, 32])), "dv")
                w.wait("px", w.at("px"))
                w.eng.tensor_tensor(oT[:, :], oU[0:HD, :, :].rearrange("p a b -> p (a b)"), rec[:, :], ALU.mult)\
                    .then_inc(sems["ot"], 1)
            else:
                w.inc("dv", 3)
            w.inc("ot")

        def output(w, b, i):
            par = i % 2
            t = b * TB + i
            if w.on("gpsimd"):
                w.wait("var", w.at("var", 1))
                w.eng.tensor_tensor(xo[:, par, :], X[:, bass.ds(t, 1), :].rearrange("p a c -> p (a c)"), bo[:, :], ALU.add)\
                    .then_inc(sems["xo"], 1)
            w.inc("xo")
            k = bank(w)
            if w.on("tensor"):
                w.wait("ot", w.at("ot"))
                w.wait("pxr", w.at("pxr", 1))
                w.eng.matmul(psX[:, k, 0:D], oT[:, i * P:(i + 1) * P], wo[:, :], start=True, stop=True).then_inc(sems["px"], 1)
            w.inc("px")
            if w.on("vector"):
                w.wait("px", w.at("px"))
                w.wait("xo", w.at("xo"))
                w.wait("y", w.at("y"))
                w.eng.tensor_tensor(res[:, par, :], psX[:, k, 0:D], xo[:, par, :], ALU.add).then_inc(sems["pxr"], 1)
                w.wait("pxr", w.at("pxr", -1))
                w.link(w.eng.bn_stats(bst[:, par, :], res[:, par, :]), "dv")
                w.eng.memset(idle[:, :], 0.0)
                w.eng.bn_aggr(mv[:, par, :], bst[:, par, :]).then_inc(sems["var"], 1)
            else:
                w.inc("dv")
            w.inc("pxr")
            w.inc("var")
            if w.on("gpsimd"):
                w.wait("var", w.at("var"))
                w.link(w.eng.tensor_tensor(rstd[:, par, 0:1], mv[:, par, 1:2], eps[:, :], ALU.add), "pl")
                w.eng.tensor_tensor(rstd[:, par, 1:2], rstd[:, par, 0:1], mhalf[:, :], ALU.pow).then_inc(sems["rstd"], 1)
            else:
                w.inc("pl")
            w.inc("rstd")

        def normed(w, b, i, later):
            if w.on("vector"):
                par = i % 2
                w.wait("rstd", w.at("rstd", later))
                w.eng.tensor_scalar(X[:, bass.ds(b * TB + i, 1), :].rearrange("p a c -> p (a c)"), res[:, par, :],
                                    mv[:, par, 0:1], rstd[:, par, 1:2], ALU.subtract, ALU.mult).then_inc(sems["y"], 1)
            w.inc("y")

        def batch(w, b):
            fetch(w, b)
            for n in range(2):
                project(w, wq, bq, qA, None, qB, 0, n)
                project(w, wk, bk, kA, kB, kA, HD, n)
            values_in(w)
            for u in range(2 * KC):
                max_tile(w, u)
            max_rows(w)
            scores(w, 0)
            for kc in range(KC):
                if kc < KC - 1:
                    scores(w, kc + 1)
                values(w, kc)
            divide(w)
            for i in range(TB):
                output(w, b, i)
                if i:
                    normed(w, b, i - 1, 1)
            normed(w, b, TB - 1, 0)

        def walk(w):
            batch(w, 0)
            w.loop(w.eng, B - 1, lambda i: batch(w, i + 1))

        @block.sync
        def _(eng):
            src = w_qkv.rearrange("(a p) o -> p a o", p=P)
            for t, c in ((wq, 0), (wk, HD)):
                for k in range(2):
                    eng.dma_start(t[:, :, k * HD:(k + 1) * HD], src[:, :, c:c + HD]).then_inc(sems["w"], 16)
            eng.dma_start(wv[:, :, :], src[:, :, 2 * HD:3 * HD]).then_inc(sems["w"], 16)
            eng.dma_start(wo[:, :], w_out).then_inc(sems["w"], 16)
            bcol = b_qkv.rearrange("(p a) -> p a", a=1)
            for t, c in ((bq, 0), (bk, HD)):
                for k in range(2):
                    eng.dma_start(t[k * HD:(k + 1) * HD, :], bcol[c:c + HD, :], allow_slow_non_contiguous=True).then_inc(sems["w"], 16)
            eng.dma_start(bv[:, :], b_qkv[2 * HD:3 * HD].partition_broadcast(P)).then_inc(sems["w"], 16)
            eng.dma_start(bo[:, :], b_out.partition_broadcast(P)).then_inc(sems["w"], 16)

        @block.gpsimd
        def _(eng):
            make_identity(eng, ident, sems["cst"])
            eng.memset(rowmask[:, :, :], 0.0).then_inc(sems["cst"], 1)
            eng.wait_ge(sems["cst"], 3)
            for off in (0, KC):
                eng.affine_select(out=rowmask[:, :, :], in_=rowmask[:, :, :], compare_op=ALU.not_equal, fill=1.0,
                                  base=-off, pattern=[[-1, KC], [0, P]], channel_multiplier=1).then_inc(sems["cst"], 1)
                eng.wait_ge(sems["cst"], 4 if off == 0 else 5)
            eng.memset(mhalf[:, :], -0.5).then_inc(sems["cst"], 1)
            eng.memset(eps[:, :], EPS).then_inc(sems["cst"], 1)
            eng.wait_ge(sems["cst"], 7)
            eng.wait_ge(sems["w"], NW)
            walk(Writer(nc, eng, "gpsimd", sems))

        @block.vector
        def _(eng):
            eng.memset(vd[:, :, HD:2 * HD], 1.0).then_inc(sems["cstv"], 1)
            eng.memset(qB[HD:P, :].bitcast(F32), 0.0).then_inc(sems["cstv"], 1)
            eng.memset(kB[HD:P, :].bitcast(F32), 0.0).then_inc(sems["cstv"], 1)
            eng.wait_ge(sems["cstv"], 3)
            eng.memset(kB[HD:HD + 16, :].bitcast(F32), 1.0).then_inc(sems["cstv"], 1)
            eng.wait_ge(sems["cst"], 5)
            eng.wait_ge(sems["w"], NW)
            walk(Writer(nc, eng, "vector", sems))

        @block.scalar
        def _(eng):
            eng.preload_act_table(ACT.Exp)
            eng.wait_ge(sems["w"], NW)
            walk(Writer(nc, eng, "scalar", sems))

        @block.tensor
        def _(eng):
            eng.wait_ge(sems["w"], NW)
            eng.wait_ge(sems["cst"], 5)
            eng.wait_ge(sems["cstv"], 4)
            walk(Writer(nc, eng, "tensor", sems))


def two_layers(nc, a, out):
    B, TK, _ = a["ctx"].shape
    TOK = a["x"].shape[0]
    NT = TOK // P
    E = a["L0_ffn_W1"].shape[0]
    y = nc.dram_tensor("y_scratch", (TOK, D), F32, kind="Internal").ap()
    weights = nc.dram_tensor("weights_scratch", (B, TOK // B), F32, kind="Internal").ap()
    layer0_self_attention(nc, a["x"], a["wqT"], a["wkT"], a["wvT"], a["woT"], y)
    with nc.sbuf_tensor("X", [P, NT, D], F32) as X, nc.sbuf_tensor("xT", [P, 2, TOK], F32) as xT, \
            nc.sbuf_tensor("gates", [P, NT, E], F32) as gates, nc.sbuf_tensor("chosen", [P, NT, 1], F32) as chosen:

        load_tokens(nc, y, X, "l")
        cross_attention(nc, "c0", X, a["ctx"], *[a["L0_xattn_" + n] for n in ("Wq", "bq", "Wk", "bk", "Wv", "bv", "Wo", "bo")],
                        a["mask"])
        turn_tokens(nc, "t0", X, xT)
        expert_gates(nc, xT, a["L0_ffn_w_red"], a["L0_ffn_wg"], gates)
        gated_mlps(nc, "f0", X, xT, gates, *[a["L0_ffn_" + n] for n in ("W1", "b1", "W2", "b2")], False)

        turn_tokens(nc, "t1", X, xT)
        layer1_self_attention(nc, X, xT, *[a["L1_attn_" + n] for n in ("W_qkv", "b_qkv", "W_out", "b_out")], B)
        cross_attention(nc, "c1", X, a["ctx"], *[a["L1_xattn_" + n] for n in ("Wq", "bq", "Wk", "bk", "Wv", "bv", "Wo", "bo")],
                        None)
        turn_tokens(nc, "t2", X, xT)
        choose_tokens(nc, xT, a["L1_ffn_w_r"], a["L1_ffn_b_r"], weights, TOK // B // 2, chosen)
        gated_mlps(nc, "f1", X, xT, chosen, *[a["L1_ffn_" + n] for n in ("W1", "b1", "W2", "b2")], True, out=out)


def kernel(**inputs):
    import numpy as np
    import concourse.bacc as _bacc
    from concourse import mybir as _mybir
    from concourse.bass_utils import run_bass_kernel_spmd as _run

    i = {n: np.asarray(v) for n, v in inputs.items()}
    shape = i["x"].shape
    d = shape[-1]
    data = {"x": i["x"].reshape(-1, d), "ctx": i["ctx_1024"], "mask": i["mask_BxS2_bk0"].reshape(-1).view(np.int32)}
    data["wqT"], data["wkT"], data["woT"] = (i["L0_attn_" + n].T for n in ("wq", "wk", "wo"))
    data["wvT"] = i["L0_attn_wv"].T.reshape(d, 4, 2, 2, 64).transpose(0, 2, 3, 1, 4).reshape(d, -1)
    for n in ("Wq", "bq", "Wo", "bo"):
        data["L0_xattn_" + n] = i["L0_xattn_" + n]
    for k, n in enumerate("kv"):
        data["L0_xattn_W" + n] = i["L0_xattn_Wkv"][:, k * d:(k + 1) * d]
        data["L0_xattn_b" + n] = i["L0_xattn_bkv"][k * d:(k + 1) * d]
    for k, n in enumerate("qkv"):
        data["L1_xattn_W" + n] = i["L1_xattn_in_proj_weight"][:, k * d:(k + 1) * d]
        data["L1_xattn_b" + n] = i["L1_xattn_in_proj_bias"][k * d:(k + 1) * d]
    data["L1_xattn_Wo"], data["L1_xattn_bo"] = i["L1_xattn_out_proj_weight"], i["L1_xattn_out_proj_bias"]
    for n in ("w_red", "wg", "W1", "b1", "W2", "b2"):
        data["L0_ffn_" + n] = i["L0_ffn_" + n]
    for n in ("W_qkv", "b_qkv", "W_out", "b_out"):
        data["L1_attn_" + n] = i["L1_attn_" + n]
    for n in ("w_r", "b_r"):
        data["L1_ffn_" + n] = i["L1_ffn_" + n]
    for n in ("W1", "b1", "W2", "b2"):
        data["L1_ffn_" + n] = i["L1_ffn_" + n][None]

    nc = _bacc.Bacc("TRN2", target_bir_lowering=False, num_devices=1)
    data = {n: np.ascontiguousarray(v) for n, v in data.items()}
    args = {n: nc.dram_tensor(n, v.shape, _mybir.dt.from_np(v.dtype), kind="ExternalInput").ap() for n, v in data.items()}
    out = nc.dram_tensor("out", (shape[0] * shape[1], d), _mybir.dt.float32, kind="ExternalOutput").ap()
    two_layers(nc, args, out)
    r = _run(nc, [data], core_ids=[0])
    return r.results[0]["out"].reshape(shape)
```

```python
from contextlib import ExitStack

import concourse.bass as bass
from concourse import mybir

F32 = mybir.dt.float32
F32R = mybir.dt.float32r
ALU = mybir.AluOpType
ACT = mybir.ActivationFunctionType
AX = mybir.AxisListType
P = 128
D = 256
EPS = 1e-5


class Tally:

    def __init__(self, sems):
        self.sems = sems
        self.count = {}
        self.per = None
        self.reg = None
        self.mute = False

    def inc(self, name, n=1):
        self.count[name] = self.count.get(name, 0) + n

    def at(self, name, back=0):
        value = self.count.get(name, 0) - back
        if self.reg is not None and self.per.get(name, 0):
            assert value > 0 or self.mute, name
            return self.reg * self.per[name] + value
        return value

    def loop(self, eng, trips, body):
        start = dict(self.count)
        self.mute = True
        body(0)
        self.mute = False
        per = {k: v - start.get(k, 0) for k, v in self.count.items()}
        self.count = dict(start)
        with eng.Fori(0, trips) as reg:
            self.per, self.reg = per, reg
            body(reg)
        self.per = self.reg = None
        self.count = {k: start.get(k, 0) + trips * n for k, n in per.items()}


class Writer(Tally):

    def __init__(self, nc, eng, role, sems, weights=0):
        super().__init__(sems)
        self.nc, self.eng, self.role = nc, eng, role
        self.weights = weights

    def on(self, role):
        return self.role == role and not self.mute

    def wait(self, name, value):
        if isinstance(value, int) and value <= 0:
            return
        self.eng.wait_ge(self.sems[name], value)

    def waits(self, *pairs):
        pairs = [(name, value if isinstance(value, int) else self.eng.to_reg(value)) for name, value in pairs]
        if not all(isinstance(value, int) for _, value in pairs):
            self.eng.wait_ge(self.sems["w"], self.weights)
        for name, value in pairs:
            self.wait(name, value)

    def fixed(self, value):
        return value if isinstance(value, int) else self.eng.snap(value)

    def link(self, ins, name):
        if ins is not None:
            ins.then_inc(self.sems[name], 1)
        self.inc(name)
        if ins is not None:
            self.wait(name, self.at(name))


class Room:

    def __init__(self, nc, ctx, tag):
        self.nc, self.ctx, self.tag = nc, ctx, tag
        self.sems = []
        ctx.callback(self.clear)

    def clear(self):
        self.nc.clear_and_free_semaphores(self.sems)
        self.nc.all_engine_barrier()

    def sb(self, name, shape, dt=F32):
        return self.ctx.enter_context(self.nc.sbuf_tensor(f"{self.tag}_{name}", shape, dt))

    def ps(self, name, shape, dt=F32):
        return self.ctx.enter_context(self.nc.psum_tensor(f"{self.tag}_{name}", shape, dt))

    def sem(self, name):
        self.sems.append(self.nc.alloc_semaphore(name=f"{self.tag}_{name}"))
        return self.sems[-1]


def make_identity(pool, tile, sem):
    pool.memset(tile[:, :], 0.0).then_inc(sem, 1)
    pool.wait_ge(sem, 1)
    pool.affine_select(out=tile[:, :], in_=tile[:, :], compare_op=ALU.not_equal, fill=1.0, base=0,
                       pattern=[[-1, P]], channel_multiplier=1).then_inc(sem, 1)


def layer0_self_attention(nc, x, wqT, wkT, wvT, woT, y):
    TOK = x.shape[0]
    HD = 64
    SEG = wqT.shape[1] // HD
    ROWS = SEG * HD
    GH = 4
    GT = GH * HD
    NG = TOK // GT
    KC = ROWS // P
    SCALE = HD ** -0.5
    RING = 4
    XB = 3

    with ExitStack() as ctx:
        m = Room(nc, ctx, "a")
        wq = m.sb("wq", [P, 2, SEG * HD])
        wk = m.sb("wk", [P, 2, SEG * HD])
        wv = m.sb("wv", [P, 2, SEG * HD])
        wo = m.sb("wo", [P, KC, D])
        ident = m.sb("ident", [P, P])
        rowmask = m.sb("rowmask", [16, KC, P], mybir.dt.bfloat16)
        xs = m.sb("xs", [P, 2, D])
        xg = m.sb("xg", [P, XB, 2, D])
        xT = m.sb("xT", [P, 2, GT])
        qhi, qlo, khi, klo = (m.sb(n, [P, 2, GH, 512], F32R) for n in ("qhi", "qlo", "khi", "klo"))
        vghi, vglo = (m.sb(n, [P, 2, 2 * 512], F32R) for n in ("vghi", "vglo"))
        qA = m.sb("qA", [P, 2, ROWS], F32R)
        qB = m.sb("qB", [P, 2, ROWS], F32R)
        kA = m.sb("kA", [P, 2, ROWS], F32R)
        kB = m.sb("kB", [P, 2, ROWS], F32R)
        vhi = m.sb("vhi", [P, 2, KC, 2 * HD], F32R)
        vlo = m.sb("vlo", [P, 2, KC, HD], F32R)
        pr = m.sb("pr", [P, 2, 512])
        plo = m.sb("plo", [P, RING, 512], F32R)
        phi = m.sb("phi", [P, RING, 512], F32R)
        mxs = m.sb("mxs", [P, KC, 2])
        mall = m.sb("mall", [P, KC])
        m16 = m.sb("m16", [P, 2 * KC], F32R)
        oU = m.sb("oU", [P, 2, 512])
        rec = m.sb("rec", [HD, 2, 512])
        inv = m.sb("inv", [HD, ROWS // 32])
        oT = m.sb("oT", [P, 2, KC, P])
        res = m.sb("res", [P, 2, D])
        bst = m.sb("bst", [P, 2, 6])
        mv = m.sb("mv", [P, 2, 2])
        rstd = m.sb("rstd", [P, 2, 2])
        mhalf = m.sb("mhalf", [P, 1])
        eps = m.sb("eps", [P, 1])
        idle = m.sb("idle", [1, 1])
        psS = m.ps("psS", [P, 2, 512])
        psO = m.ps("psO", [P, 2, 512])
        psX = m.ps("psX", [P, 2, 512])
        psM = m.ps("psM", [P, 512])

        names = ("cst", "cstv", "w", "x", "mi", "md", "ch", "ba0", "ba1", "bb0", "bb1", "bv", "mx", "mxr", "m16", "s", "e", "ph", "lo",
                 "pv", "nm", "ot", "var", "pl", "rstd", "y", "yo", "dv")
        sems = {n: m.sem(n) for n in names}
        block = ctx.enter_context(nc.Block())

        def task_list():
            todo = [("T",)] + [("Q", c) for c in range(KC)] + [("K", c) for c in range(KC)] + \
                   [("V", tt, c2) for tt in range(2) for c2 in range(2)]
            slots = {}
            for j in range(GH):
                for kc in range(KC):
                    if kc == 6:
                        slots[j, kc] = ("M",)
                    elif kc == 3 and j % 2 == 0:
                        slots[j, kc] = ("O",)
                    elif (j, kc) >= (0, 1) and todo:
                        slots[j, kc] = todo.pop(0)
            assert not todo
            return slots

        SLOTS = task_list()
        XPLAN = {1: 3, 2: 3, 3: 3, 4: 3, 5: 4}

        def load_x(w, g):
            if w.on("sync"):
                row, slot = w.fixed(g % NG * GT), w.fixed(g % XB)
                w.waits(("var", w.at("var")), ("mi", w.at("mi")))
                w.eng.dma_start(xg[:, bass.ds(slot, 1), :, :],
                                x[bass.ds(row, GT), :].rearrange("(t p) c -> p t c", p=P)).then_inc(sems["x"], 16)
                w.eng.dma_start(xs[:, :, :], x[bass.ds(row, GT), :].rearrange("(t p) c -> p t c", p=P))\
                    .then_inc(sems["x"], 16)
            w.inc("x", 32)

        def misc(w, what, G, buf):
            kind = what[0]
            if w.on("tensor"):
                w.wait("md", w.at("md"))
                if kind == "T":
                    w.wait("x", w.at("x"))
                    for cc in range(2):
                        for tt in range(2):
                            last = w.eng.transpose(psM[:, (2 * cc + tt) * P:(2 * cc + tt + 1) * P],
                                                   xs[:, tt, cc * P:(cc + 1) * P], ident[:, :])
                elif kind in "QK":
                    wt = wq if kind == "Q" else wk
                    c = what[1]
                    for cc in range(2):
                        last = w.eng.matmul(psM[:, 0:GT], wt[:, cc, c * P:(c + 1) * P], xT[:, cc, :],
                                            start=cc == 0, stop=cc == 1)
                elif kind == "V":
                    _, tt, c2 = what
                    for cc in range(2):
                        last = w.eng.matmul(psM[:, :], xT[:, cc, tt * P:(tt + 1) * P],
                                            wv[:, cc, c2 * 512:(c2 + 1) * 512], start=cc == 0, stop=cc == 1)
                elif kind == "M":
                    w.wait("m16", w.at("m16"))
                    last = w.eng.transpose(psM[0:16, 0:P], m16[:, :].bitcast(F32), ident[:, :])
                elif kind == "O":
                    w.wait("ot", w.at("ot"))
                    for c in range(KC):
                        last = w.eng.matmul(psM[:, 0:D], oT[:, buf, c, :], wo[:, c, :], start=c == 0, stop=c == KC - 1)
                last.then_inc(sems["mi"], 1)
            w.inc("mi")
            if kind == "T":
                if w.on("scalar"):
                    w.wait("mi", w.at("mi"))
                    w.eng.activation(xT[:, :, :].rearrange("p a b -> p (a b)"), psM[:, :], ACT.Copy).then_inc(sems["md"], 1)
            elif kind in "QK":
                hi, lo = (qhi, qlo) if kind == "Q" else (khi, klo)
                c = what[1]
                src = psM[:, 0:GT].rearrange("p (h t) -> p h t", t=HD)

                def dst(t):
                    v = t[:, bass.ds(buf, 1), :, c * HD:(c + 1) * HD]
                    return v.rearrange("p b h t -> p (b h) t")
                if w.on("scalar"):
                    if what == ("Q", 0):
                        for n in ("ba0", "ba1", "bb0", "bb1"):
                            w.wait(n, w.at(n))
                    w.wait("mi", w.at("mi"))
                    w.eng.activation(dst(hi), src, ACT.Copy).then_inc(sems["ch"], 1)
                w.inc("ch")
                if w.on("vector"):
                    if what == ("Q", 0):
                        for n in ("ba0", "ba1", "bb0", "bb1"):
                            w.wait(n, w.at(n))
                    w.wait("ch", w.at("ch"))
                    w.eng.tensor_tensor(dst(lo), src, dst(hi).bitcast(F32), ALU.subtract).then_inc(sems["md"], 1)
            elif kind == "V":
                _, tt, c2 = what
                part = slice(c2 * 512, (c2 + 1) * 512)
                if w.on("scalar"):
                    w.wait("bv", w.at("bv"))
                    w.wait("mi", w.at("mi"))
                    w.eng.activation(vghi[:, tt, part], psM[:, :], ACT.Copy).then_inc(sems["ch"], 1)
                w.inc("ch")
                if w.on("vector"):
                    w.wait("bv", w.at("bv"))
                    w.wait("ch", w.at("ch"))
                    w.eng.tensor_tensor(vglo[:, tt, part], psM[:, :], vghi[:, tt, part].bitcast(F32), ALU.subtract)\
                        .then_inc(sems["md"], 1)
            elif kind == "M":
                if w.on("vector"):
                    w.wait("mi", w.at("mi"))
                    w.eng.tensor_tensor(qB[HD:HD + 16, buf, :].rearrange("p (b t) -> p b t", t=P),
                                        psM[0:16, 0:P].unsqueeze(1).to_broadcast([16, KC, P]),
                                        rowmask[:, :, :], ALU.mult).then_inc(sems["md"], 1)
            elif kind == "O":
                if w.on("vector"):
                    w.wait("mi", w.at("mi"))
                    w.wait("yo", w.at("yo"))
                    xr = xg[:, bass.ds(G % XB, 1), buf, :].rearrange("p a c -> p (a c)")
                    w.eng.tensor_tensor(res[:, buf, :], psM[:, 0:D], xr, ALU.add).then_inc(sems["md"], 1)
                    w.wait("md", w.at("md", -1))
                if w.on("vector"):
                    w.link(w.eng.bn_stats(bst[:, buf, :], res[:, buf, :]), "dv")
                    w.eng.memset(idle[:, :], 0.0)
                    w.eng.bn_aggr(mv[:, buf, :], bst[:, buf, :]).then_inc(sems["var"], 1)
                else:
                    w.inc("dv")
                w.inc("var")
                if w.on("gpsimd"):
                    w.wait("var", w.at("var"))
                    w.link(w.eng.tensor_tensor(rstd[:, buf, 0:1], mv[:, buf, 1:2], eps[:, :], ALU.add), "pl")
                    w.eng.tensor_tensor(rstd[:, buf, 1:2], rstd[:, buf, 0:1], mhalf[:, :], ALU.pow).then_inc(sems["rstd"], 1)
                else:
                    w.inc("pl")
                w.inc("rstd")
            w.inc("md")

        def norm_out(w, G, buf):
            if w.on("vector"):
                w.wait("rstd", w.at("rstd"))
                w.eng.tensor_scalar(res[:, buf, :], res[:, buf, :], mv[:, buf, 0:1], rstd[:, buf, 1:2],
                                    ALU.subtract, ALU.mult).then_inc(sems["y"], 1)
            w.inc("y")
            if w.on("sync"):
                row = w.fixed(G * GT + buf * P)
                w.waits(("y", w.at("y")))
                w.eng.dma_start(y[bass.ds(row, P), :], res[:, buf, :]).then_inc(sems["yo"], 16)
            w.inc("yo", 16)

        def build(w, gbuf, j, b):
            if w.on("sync"):
                gbuf = w.fixed(gbuf)
                w.waits(("md", w.at("md")), ("s", w.at("s")))
                for t, rows, src in ((qA, 0, qhi), (qA, HD, qhi), (kA, 0, khi), (kA, HD, klo)):
                    for par in range(2):
                        w.eng.dma_start(t[rows:rows + HD, b, par * 512:(par + 1) * 512].bitcast(F32),
                                        src[par * HD:(par + 1) * HD, bass.ds(gbuf, 1), j, :].bitcast(F32)).then_inc(sems[f"ba{b}"], 16)
                for t, src in ((qB, qlo), (kB, khi)):
                    for par in range(2):
                        w.eng.dma_start(t[0:HD, b, par * 512:(par + 1) * 512].bitcast(F32),
                                        src[par * HD:(par + 1) * HD, bass.ds(gbuf, 1), j, :].bitcast(F32)).then_inc(sems[f"bb{b}"], 16)
            w.inc(f"ba{b}", 8 * 16)
            w.inc(f"bb{b}", 4 * 16)

        def build_v(w, j, b):
            if w.on("sync"):
                w.waits(("md", w.at("md")), ("pv", w.at("pv")))
                tt, half = j // 2, j % 2
                for to, src in ((vhi, vghi), (vlo, vglo)):
                    for c2 in range(2):
                        w.eng.dma_start(to[c2 * HD:(c2 + 1) * HD, b, :, 0:HD].bitcast(F32),
                                        src[half * HD:(half + 1) * HD, tt, c2 * 512:(c2 + 1) * 512]
                                        .rearrange("p (k d) -> p k d", d=HD).bitcast(F32)).then_inc(sems["bv"], 16)
            w.inc("bv", 4 * 16)

        def max_tile(w, u, b):
            if w.on("tensor"):
                if u == 0:
                    w.wait(f"ba{b}", w.at(f"ba{b}"))
                w.wait("mxr", w.at("mxr", 1))
                w.eng.matmul(psX[:, u % 2, :], qA[:, b, (u // 2) * P:(u // 2 + 1) * P], kA[:, b, (u % 2) * 512:(u % 2 + 1) * 512],
                             start=True, stop=True).then_inc(sems["mx"], 1)
            w.inc("mx")
            if w.on("vector"):
                w.wait("mx", w.at("mx"))
                w.eng.tensor_reduce(mxs[:, u // 2, u % 2:u % 2 + 1], psX[:, u % 2, :], AX.X, ALU.max).then_inc(sems["mxr"], 1)
            w.inc("mxr")

        def max_rows(w):
            if w.on("vector"):
                w.wait("mxr", w.at("mxr"))
                w.link(w.eng.tensor_reduce(mall[:, :], mxs[:, :, :], AX.X, ALU.max), "dv")
                w.link(w.eng.tensor_scalar(m16[:, 0:KC], mall[:, :], -1.0, None, ALU.mult), "dv")
                w.eng.scalar_tensor_tensor(out=m16[:, KC:2 * KC], in0=mall[:, :], scalar=-1.0,
                                           in1=m16[:, 0:KC].bitcast(F32), op0=ALU.mult, op1=ALU.subtract)\
                    .then_inc(sems["m16"], 1)
            else:
                w.inc("dv", 2)
            w.inc("m16")

        def scores(w, kc, b):
            if w.on("tensor"):
                if kc == 0:
                    w.wait(f"bb{b}", w.at(f"bb{b}"))
                    w.wait("md", w.at("md"))
                w.wait("e", w.at("e"))
                for a, q in ((0, 0), (0, 1), (1, 0), (1, 1)):
                    kt, qt = (kB, qB) if a else (kA, qA)
                    last = w.eng.matmul(psS[:, q, :], kt[:, b, kc * P:(kc + 1) * P], qt[:, b, q * 512:(q + 1) * 512],
                                        start=a == 0, stop=a == 1)
                    if a:
                        last.then_inc(sems["s"], 1)
            n = self_ring(w)
            for q in range(2):
                w.inc("s")
                if w.on("scalar"):
                    w.wait("s", w.at("s"))
                    w.wait("lo", w.at("e", 1))
                    w.eng.activation(pr[:, q, :], psS[:, q, :], ACT.Exp, scale=SCALE).then_inc(sems["e"], 1)
                    w.wait("e", w.at("e", -1))
                    w.wait("pv", w.at("e", RING - 1))
                    w.eng.activation(phi[:, n + q, :], pr[:, q, :], ACT.Copy).then_inc(sems["ph"], 1)
                w.inc("e")
                w.inc("ph")

        def low_parts(w):
            for q in range(2):
                n = (w.count["ph"] - 2 + q) % RING
                if w.on("gpsimd"):
                    w.wait("ph", w.at("ph", 1 - q))
                    w.eng.tensor_tensor(plo[:, n, :], pr[:, q, :], phi[:, n, :].bitcast(F32),
                                        ALU.subtract).then_inc(sems["lo"], 1)
                w.inc("lo")

        def self_ring(w):
            return w.count.get("e", 0) % RING

        def values_high(w, kc, b):
            if w.on("tensor"):
                if kc == 0:
                    w.wait("bv", w.at("bv"))
                    w.wait("nm", w.at("nm"))
                for q in range(2):
                    n = (w.count.get("pv", 0) + q) % RING
                    w.wait("ph", w.at("pv", -1 - q))
                    w.eng.matmul(psO[:, q, :], vhi[:, b, kc, :], phi[:, n, :], start=kc == 0, stop=False)
                    w.eng.matmul(psO[0:HD, q, :], vlo[:, b, kc, :], phi[:, n, :], start=False, stop=False)

        def values_low(w, kc, b):
            for q in range(2):
                n = w.count.get("pv", 0) % RING
                if w.on("tensor"):
                    w.wait("lo", w.at("pv", -1))
                    w.eng.matmul(psO[:, q, :], vhi[:, b, kc, :], plo[:, n, :],
                                 start=False, stop=kc == KC - 1).then_inc(sems["pv"], 1)
                w.inc("pv")

        def divide(w, j):
            if w.on("scalar"):
                w.wait("pv", w.at("pv"))
                w.wait("ot", w.at("ot"))
                w.eng.activation(oU[:, :, :], psO[:, :, :], ACT.Copy).then_inc(sems["nm"], 1)
            w.inc("nm")
            if w.on("vector"):
                w.wait("nm", w.at("nm"))
                w.link(w.eng.transpose(rec[:, :, :].rearrange("p a b -> p (a b)"), oU[HD:P, :, :].rearrange("p a b -> p (a b)")), "dv")
                w.link(w.eng.reciprocal(inv[:, :], rec[:, :, :].rearrange("p a b -> p (a b)")[:, 0:ROWS:32]), "dv")
                w.link(w.eng.transpose(rec[:, :, :].rearrange("p a b -> p (a b)"),
                                       inv[:, :].unsqueeze(2).to_broadcast([HD, 32, 32]).rearrange("p a b -> p a b")), "dv")
                for q in range(2):
                    w.eng.tensor_tensor(oT[q * HD:(q + 1) * HD, j // 2, :, (j % 2) * HD:(j % 2 + 1) * HD],
                                        oU[0:HD, q, :].rearrange("p (c t) -> p c t", t=HD),
                                        rec[:, q, :].rearrange("p (c t) -> p c t", t=HD), ALU.mult)\
                        .then_inc(sems["ot"], 1)
            else:
                w.inc("dv", 3)
            w.inc("ot", 2)

        def group(w, G, first=False, last=False):
            for j in range(GH):
                more = not (last and j == GH - 1)
                b, nb = j % 2, (j + 1) % 2
                for kc in range(KC):
                    n = XPLAN.get(kc, 0) if more else 0
                    u = sum(XPLAN.get(i, 0) for i in range(kc))

                    def max_tiles(first, last):
                        for i in range(first, min(last, n)):
                            max_tile(w, u + i, nb)
                    if kc < KC - 1:
                        scores(w, kc + 1, b)
                    elif more:
                        scores(w, 0, nb)
                    if kc == KC - 2 and not (last and j >= 2):
                        build(w, (G + (j + 2) // GH) % 2, (j + 2) % GH, b)
                    max_tiles(0, 1)
                    task = SLOTS.get((j, kc))
                    if task == ("M",) and more:
                        misc(w, task, G, nb)
                    values_high(w, kc, b)
                    max_tiles(1, 2)
                    if task and task[0] != "M":
                        if task[0] == "O":
                            if not (first and j == 0):
                                misc(w, task, G - (j == 0), 1 if j == 0 else 0)
                        elif not last:
                            misc(w, task, G + 1, (G + 1) % 2)
                    max_tiles(2, n)
                    values_low(w, kc, b)
                    if more or kc < KC - 1:
                        low_parts(w)
                    if more and kc == 5:
                        max_rows(w)
                    if kc == KC - 1:
                        divide(w, j)
                    if kc == 4 and j % 2 == 0 and not (first and j == 0):
                        norm_out(w, G - (j == 0), 1 if j == 0 else 0)
                    if kc == 1 and more:
                        build_v(w, (j + 1) % GH, nb)
                    if kc == 7 and j == 1 and not last:
                        load_x(w, G + 2)

        def walk(w):
            load_x(w, 0)
            misc(w, ("T",), 0, 0)
            load_x(w, 1)
            for kind in "QK":
                for c in range(KC):
                    misc(w, (kind, c), 0, 0)
            build(w, 0, 0, 0)
            build(w, 0, 1, 1)
            for tt in range(2):
                for c2 in range(2):
                    misc(w, ("V", tt, c2), 0, 0)
            build_v(w, 0, 0)
            for u in range(2 * KC):
                max_tile(w, u, 0)
            max_rows(w)
            misc(w, ("M",), 0, 0)
            scores(w, 0, 0)
            low_parts(w)
            group(w, 0, first=True)
            w.loop(w.eng, NG - 2, lambda i: group(w, i + 1))
            group(w, NG - 1, last=True)
            misc(w, ("O",), NG - 1, 1)
            norm_out(w, NG - 1, 1)
            return w

        @block.sync
        def _(eng):
            for t, src in ((wq, wqT), (wk, wkT), (wv, wvT)):
                eng.dma_start(t[:, :, :], src.rearrange("(a p) o -> p a o", p=P)).then_inc(sems["w"], 16)
            eng.dma_start(wo[:, :, :], woT.rearrange("(c p) e -> p c e", p=P)).then_inc(sems["w"], 16)
            w = walk(Writer(nc, eng, "sync", sems, weights=64))
            w.wait("yo", w.at("yo"))

        @block.gpsimd
        def _(eng):
            make_identity(eng, ident, sems["cst"])
            eng.memset(rowmask[:, :, :], 0.0).then_inc(sems["cst"], 1)
            eng.wait_ge(sems["cst"], 3)
            for off in (0, KC):
                eng.affine_select(out=rowmask[:, :, :], in_=rowmask[:, :, :], compare_op=ALU.not_equal, fill=1.0,
                                  base=-off, pattern=[[-1, KC], [0, P]], channel_multiplier=1).then_inc(sems["cst"], 1)
                eng.wait_ge(sems["cst"], 4 if off == 0 else 5)
            eng.memset(mhalf[:, :], -0.5).then_inc(sems["cst"], 1)
            eng.memset(eps[:, :], EPS).then_inc(sems["cst"], 1)
            eng.wait_ge(sems["cst"], 7)
            walk(Writer(nc, eng, "gpsimd", sems))

        @block.vector
        def _(eng):
            eng.memset(vhi[:, :, :, HD:2 * HD].bitcast(F32), 1.0).then_inc(sems["cstv"], 1)
            eng.memset(qB[HD:P, :, :].bitcast(F32), 0.0).then_inc(sems["cstv"], 1)
            eng.memset(kB[HD:P, :, :].bitcast(F32), 0.0).then_inc(sems["cstv"], 1)
            eng.wait_ge(sems["cstv"], 3)
            eng.memset(kB[HD:HD + 16, :, :].bitcast(F32), 1.0).then_inc(sems["cstv"], 1)
            eng.wait_ge(sems["cst"], 6)
            walk(Writer(nc, eng, "vector", sems))

        @block.scalar
        def _(eng):
            eng.preload_act_table(ACT.Exp)
            walk(Writer(nc, eng, "scalar", sems))

        @block.tensor
        def _(eng):
            eng.wait_ge(sems["w"], 64)
            eng.wait_ge(sems["cst"], 6)
            eng.wait_ge(sems["cstv"], 4)
            walk(Writer(nc, eng, "tensor", sems))


def load_tokens(nc, y, X, tag):
    with ExitStack() as ctx:
        m = Room(nc, ctx, tag)
        came = m.sem("came")
        block = ctx.enter_context(nc.Block())

        @block.sync
        def _(eng):
            src = y.rearrange("(t p) c -> p t c", p=P)
            n = X.shape[1] // 4
            for i in range(4):
                eng.dma_start(X[:, i * n:(i + 1) * n, :], src[:, i * n:(i + 1) * n, :]).then_inc(came, 16)
            eng.wait_ge(came, 64)


def cross_attention(nc, tag, X, kv, w_q, b_q, w_k, b_k, w_v, b_v, w_o, b_o, mask):
    B, TK, _ = kv.shape
    NT = X.shape[1]
    TB = NT // B
    H, HD = 16, 16
    KP = 80
    NCH = H * KP // P
    HALF = H // 2
    SCALE = HD ** -0.5
    FAR = -1e30
    NW = 16 * (9 if mask is not None else 8)

    with ExitStack() as ctx:
        m = Room(nc, ctx, tag)
        wq, wk, wv, wo = (m.sb(n, [P, 2, D]) for n in ("wq", "wk", "wv", "wo"))
        bq, bk = (m.sb(n, [P, 2]) for n in ("bq", "bk"))
        bqs = m.sb("bqs", [P, 2])
        bv = m.sb("bv", [P, D])
        bo = m.sb("bo", [P, D])
        ident = m.sb("ident", [P, P])
        hmask = m.sb("hmask", [P, HALF])
        cx = m.sb("cx", [KP, D])
        cxT = m.sb("cxT", [P, 2, HALF, KP])
        vmask = m.sb("vmask", [P, NCH // 2, HALF])
        kt = m.sb("kt", [P, 2, KP])
        vt = m.sb("vt", [P, NCH // 2, D])
        kblk = m.sb("kblk", [P, B, 2, HALF, KP])
        vall = m.sb("vall", [P, B, NCH, P])
        vs = m.sb("vs", [P, NCH, P])
        mraw = m.sb("mraw", [P, B * TK // 4], mybir.dt.int32)
        mbias = m.sb("mbias", [P, B, KP])
        xs = m.sb("xs", [P, D])
        xb = m.sb("xb", [P, D])
        xT = m.sb("xT", [P, 2, P])
        qT = m.sb("qT", [P, 2, P])
        E = m.sb("E", [P, 2, H, KP])
        mx = m.sb("mx", [P, H])
        sm = m.sb("sm", [P, H])
        inv = m.sb("inv", [P, 2, H])
        pT = m.sb("pT", [P, NCH, P])
        oT = m.sb("oT", [P, 2, P])
        res = m.sb("res", [P, 2, D])
        bst = m.sb("bst", [P, 2, 6])
        mv = m.sb("mv", [P, 2, 2])
        rstd = m.sb("rstd", [P, 2, 2])
        mhalf = m.sb("mhalf", [P, 1])
        eps = m.sb("eps", [P, 1])
        idle = m.sb("idle", [1, 1])
        psQ = m.ps("psQ", [P, 2, 2, P])
        psS = m.ps("psS", [P, 4, 512])
        psP = m.ps("psP", [P, 2, 4, P])
        psO = m.ps("psO", [P, 2, D])
        names = ("cst", "cstv", "w", "cx", "ct", "cte", "kv", "kve", "vd", "dv", "xs", "tr", "xt", "q", "qe", "s",
                 "sa", "sb", "ex", "sm", "pn", "pt", "pe", "pv", "pve", "xb", "o", "var", "pl", "rstd", "y", "ph")
        sems = {n: m.sem(n) for n in names}
        block = ctx.enter_context(nc.Block())

        def prepare(w, b):
            if w.on("gpsimd"):
                w.waits(("ct", w.at("ct")))
                w.eng.dma_start(cx[0:TK, :], kv[bass.ds(b, 1), :, :].rearrange("b k c -> (b k) c")).then_inc(sems["cx"], 16)
            w.inc("cx", 16)
            if w.on("tensor"):
                w.wait("cx", w.at("cx"))
                w.wait("kve", w.at("kve"))
                for cc in range(2):
                    last = w.eng.transpose(psQ[:, 0, cc, 0:KP], cx[:, cc * P:(cc + 1) * P], ident[0:KP, 0:KP])
                last.then_inc(sems["ct"], 1)
            w.inc("ct")
            if w.on("scalar"):
                w.wait("ct", w.at("ct"))
                w.wait("kv", w.at("kv"))
                w.eng.activation(cxT[:, :, :, :], psQ[:, 0, :, 0:KP].unsqueeze(2).to_broadcast([P, 2, HALF, KP]), ACT.Copy).then_inc(sems["cte"], 1)
            w.inc("cte")
            if w.on("tensor"):
                w.wait("cte", w.at("cte"))
                for hh in range(2):
                    for cc in range(2):
                        w.eng.matmul(psQ[:, 1, hh, 0:KP], wk[:, cc, hh * P:(hh + 1) * P], cxT[:, cc, 0, :],
                                     start=cc == 0, stop=cc == 1)
                for i in range(NCH // 2):
                    for cc in range(2):
                        rows = cxT[:, cc, :, :].rearrange("p h k -> p (h k)")[:, i * P:(i + 1) * P]
                        last = w.eng.matmul(psS[:, i // 2, (i % 2) * D:(i % 2 + 1) * D], rows, wv[:, cc, :],
                                            start=cc == 0, stop=cc == 1)
                last.then_inc(sems["kv"], 1)
            w.inc("kv")
            if w.on("vector"):
                w.wait("kv", w.at("kv"))
                w.wait("dv", w.at("dv"))
                w.wait("vd", w.at("vd"))
                w.link(w.eng.tensor_tensor(kt[:, :, :], psQ[:, 1, :, 0:KP], bk[:, :].unsqueeze(2).to_broadcast([P, 2, KP]),
                                           ALU.add), "dv")
                w.link(w.eng.tensor_tensor(vt[:, 0:4, :], psS[:, 0:2, :].rearrange("p a (i c) -> p (a i) c", i=2),
                                           bv[:, :].unsqueeze(1).to_broadcast([P, 4, D]), ALU.add), "dv")
                w.eng.tensor_tensor(vt[:, 4, :], psS[:, 2, 0:D], bv[:, :], ALU.add).then_inc(sems["kve"], 1)
                w.wait("kve", w.at("kve", -1))
                for hh in range(2):
                    w.link(w.eng.tensor_tensor(kblk[:, bass.ds(b, 1), hh, :, :].rearrange("p b h k -> p (b h) k"),
                                               kt[:, hh:hh + 1, :].to_broadcast([P, HALF, KP]),
                                               hmask[:, :].unsqueeze(2).to_broadcast([P, HALF, KP]), ALU.mult), "dv")
                    for i in range(NCH // 2):
                        w.eng.tensor_tensor(vall[:, bass.ds(b, 1), hh * 5 + i, :].rearrange("p b (h d) -> p (b h) d", d=HD),
                                            vt[:, i, hh * P:(hh + 1) * P].rearrange("p (h d) -> p h d", d=HD),
                                            vmask[:, i, :].unsqueeze(2).to_broadcast([P, HALF, HD]), ALU.mult)\
                            .then_inc(sems["vd"], 1)
            else:
                w.inc("dv", 4)
            w.inc("kve")
            w.inc("vd", NCH)

        def copy_x(w, t):
            if w.on("gpsimd"):
                w.wait("tr", w.at("tr"))
                w.eng.tensor_copy(xs[:, :], X[:, bass.ds(t, 1), :].rearrange("p a c -> p (a c)")).then_inc(sems["xs"], 1)
            w.inc("xs")

        def turn_x(w):
            if w.on("tensor"):
                w.wait("xs", w.at("xs"))
                w.wait("xt", w.at("xt"))
                w.wait("qe", w.at("qe"))
                for cc in range(2):
                    last = w.eng.transpose(psQ[:, 0, cc, :], xs[:, cc * P:(cc + 1) * P], ident[:, :])
                last.then_inc(sems["tr"], 1)
            w.inc("tr")
            if w.on("scalar"):
                w.wait("tr", w.at("tr"))
                w.wait("q", w.at("q"))
                w.eng.activation(xT[:, :, :], psQ[:, 0, :, :], ACT.Copy).then_inc(sems["xt"], 1)
            w.inc("xt")

        def queries(w):
            if w.on("tensor"):
                w.wait("xt", w.at("xt"))
                w.wait("qe", w.at("qe"))
                for hh in range(2):
                    for cc in range(2):
                        last = w.eng.matmul(psQ[:, 1, hh, :], wq[:, cc, hh * P:(hh + 1) * P], xT[:, cc, :],
                                            start=cc == 0, stop=cc == 1)
                last.then_inc(sems["q"], 1)
            w.inc("q")
            if w.on("scalar"):
                w.wait("q", w.at("q"))
                w.wait("s", w.at("s"))
                for hh in range(2):
                    last = w.eng.activation(qT[:, hh, :], psQ[:, 1, hh, :], ACT.Identity, bias=bqs[:, hh:hh + 1], scale=SCALE)
                last.then_inc(sems["qe"], 1)
            w.inc("qe")

        def scores(w, t):
            b = t // TB
            if w.on("tensor"):
                w.wait("qe", w.at("qe"))
                w.wait("sa", w.at("sa"))
                for hh in range(2):
                    for g in range(2):
                        last = w.eng.matmul(psS[:, 2 * hh + g, 0:4 * KP], qT[:, hh, :],
                                            kblk[:, bass.ds(b, 1), hh, 4 * g:4 * g + 4, :].rearrange("p b h k -> p (b h k)"),
                                            start=True, stop=True)
                last.then_inc(sems["s"], 1)
            w.inc("s")

        def less_max(w, t, par):
            b = t // TB
            if w.on("vector"):
                w.wait("s", w.at("s"))
                w.wait("pt", w.at("pt"))
                e4 = E[:, par, :, :].rearrange("p (g h) k -> p g h k", g=4)
                s4 = psS[:, :, 0:4 * KP].rearrange("p g (h k) -> p g h k", k=KP)
                for g in range(4):
                    last = w.eng.tensor_tensor(e4[:, g, :, :], s4[:, g, :, :],
                                               mbias[:, bass.ds(b, 1), :].to_broadcast([P, 4, KP]), ALU.add)
                last.then_inc(sems["sa"], 1)
                w.wait("sa", w.at("sa", -1))
                w.link(w.eng.tensor_reduce(mx[:, :], E[:, par, :, :], AX.X, ALU.max), "dv")
                w.eng.tensor_tensor(E[:, par, :, :], E[:, par, :, :], mx[:, :].unsqueeze(2).to_broadcast([P, H, KP]),
                                    ALU.subtract).then_inc(sems["sb"], 1)
            else:
                w.inc("dv")
            w.inc("sa")
            w.inc("sb")

        def exponentials(w, par):
            if w.on("scalar"):
                w.wait("sb", w.at("sb"))
                w.eng.activation(E[:, par, :, :], E[:, par, :, :], ACT.Exp).then_inc(sems["ex"], 1)
            w.inc("ex")

        def sums(w, par):
            if w.on("vector"):
                w.wait("ex", w.at("ex"))
                w.link(w.eng.tensor_reduce(sm[:, :], E[:, par, :, :], AX.X, ALU.add), "dv")
                w.eng.reciprocal(inv[:, par, :], sm[:, :]).then_inc(sems["sm"], 1)
            else:
                w.inc("dv")
            w.inc("sm")
            if w.on("gpsimd"):
                w.wait("sm", w.at("sm"))
                w.eng.tensor_tensor(E[:, par, :, :], E[:, par, :, :], inv[:, par, :].unsqueeze(2).to_broadcast([P, H, KP]),
                                    ALU.mult).then_inc(sems["pn"], 1)
            w.inc("pn")

        def fetch_values(w, t):
            b = t // TB
            if w.on("scalar"):
                w.wait("pv", w.at("pv"))
                w.eng.activation(vs[:, :, :], vall[:, bass.ds(b, 1), :, :].rearrange("p b n c -> p (b n) c"), ACT.Copy)\
                    .then_inc(sems["pe"], 1)
            w.inc("pe")

        def turn_p(w, i, par, later=1):
            c0, c1 = 4 * i, min(4 * i + 4, NCH)
            e = E[:, par, :, :].rearrange("p h k -> p (h k)")
            if w.on("tensor"):
                if i == 0:
                    w.wait("pn", w.at("pn", later))
                w.wait("pe", w.at("pe", 1))
                for c in range(c0, c1):
                    last = w.eng.transpose(psP[:, i % 2, c - c0, :], e[:, c * P:(c + 1) * P], ident[:, :])
                if i == 2:
                    last.then_inc(sems["pt"], 1)
                else:
                    last.then_inc(sems["ph"], 1)
            if i == 2:
                w.inc("pt")
            else:
                w.inc("ph")
            if w.on("scalar"):
                w.wait("pt" if i == 2 else "ph", w.at("pt" if i == 2 else "ph"))
                w.eng.activation(pT[:, c0:c1, :], psP[:, i % 2, 0:c1 - c0, :], ACT.Copy).then_inc(sems["pe"], 1)
            w.inc("pe")

        def outputs(w, t):
            if w.on("tensor"):
                w.wait("pe", w.at("pe"))
                w.wait("var", w.at("var"))
                for hh in range(2):
                    for i in range(5):
                        last = w.eng.matmul(psO[:, 0, hh * P:(hh + 1) * P], vs[:, 5 * hh + i, :], pT[:, 5 * hh + i, :],
                                            start=i == 0, stop=i == 4)
                last.then_inc(sems["pv"], 1)
            w.inc("pv")
            if w.on("vector"):
                w.wait("pv", w.at("pv"))
                w.wait("o", w.at("o"))
                w.eng.tensor_copy(oT[:, :, :].rearrange("p a b -> p (a b)"), psO[:, 0, :]).then_inc(sems["pve"], 1)
            w.inc("pve")
            if w.on("gpsimd"):
                w.wait("var", w.at("var"))
                w.eng.tensor_tensor(xb[:, :], X[:, bass.ds(t, 1), :].rearrange("p a c -> p (a c)"), bo[:, :], ALU.add)\
                    .then_inc(sems["xb"], 1)
            w.inc("xb")

        def project(w, par):
            if w.on("tensor"):
                w.wait("pve", w.at("pve"))
                for hh in range(2):
                    last = w.eng.matmul(psO[:, 1, :], oT[:, hh, :], wo[:, hh, :], start=hh == 0, stop=hh == 1)
                last.then_inc(sems["o"], 1)
            w.inc("o")
            if w.on("vector"):
                w.wait("o", w.at("o"))
                w.wait("xb", w.at("xb"))
                w.link(w.eng.tensor_tensor(res[:, par, :], psO[:, 1, :], xb[:, :], ALU.add), "dv")
                w.link(w.eng.bn_stats(bst[:, par, :], res[:, par, :]), "dv")
                w.eng.memset(idle[:, :], 0.0)
                w.eng.bn_aggr(mv[:, par, :], bst[:, par, :]).then_inc(sems["var"], 1)
            else:
                w.inc("dv", 2)
            w.inc("var")
            if w.on("gpsimd"):
                w.wait("var", w.at("var"))
                w.link(w.eng.tensor_tensor(rstd[:, par, 0:1], mv[:, par, 1:2], eps[:, :], ALU.add), "pl")
                w.eng.tensor_tensor(rstd[:, par, 1:2], rstd[:, par, 0:1], mhalf[:, :], ALU.pow).then_inc(sems["rstd"], 1)
            else:
                w.inc("pl")
            w.inc("rstd")

        def normed(w, t, par):
            if w.on("vector"):
                w.wait("rstd", w.at("rstd"))
                w.eng.tensor_scalar(X[:, bass.ds(t, 1), :].rearrange("p a c -> p (a c)"), res[:, par, :],
                                    mv[:, par, 0:1], rstd[:, par, 1:2], ALU.subtract, ALU.mult).then_inc(sems["y"], 1)
            w.inc("y")

        def tile(w, t, par, left=3, first=False):
            if left >= 2:
                scores(w, t + 2)
            if left >= 3:
                copy_x(w, t + 3)
            if left >= 1:
                sums(w, 1 - par)
            fetch_values(w, t)
            turn_p(w, 0, par, 1 if left else 0)
            if not first:
                project(w, 1 - par)
            turn_p(w, 1, par)
            if left >= 3:
                turn_x(w)
            turn_p(w, 2, par)
            if left >= 2:
                less_max(w, t + 2, par)
            if not first:
                normed(w, t - 1, 1 - par)
            if left >= 3:
                queries(w)
            outputs(w, t)
            if left >= 2:
                exponentials(w, par)

        def walk(w):
            prepare(w, 0)
            w.loop(w.eng, B - 1, lambda i: prepare(w, i + 1))
            if w.role == "tensor":
                w.wait("dv", w.at("dv"))
                w.wait("kve", w.at("kve"))
            if w.role == "scalar":
                w.wait("vd", w.at("vd"))
            for t in range(3):
                copy_x(w, t)
                turn_x(w)
                queries(w)
                if t < 2:
                    scores(w, t)
                    less_max(w, t, t)
                    exponentials(w, t)
                if t == 0:
                    sums(w, 0)
            tile(w, 0, 0, first=True)
            tile(w, 1, 1)
            w.loop(w.eng, NT // 2 - 3, lambda i: (tile(w, 2 * i + 2, 0), tile(w, 2 * i + 3, 1)))
            for t in range(NT - 4, NT):
                tile(w, t, t % 2, left=min(3, NT - 1 - t))
            project(w, 1)
            normed(w, NT - 1, 1)

        @block.sync
        def _(eng):
            for t, src in ((wq, w_q), (wk, w_k), (wv, w_v), (wo, w_o)):
                eng.dma_start(t[:, :, :], src.rearrange("(a p) o -> p a o", p=P)).then_inc(sems["w"], 16)
            for t, src in ((bq, b_q), (bk, b_k)):
                eng.dma_start(t[:, :], src.rearrange("(a p) -> p a", p=P), allow_slow_non_contiguous=True).then_inc(sems["w"], 16)
            for t, src in ((bv, b_v), (bo, b_o)):
                eng.dma_start(t[:, :], src.partition_broadcast(P)).then_inc(sems["w"], 16)
            if mask is not None:
                eng.dma_start(mraw[:, :], mask.partition_broadcast(P)).then_inc(sems["w"], 16)

        @block.gpsimd
        def _(eng):
            make_identity(eng, ident, sems["cst"])
            eng.memset(hmask[:, :], 1.0).then_inc(sems["cst"], 1)
            eng.memset(mhalf[:, :], -0.5).then_inc(sems["cst"], 1)
            eng.memset(eps[:, :], EPS).then_inc(sems["cst"], 1)
            eng.wait_ge(sems["cst"], 5)
            eng.affine_select(out=hmask[:, :], in_=hmask[:, :], compare_op=ALU.is_ge, fill=0.0, base=0,
                              pattern=[[-HD, HALF]], channel_multiplier=1).then_inc(sems["cst"], 1)
            eng.wait_ge(sems["cst"], 6)
            eng.affine_select(out=hmask[:, :], in_=hmask[:, :], compare_op=ALU.is_ge, fill=0.0, base=HD - 1,
                              pattern=[[HD, HALF]], channel_multiplier=-1).then_inc(sems["cst"], 1)
            eng.memset(vmask[:, :, :], 1.0).then_inc(sems["cst"], 1)
            eng.wait_ge(sems["cst"], 8)
            eng.affine_select(out=vmask[:, :, :], in_=vmask[:, :, :], compare_op=ALU.is_ge, fill=0.0, base=0,
                              pattern=[[P, NCH // 2], [-KP, HALF]], channel_multiplier=1).then_inc(sems["cst"], 1)
            eng.wait_ge(sems["cst"], 9)
            eng.affine_select(out=vmask[:, :, :], in_=vmask[:, :, :], compare_op=ALU.is_ge, fill=0.0, base=KP - 1,
                              pattern=[[-P, NCH // 2], [KP, HALF]], channel_multiplier=-1).then_inc(sems["cst"], 1)
            eng.wait_ge(sems["w"], NW)
            eng.wait_ge(sems["cstv"], 2)
            walk(Writer(nc, eng, "gpsimd", sems, weights=NW))

        @block.vector
        def _(eng):
            eng.memset(cx[:, :], 0.0).then_inc(sems["cstv"], 1)
            eng.memset(mbias[:, :, :], FAR).then_inc(sems["cstv"], 1)
            eng.wait_ge(sems["cstv"], 2)
            eng.wait_ge(sems["w"], NW)
            if mask is not None:
                eng.tensor_scalar(mbias[:, :, 0:TK], mraw[:, :].bitcast(mybir.dt.uint8).rearrange("p (b k) -> p b k", k=TK), FAR, None, ALU.mult).then_inc(sems["cstv"], 1)
            else:
                eng.memset(mbias[:, :, 0:TK], 0.0).then_inc(sems["cstv"], 1)
            eng.tensor_scalar(bqs[:, :], bq[:, :], SCALE, None, ALU.mult).then_inc(sems["cstv"], 1)
            eng.wait_ge(sems["cstv"], 4)
            eng.wait_ge(sems["cst"], 10)
            walk(Writer(nc, eng, "vector", sems))

        @block.scalar
        def _(eng):
            eng.preload_act_table(ACT.Exp)
            eng.wait_ge(sems["cstv"], 4)
            walk(Writer(nc, eng, "scalar", sems, weights=NW))

        @block.tensor
        def _(eng):
            eng.wait_ge(sems["w"], NW)
            eng.wait_ge(sems["cst"], 7)
            walk(Writer(nc, eng, "tensor", sems))

GELU = ACT.Gelu


def turn_tokens(nc, tag, X, xT):
    NT = X.shape[1]
    with ExitStack() as ctx:
        m = Room(nc, ctx, tag)
        ident = m.sb("ident", [P, P])
        xs = m.sb("xs", [P, 2, D])
        psT = m.ps("psT", [P, 2, 2, 256])
        sems = {n: m.sem(n) for n in ("cst", "xs", "tr", "xt")}
        block = ctx.enter_context(nc.Block())

        def tile(w, t, par):
            if w.on("scalar"):
                w.wait("tr", w.at("tr", 1))
                w.eng.activation(xs[:, par, :], X[:, bass.ds(t, 1), :].rearrange("p a c -> p (a c)"), ACT.Copy)\
                    .then_inc(sems["xs"], 1)
            w.inc("xs")
            if w.on("tensor"):
                w.wait("xs", w.at("xs"))
                w.wait("xt", w.at("xt", 1))
                for cc in range(2):
                    last = w.eng.transpose(psT[:, par, cc, 0:P], xs[:, par, cc * P:(cc + 1) * P], ident[:, :])
                last.then_inc(sems["tr"], 1)
            w.inc("tr")
            if w.on("vector"):
                w.wait("tr", w.at("tr"))
                w.eng.tensor_copy(xT[:, :, bass.ds(t * P, P)], psT[:, par, :, 0:P]).then_inc(sems["xt"], 1)
            w.inc("xt")

        def walk(w):
            tile(w, 0, 0)
            tile(w, 1, 1)
            w.loop(w.eng, NT // 2 - 1, lambda i: (tile(w, 2 * i + 2, 0), tile(w, 2 * i + 3, 1)))

        @block.gpsimd
        def _(eng):
            make_identity(eng, ident, sems["cst"])

        @block.scalar
        def _(eng):
            walk(Writer(nc, eng, "scalar", sems))

        @block.vector
        def _(eng):
            walk(Writer(nc, eng, "vector", sems))

        @block.tensor
        def _(eng):
            eng.wait_ge(sems["cst"], 2)
            walk(Writer(nc, eng, "tensor", sems))


def expert_gates(nc, xT, w_red, wg, gates):
    NT = gates.shape[1]
    E, G = wg.shape
    TILES = 4
    with ExitStack() as ctx:
        m = Room(nc, ctx, "g")
        ident = m.sb("ident", [P, P])
        wr = m.sb("wr", [P, 2, G])
        wgt = m.sb("wgt", [E, G])
        sq = m.sb("sq", [E, G])
        nrm = m.sb("nrm", [E, 4])
        half = m.sb("half", [E, 1])
        wn = m.sb("wn", [E, G])
        wnT = m.sb("wnT", [G, E])
        xr = m.sb("xr", [G, 512])
        lg = m.sb("lg", [P, NT, E])
        mx = m.sb("mx", [P, NT])
        ex = m.sb("ex", [P, NT, E])
        sm = m.sb("sm", [P, NT])
        sc = m.sb("sc", [P, NT])
        first = m.sb("first", [P, E])
        hit = m.sb("hit", [P, NT, E])
        hm = m.sb("hm", [P, NT])
        psR = m.ps("psR", [P, 512])
        psL = m.ps("psL", [P, 512])
        sems = {n: m.sem(n) for n in ("cst", "w", "nv", "np", "nt", "nte", "r", "re", "l", "le", "dv", "ex")}
        block = ctx.enter_context(nc.Block())

        def group(w, g):
            if w.on("tensor"):
                w.wait("re", w.at("re"))
                for cc in range(2):
                    last = w.eng.matmul(psR[0:G, :], wr[:, cc, :], xT[:, cc, bass.ds(g * 512, 512)],
                                        start=cc == 0, stop=cc == 1)
                last.then_inc(sems["r"], 1)
            w.inc("r")
            if w.on("scalar"):
                w.wait("r", w.at("r"))
                w.wait("l", w.at("l"))
                w.eng.activation(xr[:, :], psR[0:G, :], ACT.Copy).then_inc(sems["re"], 1)
            w.inc("re")
            if w.on("tensor"):
                w.wait("re", w.at("re"))
                w.wait("le", w.at("le"))
                for i in range(TILES):
                    last = w.eng.matmul(psL[:, i * E:(i + 1) * E], xr[:, i * P:(i + 1) * P], wnT[:, :], start=True, stop=True)
                last.then_inc(sems["l"], 1)
            w.inc("l")
            if w.on("vector"):
                w.wait("l", w.at("l"))
                w.eng.tensor_copy(lg[:, bass.ds(g * TILES, TILES), :],
                                  psL[:, 0:TILES * E].rearrange("p (t e) -> p t e", e=E)).then_inc(sems["le"], 1)
            w.inc("le")

        def walk(w):
            group(w, 0)
            w.loop(w.eng, NT // TILES - 1, lambda i: group(w, i + 1))
            return w

        def spread(t):
            return t[:, :].unsqueeze(2).to_broadcast([P, NT, E])

        @block.sync
        def _(eng):
            eng.dma_start(wr[:, :, :], w_red.rearrange("(a p) g -> p a g", p=P)).then_inc(sems["w"], 16)
            eng.dma_start(wgt[:, :], wg).then_inc(sems["w"], 16)

        @block.gpsimd
        def _(eng):
            make_identity(eng, ident, sems["cst"])
            eng.memset(half[:, :], 0.5).then_inc(sems["cst"], 1)
            for e in range(E):
                eng.memset(first[:, e:e + 1], float(E - e)).then_inc(sems["cst"], 1)
            eng.wait_ge(sems["cst"], 3 + E)
            eng.wait_ge(sems["nv"], 2)
            eng.tensor_tensor(nrm[:, 1:2], nrm[:, 0:1], half[:, :], ALU.pow).then_inc(sems["np"], 1)

        @block.scalar
        def _(eng):
            eng.preload_act_table(ACT.Exp)
            eng.wait_ge(sems["nt"], 1)
            eng.activation(wnT[:, :], psL[0:G, 0:E], ACT.Copy).then_inc(sems["nte"], 1)
            walk(Writer(nc, eng, "scalar", sems))
            eng.wait_ge(sems["dv"], 2)
            eng.activation(ex[:, :, :], lg[:, :, :], ACT.Exp).then_inc(sems["ex"], 1)

        @block.tensor
        def _(eng):
            eng.wait_ge(sems["cst"], 2)
            eng.wait_ge(sems["nv"], 5)
            eng.transpose(psL[0:G, 0:E], wn[:, :], ident[0:E, 0:E]).then_inc(sems["nt"], 1)
            eng.wait_ge(sems["nte"], 1)
            walk(Writer(nc, eng, "tensor", sems))

        @block.vector
        def _(eng):
            eng.wait_ge(sems["w"], 32)
            w = Writer(nc, eng, "vector", sems)
            w.link(eng.tensor_tensor(sq[:, :], wgt[:, :], wgt[:, :], ALU.mult), "nv")
            w.link(eng.tensor_reduce(nrm[:, 0:1], sq[:, :], AX.X, ALU.add), "nv")
            eng.wait_ge(sems["np"], 1)
            w.link(eng.tensor_scalar(nrm[:, 2:3], nrm[:, 1:2], 1e-4, None, ALU.max), "nv")
            w.link(eng.reciprocal(nrm[:, 3:4], nrm[:, 2:3]), "nv")
            w.link(eng.tensor_scalar(wn[:, :], wgt[:, :], nrm[:, 3:4], None, ALU.mult), "nv")
            walk(w)
            eng.wait_ge(sems["le"], NT // TILES)
            w.link(eng.tensor_reduce(mx[:, :], lg[:, :, :], AX.X, ALU.max), "dv")
            eng.wait_ge(sems["cst"], 3 + E)
            w.link(eng.tensor_tensor(lg[:, :, :], lg[:, :, :], spread(mx), ALU.subtract), "dv")
            eng.wait_ge(sems["ex"], 1)
            w.link(eng.tensor_reduce(sm[:, :], ex[:, :, :], AX.X, ALU.add), "dv")
            w.link(eng.reciprocal(sc[:, :], sm[:, :]), "dv")
            w.link(eng.tensor_scalar(hit[:, :, :], lg[:, :, :], 0.0, None, ALU.is_equal), "dv")
            w.link(eng.tensor_tensor(hit[:, :, :], hit[:, :, :], first[:, :].unsqueeze(1).to_broadcast([P, NT, E]), ALU.mult), "dv")
            w.link(eng.tensor_reduce(hm[:, :], hit[:, :, :], AX.X, ALU.max), "dv")
            w.link(eng.tensor_tensor(hit[:, :, :], hit[:, :, :], spread(hm), ALU.is_equal), "dv")
            w.link(eng.tensor_tensor(gates[:, :, :], hit[:, :, :], spread(sc), ALU.mult), "dv")


def choose_tokens(nc, xT, w_r, b_r, scratch, keep, gates):
    NT = gates.shape[1]
    B = scratch.shape[0]
    S = scratch.shape[1]
    TB = NT // B
    with ExitStack() as ctx:
        m = Room(nc, ctx, "t")
        wr = m.sb("wr", [P, 2, 1])
        br = m.sb("br", [1, 1])
        row = m.sb("row", [1, B * S])
        col = m.sb("col", [P, NT])
        rows = m.sb("rows", [P, B, S])
        ge = m.sb("ge", [P, S])
        cnt = m.sb("cnt", [P, NT])
        psW = m.ps("psW", [P, 2, 512])
        sems = {n: m.sem(n) for n in ("w", "r", "re", "out", "back", "cnt")}
        block = ctx.enter_context(nc.Block())
        N = B * S // 512

        @block.sync
        def _(eng):
            eng.dma_start(wr[:, :, :], w_r.rearrange("(a p) g -> p a g", p=P), allow_slow_non_contiguous=True).then_inc(sems["w"], 16)
            eng.dma_start(br[:, :], b_r.rearrange("(a b) -> a b", a=1)).then_inc(sems["w"], 16)
            eng.wait_ge(sems["re"], N)
            eng.dma_start(scratch.rearrange("b s -> (b s)").unsqueeze(0), row[:, :]).then_inc(sems["out"], 16)
            eng.wait_ge(sems["out"], 16)
            eng.dma_start(rows[:, :, :], scratch.partition_broadcast(P)).then_inc(sems["back"], 16)
            eng.dma_start(col[:, :], scratch.rearrange("b (t p) -> p (b t)", p=P), allow_slow_non_contiguous=True)\
                .then_inc(sems["back"], 16)

        @block.tensor
        def _(eng):
            eng.wait_ge(sems["w"], 32)
            for n in range(N):
                if n >= 2:
                    eng.wait_ge(sems["re"], n - 1)
                for cc in range(2):
                    last = eng.matmul(psW[0:1, n % 2, :], wr[:, cc, :], xT[:, cc, n * 512:(n + 1) * 512],
                                      start=cc == 0, stop=cc == 1)
                last.then_inc(sems["r"], 1)

        @block.vector
        def _(eng):
            eng.wait_ge(sems["w"], 32)
            for n in range(N):
                eng.wait_ge(sems["r"], n + 1)
                eng.tensor_scalar(row[:, n * 512:(n + 1) * 512], psW[0:1, n % 2, :], br[:, :], None, ALU.add)\
                    .then_inc(sems["re"], 1)
            eng.wait_ge(sems["back"], 32)
            for t in range(NT):
                eng.tensor_scalar(ge[:, :], rows[:, t // TB, :], col[:, t:t + 1], None, ALU.is_ge, ALU.add,
                                  accum_out=cnt[:, t:t + 1]).then_inc(sems["cnt"], 1)
                eng.wait_ge(sems["cnt"], t + 1)
            eng.tensor_scalar(gates[:, :, :].rearrange("p t e -> p (t e)"), cnt[:, :], float(keep), None, ALU.is_lt)\
                .then_inc(sems["cnt"], 1)
            eng.wait_ge(sems["cnt"], NT + 1)


def chosen_mlp(nc, X, xT, chosen, W1, b1, W2, b2, out):
    _, H = W1.shape
    NT = X.shape[1]
    HC = H // P
    NG = NT // 4
    with ExitStack() as ctx:
        m = Room(nc, ctx, "f")
        w1 = m.sb("w1", [P, 2, H])
        w2 = m.sb("w2", [P, HC, D])
        b1s = m.sb("b1s", [P, HC])
        b2s = m.sb("b2s", [P, D])
        hT = m.sb("hT", [P, 2, HC, 512])
        tmp = m.sb("tmp", [P, 2, D])
        pick = m.sb("pick", [P, 2, D])
        f = m.sb("f", [P, NT])
        res = m.sb("res", [P, 2, D])
        bst = m.sb("bst", [P, 2, 6])
        mv = m.sb("mv", [P, 2, 2])
        rstd = m.sb("rstd", [P, 2, 2])
        mhalf = m.sb("mhalf", [P, 1])
        eps = m.sb("eps", [P, 1])
        idle = m.sb("idle", [1, 1])
        psH = m.ps("psH", [P, 4, 512])
        psO = m.ps("psO", [P, 4, 512])
        sems = {n: m.sem(n) for n in ("cst", "cstv", "w", "h", "he", "o", "oe", "dv", "var", "pl", "rstd", "y", "st")}
        block = ctx.enter_context(nc.Block())

        def up(w, g, par):
            for hc in range(HC):
                bank = hc % 4
                if w.on("tensor"):
                    w.wait("he", w.at("he", 3))
                    for cc in range(2):
                        last = w.eng.matmul(psH[:, bank, :], w1[:, cc, hc * P:(hc + 1) * P],
                                            xT[:, cc, bass.ds(g * 512, 512)], start=cc == 0, stop=cc == 1)
                    last.then_inc(sems["h"], 1)
                w.inc("h")
                if w.on("scalar"):
                    w.wait("h", w.at("h"))
                    w.wait("o", w.at("o"))
                    w.eng.activation(hT[:, par, hc, :], psH[:, bank, :], GELU, bias=b1s[:, hc:hc + 1]).then_inc(sems["he"], 1)
                w.inc("he")

        def normed(w, t, par, later=0):
            if w.on("vector"):
                w.wait("rstd", w.at("rstd", later))
                w.eng.tensor_scalar(X[:, bass.ds(t, 1), :].rearrange("p t c -> p (t c)"), res[:, par, :],
                                    mv[:, par, 0:1], rstd[:, par, 1:2], ALU.subtract, ALU.mult).then_inc(sems["y"], 1)
            w.inc("y")
            if w.on("sync"):
                row = w.fixed(t * P)
                tt = w.fixed(t)
                w.waits(("y", w.at("y")))
                w.eng.dma_start(out[bass.ds(row, P), :], X[:, bass.ds(tt, 1), :].rearrange("p t c -> p (t c)"))\
                    .then_inc(sems["st"], 16)
            w.inc("st", 16)

        def down(w, g, par, later, first=False):
            for i in range(4):
                t, b = g * 4 + i, i % 2
                if w.on("tensor"):
                    w.wait("he", w.at("he", later))
                    w.wait("oe", w.at("oe", 3))
                    for hc in range(HC):
                        last = w.eng.matmul(psO[:, i, 0:D], hT[:, par, hc, i * P:(i + 1) * P], w2[:, hc, :],
                                            start=hc == 0, stop=hc == HC - 1)
                    last.then_inc(sems["o"], 1)
                w.inc("o")
                if w.on("vector"):
                    w.wait("o", w.at("o"))
                    w.eng.tensor_tensor(tmp[:, b, :], psO[:, i, 0:D], b2s[:, :], ALU.add).then_inc(sems["oe"], 1)
                    w.wait("oe", w.at("oe", -1))
                    w.link(w.eng.tensor_scalar(pick[:, b, :], tmp[:, b, :], chosen[:, bass.ds(t, 1), :].rearrange("p t e -> p (t e)"),
                                               None, ALU.mult), "dv")
                    w.wait("y", w.at("y"))
                    w.link(w.eng.scalar_tensor_tensor(out=res[:, b, :], in0=X[:, bass.ds(t, 1), :].rearrange("p t c -> p (t c)"),
                                                      scalar=f[:, bass.ds(t, 1)], in1=pick[:, b, :],
                                                      op0=ALU.mult, op1=ALU.add), "dv")
                    w.link(w.eng.bn_stats(bst[:, b, :], res[:, b, :]), "dv")
                    w.eng.memset(idle[:, :], 0.0)
                    w.eng.bn_aggr(mv[:, b, :], bst[:, b, :]).then_inc(sems["var"], 1)
                else:
                    w.inc("dv", 3)
                w.inc("oe")
                w.inc("var")
                if w.on("gpsimd"):
                    w.wait("var", w.at("var"))
                    w.link(w.eng.tensor_tensor(rstd[:, b, 0:1], mv[:, b, 1:2], eps[:, :], ALU.add), "pl")
                    w.eng.tensor_tensor(rstd[:, b, 1:2], rstd[:, b, 0:1], mhalf[:, :], ALU.pow).then_inc(sems["rstd"], 1)
                else:
                    w.inc("pl")
                w.inc("rstd")
                if not (first and i == 0):
                    normed(w, t - 1, 1 - b, 1)

        def walk(w):
            up(w, 0, 0)
            up(w, 1, 1)
            down(w, 0, 0, HC, first=True)

            def two(i):
                up(w, 2 * i + 2, 0)
                down(w, 2 * i + 1, 1, HC)
                up(w, 2 * i + 3, 1)
                down(w, 2 * i + 2, 0, HC)
            w.loop(w.eng, NG // 2 - 1, two)
            down(w, NG - 1, 1, 0)
            normed(w, NT - 1, 1)
            return w

        @block.sync
        def _(eng):
            eng.dma_start(w1[:, :, :], W1.rearrange("(a p) h -> p a h", p=P)).then_inc(sems["w"], 16)
            eng.dma_start(w2[:, :, :], W2.rearrange("(a p) c -> p a c", p=P)).then_inc(sems["w"], 16)
            eng.dma_start(b1s[:, :], b1.rearrange("(a p) -> p a", p=P), allow_slow_non_contiguous=True).then_inc(sems["w"], 16)
            eng.dma_start(b2s[:, :], b2.partition_broadcast(P)).then_inc(sems["w"], 16)
            w = walk(Writer(nc, eng, "sync", sems, weights=64))
            w.wait("st", w.at("st"))

        @block.gpsimd
        def _(eng):
            eng.memset(mhalf[:, :], -0.5).then_inc(sems["cst"], 1)
            eng.memset(eps[:, :], EPS).then_inc(sems["cst"], 1)
            eng.wait_ge(sems["cst"], 2)
            walk(Writer(nc, eng, "gpsimd", sems))

        @block.vector
        def _(eng):
            eng.tensor_scalar(f[:, :], chosen[:, :, 0], -1.0, 2.0, ALU.mult, ALU.add).then_inc(sems["cstv"], 1)
            eng.wait_ge(sems["cstv"], 1)
            eng.wait_ge(sems["w"], 64)
            walk(Writer(nc, eng, "vector", sems))

        @block.scalar
        def _(eng):
            eng.preload_act_table(GELU)
            eng.wait_ge(sems["w"], 64)
            walk(Writer(nc, eng, "scalar", sems))

        @block.tensor
        def _(eng):
            eng.wait_ge(sems["w"], 64)
            walk(Writer(nc, eng, "tensor", sems))


def layer1_self_attention(nc, X, xT, w_qkv, b_qkv, w_out, b_out, B):
    NT = X.shape[1]
    TB = NT // B
    S = TB * P
    HD = w_out.shape[0]
    KC = S // P
    SCALE = HD ** -0.5
    RING = 4
    NW = 16 * 12
    with ExitStack() as ctx:
        m = Room(nc, ctx, "s")
        wq = m.sb("wq", [P, 2, 2 * HD])
        wk = m.sb("wk", [P, 2, 2 * HD])
        wv = m.sb("wv", [P, 2, HD])
        wo = m.sb("wo", [HD, D])
        bq = m.sb("bq", [P, 1])
        bk = m.sb("bk", [P, 1])
        bv = m.sb("bv", [P, HD])
        bo = m.sb("bo", [P, D])
        ident = m.sb("ident", [P, P])
        rowmask = m.sb("rowmask", [16, KC, P])
        xb = m.sb("xb", [P, 2, S])
        qA = m.sb("qA", [P, S], F32R)
        qB = m.sb("qB", [P, S], F32R)
        kA = m.sb("kA", [P, S], F32R)
        kB = m.sb("kB", [P, S], F32R)
        vd = m.sb("vd", [P, KC, 2 * HD])
        pr = m.sb("pr", [P, RING, 512])
        mxs = m.sb("mxs", [P, KC, 2])
        mall = m.sb("mall", [P, KC])
        m16 = m.sb("m16", [P, 2 * KC], F32R)
        oU = m.sb("oU", [P, 2, 512])
        turned = m.sb("turned", [HD, S])
        inv = m.sb("inv", [HD, S // 32])
        rec = m.sb("rec", [HD, S])
        oT = m.sb("oT", [HD, S])
        xo = m.sb("xo", [P, 2, D])
        res = m.sb("res", [P, 2, D])
        bst = m.sb("bst", [P, 2, 6])
        mv = m.sb("mv", [P, 2, 2])
        rstd = m.sb("rstd", [P, 2, 2])
        mhalf = m.sb("mhalf", [P, 1])
        eps = m.sb("eps", [P, 1])
        idle = m.sb("idle", [1, 1])
        psS = m.ps("psS", [P, RING, 512])
        psO = m.ps("psO", [P, 2, 512])
        psX = m.ps("psX", [P, 2, 512])
        names = ("cst", "cstv", "w", "xb", "ch", "px", "pxr", "m16", "s", "e", "pv", "nm", "ot", "xo", "var", "pl",
                 "rstd", "y", "dv")
        sems = {n: m.sem(n) for n in names}
        block = ctx.enter_context(nc.Block())

        def bank(w):
            return w.count.get("px", 0) % 2

        def fetch(w, b):
            if w.on("gpsimd"):
                w.wait("px", w.at("px"))
                w.eng.tensor_copy(xb[:, :, :], xT[:, :, bass.ds(b * S, S)]).then_inc(sems["xb"], 1)
            w.inc("xb")

        def project(w, wt, bias, hi, hi2, lo, lo_from, n):
            k = bank(w)
            cols = slice(n * 512, (n + 1) * 512)
            if w.on("tensor"):
                w.wait("xb", w.at("xb"))
                w.wait("pxr", w.at("pxr", 1))
                for cc in range(2):
                    last = w.eng.matmul(psX[:, k, :], wt[:, cc, :], xb[:, cc, cols], start=cc == 0, stop=cc == 1)
                last.then_inc(sems["px"], 1)
            w.inc("px")
            if w.on("scalar"):
                w.wait("px", w.at("px"))
                w.wait("s", w.at("s"))
                w.eng.activation(hi[:, cols], psX[:, k, :], ACT.Identity, bias=bias[:, :]).then_inc(sems["ch"], 1)
                if hi2 is not None:
                    w.eng.activation(hi2[0:HD, cols], psX[0:HD, k, :], ACT.Identity, bias=bias[0:HD, :]).then_inc(sems["ch"], 1)
            w.inc("ch", 1 if hi2 is None else 2)
            if w.on("vector"):
                r = slice(lo_from, lo_from + HD)
                w.wait("ch", w.at("ch"))
                w.wait("px", w.at("px"))
                w.eng.scalar_tensor_tensor(out=lo[r, cols], in0=psX[r, k, :], scalar=bias[r, :],
                                           in1=hi[r, cols].bitcast(F32), op0=ALU.add, op1=ALU.subtract)\
                    .then_inc(sems["pxr"], 1)
            w.inc("pxr")

        def values_in(w):
            k = bank(w)
            if w.on("tensor"):
                w.wait("pxr", w.at("pxr", 1))
                for t in range(KC):
                    for cc in range(2):
                        last = w.eng.matmul(psX[:, k, t * HD:(t + 1) * HD], xb[:, cc, t * P:(t + 1) * P], wv[:, cc, :],
                                            start=cc == 0, stop=cc == 1)
                last.then_inc(sems["px"], 1)
            w.inc("px")
            if w.on("vector"):
                w.wait("px", w.at("px"))
                w.wait("pv", w.at("pv"))
                w.eng.tensor_tensor(vd[:, :, 0:HD], psX[:, k, :].rearrange("p (t d) -> p t d", d=HD),
                                    bv[:, :].unsqueeze(1).to_broadcast([P, KC, HD]), ALU.add).then_inc(sems["pxr"], 1)
            w.inc("pxr")

        def max_tile(w, u):
            k = bank(w)
            if w.on("tensor"):
                w.wait("pxr", w.at("pxr", 1 if u else 0))
                w.eng.matmul(psX[:, k, :], qA[:, (u // 2) * P:(u // 2 + 1) * P], kA[:, (u % 2) * 512:(u % 2 + 1) * 512],
                             start=True, stop=True).then_inc(sems["px"], 1)
            w.inc("px")
            if w.on("vector"):
                w.wait("px", w.at("px"))
                w.eng.tensor_reduce(mxs[:, u // 2, u % 2:u % 2 + 1], psX[:, k, :], AX.X, ALU.max).then_inc(sems["pxr"], 1)
            w.inc("pxr")

        def max_rows(w):
            if w.on("vector"):
                w.wait("pxr", w.at("pxr"))
                w.link(w.eng.tensor_reduce(mall[:, :], mxs[:, :, :], AX.X, ALU.max), "dv")
                w.link(w.eng.tensor_scalar(m16[:, 0:KC], mall[:, :], -1.0, None, ALU.mult), "dv")
                w.eng.scalar_tensor_tensor(out=m16[:, KC:2 * KC], in0=mall[:, :], scalar=-1.0,
                                           in1=m16[:, 0:KC].bitcast(F32), op0=ALU.mult, op1=ALU.subtract)\
                    .then_inc(sems["m16"], 1)
            else:
                w.inc("dv", 2)
            w.inc("m16")
            k = bank(w)
            if w.on("tensor"):
                w.wait("m16", w.at("m16"))
                w.wait("pxr", w.at("pxr", 1))
                w.eng.transpose(psX[0:16, k, 0:P], m16[:, :].bitcast(F32), ident[:, :]).then_inc(sems["px"], 1)
            w.inc("px")
            if w.on("vector"):
                w.wait("px", w.at("px"))
                w.eng.tensor_tensor(qB[HD:HD + 16, :].rearrange("p (b t) -> p b t", t=P),
                                    psX[0:16, k, 0:P].unsqueeze(1).to_broadcast([16, KC, P]),
                                    rowmask[:, :, :], ALU.mult).then_inc(sems["pxr"], 1)
            w.inc("pxr")

        def scores(w, kc):
            n = w.count.get("e", 0) % RING
            if w.on("tensor"):
                if kc == 0:
                    w.wait("pxr", w.at("pxr"))
                w.wait("e", w.at("e", RING - 2))
                for a, q in ((0, 0), (0, 1), (1, 0), (1, 1)):
                    kt, qt = (kB, qB) if a else (kA, qA)
                    last = w.eng.matmul(psS[:, n + q, :], kt[:, kc * P:(kc + 1) * P], qt[:, q * 512:(q + 1) * 512],
                                        start=a == 0, stop=a == 1)
                    if a:
                        last.then_inc(sems["s"], 1)
            for q in range(2):
                w.inc("s")
                if w.on("scalar"):
                    w.wait("s", w.at("s"))
                    w.wait("pv", w.at("e", RING - 1))
                    w.eng.activation(pr[:, n + q, :], psS[:, n + q, :], ACT.Exp, scale=SCALE).then_inc(sems["e"], 1)
                w.inc("e")

        def values(w, kc):
            for q in range(2):
                n = w.count.get("pv", 0) % RING
                if w.on("tensor"):
                    w.wait("nm", w.at("nm"))
                    w.wait("e", w.at("pv", -1))
                    w.eng.matmul(psO[:, q, :], vd[:, kc, :], pr[:, n, :],
                                 start=kc == 0, stop=kc == KC - 1).then_inc(sems["pv"], 1)
                w.inc("pv")

        def divide(w):
            if w.on("scalar"):
                w.wait("pv", w.at("pv"))
                w.wait("ot", w.at("ot"))
                w.eng.activation(oU[:, :, :], psO[:, :, :], ACT.Copy).then_inc(sems["nm"], 1)
            w.inc("nm")
            if w.on("vector"):
                w.wait("nm", w.at("nm"))
                w.link(w.eng.transpose(turned[:, :], oU[HD:P, :, :].rearrange("p a b -> p (a b)")), "dv")
                w.link(w.eng.reciprocal(inv[:, :], turned[:, 0:S:32]), "dv")
                w.link(w.eng.transpose(rec[:, :], inv[:, :].unsqueeze(2).to_broadcast([HD, 32, 32])), "dv")
                w.wait("px", w.at("px"))
                w.eng.tensor_tensor(oT[:, :], oU[0:HD, :, :].rearrange("p a b -> p (a b)"), rec[:, :], ALU.mult)\
                    .then_inc(sems["ot"], 1)
            else:
                w.inc("dv", 3)
            w.inc("ot")

        def output(w, b, i):
            par = i % 2
            t = b * TB + i
            if w.on("gpsimd"):
                w.wait("var", w.at("var", 1))
                w.eng.tensor_tensor(xo[:, par, :], X[:, bass.ds(t, 1), :].rearrange("p a c -> p (a c)"), bo[:, :], ALU.add)\
                    .then_inc(sems["xo"], 1)
            w.inc("xo")
            k = bank(w)
            if w.on("tensor"):
                w.wait("ot", w.at("ot"))
                w.wait("pxr", w.at("pxr", 1))
                w.eng.matmul(psX[:, k, 0:D], oT[:, i * P:(i + 1) * P], wo[:, :], start=True, stop=True).then_inc(sems["px"], 1)
            w.inc("px")
            if w.on("vector"):
                w.wait("px", w.at("px"))
                w.wait("xo", w.at("xo"))
                w.wait("y", w.at("y"))
                w.eng.tensor_tensor(res[:, par, :], psX[:, k, 0:D], xo[:, par, :], ALU.add).then_inc(sems["pxr"], 1)
                w.wait("pxr", w.at("pxr", -1))
                w.link(w.eng.bn_stats(bst[:, par, :], res[:, par, :]), "dv")
                w.eng.memset(idle[:, :], 0.0)
                w.eng.bn_aggr(mv[:, par, :], bst[:, par, :]).then_inc(sems["var"], 1)
            else:
                w.inc("dv")
            w.inc("pxr")
            w.inc("var")
            if w.on("gpsimd"):
                w.wait("var", w.at("var"))
                w.link(w.eng.tensor_tensor(rstd[:, par, 0:1], mv[:, par, 1:2], eps[:, :], ALU.add), "pl")
                w.eng.tensor_tensor(rstd[:, par, 1:2], rstd[:, par, 0:1], mhalf[:, :], ALU.pow).then_inc(sems["rstd"], 1)
            else:
                w.inc("pl")
            w.inc("rstd")

        def normed(w, b, i, later):
            if w.on("vector"):
                par = i % 2
                w.wait("rstd", w.at("rstd", later))
                w.eng.tensor_scalar(X[:, bass.ds(b * TB + i, 1), :].rearrange("p a c -> p (a c)"), res[:, par, :],
                                    mv[:, par, 0:1], rstd[:, par, 1:2], ALU.subtract, ALU.mult).then_inc(sems["y"], 1)
            w.inc("y")

        def batch(w, b, first=False):
            for n in range(2):
                project(w, wq, bq, qA, None, qB, 0, n)
                project(w, wk, bk, kA, kB, kA, HD, n)
            values_in(w)
            fetch(w, (b + 1) % B)
            for u in range(2 * KC):
                max_tile(w, u)
            max_rows(w)
            scores(w, 0)
            for kc in range(KC):
                if kc < KC - 1:
                    scores(w, kc + 1)
                if not first:
                    output(w, b - 1, kc)
                    if kc:
                        normed(w, b - 1, kc - 1, 1)
                values(w, kc)
            if not first:
                normed(w, b - 1, TB - 1, 0)
            divide(w)

        def walk(w):
            fetch(w, 0)
            batch(w, 0, first=True)
            batch(w, 1)
            w.loop(w.eng, B - 2, lambda i: batch(w, i + 2))
            for i in range(TB):
                output(w, B - 1, i)
                if i:
                    normed(w, B - 1, i - 1, 1)
            normed(w, B - 1, TB - 1, 0)

        @block.sync
        def _(eng):
            src = w_qkv.rearrange("(a p) o -> p a o", p=P)
            for t, c in ((wq, 0), (wk, HD)):
                for k in range(2):
                    eng.dma_start(t[:, :, k * HD:(k + 1) * HD], src[:, :, c:c + HD]).then_inc(sems["w"], 16)
            eng.dma_start(wv[:, :, :], src[:, :, 2 * HD:3 * HD]).then_inc(sems["w"], 16)
            eng.dma_start(wo[:, :], w_out).then_inc(sems["w"], 16)
            bcol = b_qkv.rearrange("(p a) -> p a", a=1)
            for t, c in ((bq, 0), (bk, HD)):
                for k in range(2):
                    eng.dma_start(t[k * HD:(k + 1) * HD, :], bcol[c:c + HD, :], allow_slow_non_contiguous=True).then_inc(sems["w"], 16)
            eng.dma_start(bv[:, :], b_qkv[2 * HD:3 * HD].partition_broadcast(P)).then_inc(sems["w"], 16)
            eng.dma_start(bo[:, :], b_out.partition_broadcast(P)).then_inc(sems["w"], 16)

        @block.gpsimd
        def _(eng):
            make_identity(eng, ident, sems["cst"])
            eng.memset(rowmask[:, :, :], 0.0).then_inc(sems["cst"], 1)
            eng.wait_ge(sems["cst"], 3)
            for off in (0, KC):
                eng.affine_select(out=rowmask[:, :, :], in_=rowmask[:, :, :], compare_op=ALU.not_equal, fill=1.0,
                                  base=-off, pattern=[[-1, KC], [0, P]], channel_multiplier=1).then_inc(sems["cst"], 1)
                eng.wait_ge(sems["cst"], 4 if off == 0 else 5)
            eng.memset(mhalf[:, :], -0.5).then_inc(sems["cst"], 1)
            eng.memset(eps[:, :], EPS).then_inc(sems["cst"], 1)
            eng.wait_ge(sems["cst"], 7)
            eng.wait_ge(sems["w"], NW)
            walk(Writer(nc, eng, "gpsimd", sems))

        @block.vector
        def _(eng):
            eng.memset(vd[:, :, HD:2 * HD], 1.0).then_inc(sems["cstv"], 1)
            eng.memset(qB[HD:P, :].bitcast(F32), 0.0).then_inc(sems["cstv"], 1)
            eng.memset(kB[HD:P, :].bitcast(F32), 0.0).then_inc(sems["cstv"], 1)
            eng.wait_ge(sems["cstv"], 3)
            eng.memset(kB[HD:HD + 16, :].bitcast(F32), 1.0).then_inc(sems["cstv"], 1)
            eng.wait_ge(sems["cst"], 5)
            eng.wait_ge(sems["w"], NW)
            walk(Writer(nc, eng, "vector", sems))

        @block.scalar
        def _(eng):
            eng.preload_act_table(ACT.Exp)
            eng.wait_ge(sems["w"], NW)
            walk(Writer(nc, eng, "scalar", sems))

        @block.tensor
        def _(eng):
            eng.wait_ge(sems["w"], NW)
            eng.wait_ge(sems["cst"], 5)
            eng.wait_ge(sems["cstv"], 4)
            walk(Writer(nc, eng, "tensor", sems))

I32 = mybir.dt.int32


def route_tokens(nc, gates, score, pos, rows):
    NT, E = gates.shape[1], gates.shape[2]
    NJ = rows.shape[1]
    with ExitStack() as ctx:
        m = Room(nc, ctx, "r")
        tri = m.sb("tri", [P, P])
        ones = m.sb("ones", [P, P])
        ints = m.sb("ints", [P, NJ + NT + 1], I32)
        nums = m.sb("nums", [P, NJ + NT + 1])
        hit = m.sb("hit", [P, NT, E])
        tot = m.sb("tot", [P, NT, E])
        scan = m.sb("scan", [P, 2, NT, E])
        at = m.sb("at", [P, NT, E])
        over = m.sb("over", [P, E, NT])
        tiles = m.sb("tiles", [P, E])
        ends = m.sb("ends", [P, E])
        base = m.sb("base", [P, E])
        posf = m.sb("posf", [P, NT])
        past = m.sb("past", [P, NJ, E])
        rowf = m.sb("rowf", [P, NJ, 2])
        ps = m.ps("ps", [P, 2, NT * E])
        sems = {n: m.sem(n) for n in ("cst", "hit", "mm", "dv")}
        block = ctx.enter_context(nc.Block())

        @block.gpsimd
        def _(eng):
            eng.memset(ones[:, :], 1.0).then_inc(sems["cst"], 1)
            eng.memset(tri[:, :], 1.0).then_inc(sems["cst"], 1)
            eng.iota(ints[:, 0:NJ], [[1, NJ]], base=0, channel_multiplier=0).then_inc(sems["cst"], 1)
            eng.iota(ints[:, NJ:NJ + NT], [[P, NT]], base=0, channel_multiplier=0).then_inc(sems["cst"], 1)
            eng.iota(ints[:, NJ + NT:], [[0, 1]], base=0, channel_multiplier=1).then_inc(sems["cst"], 1)
            eng.wait_ge(sems["cst"], 5)
            eng.affine_select(out=tri[:, :], in_=tri[:, :], compare_op=ALU.is_ge, fill=0.0, base=-1,
                              pattern=[[1, P]], channel_multiplier=-1).then_inc(sems["cst"], 1)

        @block.tensor
        def _(eng):
            eng.wait_ge(sems["cst"], 6)
            eng.wait_ge(sems["hit"], 1)
            h = hit[:, :, :].rearrange("p t e -> p (t e)")
            eng.matmul(ps[:, 0, :], tri[:, :], h, start=True, stop=True)
            eng.matmul(ps[:, 1, :], ones[:, :], h, start=True, stop=True).then_inc(sems["mm"], 1)

        @block.vector
        def _(eng):
            w = Writer(nc, eng, "vector", sems)
            eng.tensor_scalar(hit[:, :, :], gates[:, :, :], 0.0, None, ALU.is_gt).then_inc(sems["hit"], 1)
            w.link(eng.tensor_reduce(score[:, :], gates[:, :, :], AX.X, ALU.max), "dv")
            eng.wait_ge(sems["cst"], 6)
            w.link(eng.tensor_copy(nums[:, :], ints[:, :]), "dv")
            eng.wait_ge(sems["mm"], 1)
            w.link(eng.tensor_copy(tot[:, :, :].rearrange("p t e -> p (t e)"), ps[:, 1, :]), "dv")
            w.link(eng.tensor_copy(scan[:, 0, :, :], tot[:, :, :]), "dv")
            k, reach = 0, 1
            while reach < NT:
                w.link(eng.tensor_copy(scan[:, 1 - k, 0:reach, :], scan[:, k, 0:reach, :]), "dv")
                w.link(eng.tensor_tensor(scan[:, 1 - k, reach:, :], scan[:, k, reach:, :], scan[:, k, 0:NT - reach, :], ALU.add), "dv")
                k, reach = 1 - k, 2 * reach
            w.link(eng.tensor_tensor(over[:, :, :], scan[:, k, NT - 1, :].unsqueeze(2).to_broadcast([P, E, NT]),
                                     nums[:, NJ:NJ + NT].unsqueeze(1).to_broadcast([P, E, NT]), ALU.is_gt), "dv")
            w.link(eng.tensor_reduce(tiles[:, :], over[:, :, :], AX.X, ALU.add), "dv")
            w.link(eng.tensor_copy(ends[:, 0:1], tiles[:, 0:1]), "dv")
            for e in range(1, E):
                w.link(eng.tensor_tensor(ends[:, e:e + 1], ends[:, e - 1:e], tiles[:, e:e + 1], ALU.add), "dv")
            w.link(eng.tensor_tensor(base[:, :], ends[:, :], tiles[:, :], ALU.subtract), "dv")
            w.link(eng.tensor_scalar(base[:, :], base[:, :], float(P), None, ALU.mult), "dv")
            w.link(eng.tensor_tensor(at[:, :, :], scan[:, k, :, :], tot[:, :, :], ALU.subtract), "dv")
            w.link(eng.tensor_tensor(at[:, :, :].rearrange("p t e -> p (t e)"), at[:, :, :].rearrange("p t e -> p (t e)"),
                                     ps[:, 0, :], ALU.add), "dv")
            w.link(eng.tensor_tensor(at[:, :, :], at[:, :, :], base[:, :].unsqueeze(1).to_broadcast([P, NT, E]), ALU.add), "dv")
            w.link(eng.tensor_tensor(at[:, :, :], at[:, :, :], hit[:, :, :], ALU.mult), "dv")
            w.link(eng.tensor_reduce(posf[:, :], at[:, :, :], AX.X, ALU.add), "dv")
            w.link(eng.tensor_copy(pos[:, :], posf[:, :]), "dv")
            w.link(eng.tensor_tensor(past[:, :, :], ends[:, :].unsqueeze(1).to_broadcast([P, NJ, E]),
                                     nums[:, 0:NJ].unsqueeze(2).to_broadcast([P, NJ, E]), ALU.is_le), "dv")
            w.link(eng.tensor_reduce(rowf[:, :, 1], past[:, :, :], AX.X, ALU.add), "dv")
            w.link(eng.tensor_scalar(rowf[:, :, 1], rowf[:, :, 1], float(E - 1), None, ALU.min), "dv")
            w.link(eng.tensor_scalar(rowf[:, :, 0], rowf[:, :, 1], float(P), nums[:, NJ + NT:], ALU.mult, ALU.add), "dv")
            w.link(eng.tensor_copy(rows[:, :, :], rowf[:, :, :]), "dv")


def sort_tokens(nc, X, pos, xs):
    NT = X.shape[1]
    NJ = xs.shape[0] // P
    FILLS = 4
    with ExitStack() as ctx:
        m = Room(nc, ctx, "o")
        zero = m.sb("zero", [P, NJ // FILLS, D])
        xb = m.sb("xb", [P, 2, D])
        at = m.sb("at", [P, 2], I32)
        idle = m.sb("idle", [1, 1])
        one = m.sb("one", [1, 1])
        sems = {n: m.sem(n) for n in ("z", "one", "fill", "xb", "cp", "id", "sc0", "sc1")}
        block = ctx.enter_context(nc.Block())

        def tile(w, t, par):
            if w.on("scalar"):
                w.wait(f"sc{par}", w.at(f"sc{par}"))
                w.eng.activation(xb[:, par, :], X[:, bass.ds(t, 1), :].rearrange("p a c -> p (a c)"), ACT.Copy)\
                    .then_inc(sems["xb"], 1)
            w.inc("xb")
            if w.on("gpsimd"):
                w.wait(f"sc{par}", w.at(f"sc{par}"))
                w.wait("xb", w.at("xb"))
                w.eng.tensor_copy(at[:, par:par + 1], pos[:, bass.ds(t, 1)]).then_inc(sems["cp"], 1)
                w.wait("cp", w.at("cp", -1))
                w.wait("id", w.at("id"))
                w.eng.tensor_tensor(idle[:, :], one[:, :], one[:, :], ALU.add).then_inc(sems["id"], 1)
                w.eng.indirect_dma_start(xs, bass.IndirectOffsetOnAxis(ap=at[:, par:par + 1], axis=0), xb[:, par, :], None)\
                    .then_inc(sems[f"sc{par}"], 16)
            w.inc("cp")
            w.inc("id")
            w.inc(f"sc{par}", 16)

        def walk(w):
            tile(w, 0, 0)
            tile(w, 1, 1)
            w.loop(w.eng, NT // 2 - 1, lambda i: (tile(w, 2 * i + 2, 0), tile(w, 2 * i + 3, 1)))

        @block.scalar
        def _(eng):
            walk(Writer(nc, eng, "scalar", sems))

        @block.vector
        def _(eng):
            eng.memset(zero[:, :, :], 0.0).then_inc(sems["z"], 1)

        @block.sync
        def _(eng):
            eng.wait_ge(sems["z"], 1)
            dst = xs.rearrange("(j p) c -> p j c", p=P)
            n = NJ // FILLS
            for i in range(FILLS):
                eng.dma_start(dst[:, i * n:(i + 1) * n, :], zero[:, :, :]).then_inc(sems["fill"], 16)

        @block.gpsimd
        def _(eng):
            eng.memset(one[:, :], 1.0).then_inc(sems["one"], 1)
            eng.wait_ge(sems["one"], 1)
            eng.wait_ge(sems["fill"], 16 * FILLS)
            w = Writer(nc, eng, "gpsimd", sems)
            walk(w)
            for n in ("sc0", "sc1"):
                w.wait(n, w.at(n))


def expert_mlps(nc, xs, rows, W1, b1, W2, b2, os):
    E, _, H = W1.shape
    NJ = rows.shape[1]
    HC = H // P
    SLOTS = 4
    w1r = W1.rearrange("e (p a) h -> (e p) (a h)", a=2)
    w2r = W2.rearrange("e (p a) c -> (e p) (a c)", a=HC)
    b1r = b1.rearrange("e (p a) -> (e p) a", a=HC)
    with ExitStack() as ctx:
        m = Room(nc, ctx, "e")
        ident = m.sb("ident", [P, P])
        w1 = m.sb("w1", [P, SLOTS, 2, H])
        w2 = m.sb("w2", [P, SLOTS, HC, D])
        b1t = m.sb("b1t", [P, SLOTS, HC])
        b2t = m.sb("b2t", [P, SLOTS, D])
        at = m.sb("at", [P, SLOTS, 2], I32)
        xg = m.sb("xg", [P, 2, D])
        xT = m.sb("xT", [P, 2, 2, P])
        hT = m.sb("hT", [P, 2, HC, P])
        ob = m.sb("ob", [P, 2, D])
        idle = m.sb("idle", [1, 1])
        one = m.sb("one", [1, 1])
        psT = m.ps("psT", [P, 2, 512])
        psH = m.ps("psH", [P, 2, HC, P])
        psO = m.ps("psO", [P, 2, 512])
        sems = {n: m.sem(n) for n in ("cst", "w", "x0", "x1", "w0", "w1", "w2", "w3", "cp", "id", "tr", "xt", "h", "he", "o", "od", "st0", "st1")}
        block = ctx.enter_context(nc.Block())

        def load(w, j, par):
            if w.on("sync"):
                row = w.fixed(j * P)
                w.waits(("tr", w.at("tr")))
                w.eng.dma_start(xg[:, par, :], xs[bass.ds(row, P), :]).then_inc(sems[f"x{par}"], 16)
            w.inc(f"x{par}", 16)

        def fetch(w, j, slot):
            if w.on("gpsimd"):
                w.wait("o", w.at("o"))
                w.wait("od", w.at("od"))
                w.eng.tensor_copy(at[:, slot, :], rows[:, bass.ds(j, 1), :].rearrange("p a b -> p (a b)")).then_inc(sems["cp"], 1)
                w.wait("cp", w.at("cp", -1))
                w.wait("id", w.at("id"))
                w.eng.tensor_tensor(idle[:, :], one[:, :], one[:, :], ALU.add).then_inc(sems["id"], 1)
                for t, src, k in ((w1[:, slot, :, :].rearrange("p a h -> p (a h)"), w1r, 0),
                                  (b1t[:, slot, :], b1r, 0),
                                  (w2[:, slot, :, :].rearrange("p a c -> p (a c)"), w2r, 0),
                                  (b2t[:, slot, :], b2, 1)):
                    w.eng.indirect_dma_start(t, None, src, bass.IndirectOffsetOnAxis(ap=at[:, slot, k:k + 1], axis=0))\
                        .then_inc(sems[f"w{slot}"], 16)
            w.inc("cp")
            w.inc("id")
            w.inc(f"w{slot}", 64)

        def turn(w, par):
            if w.on("tensor"):
                w.wait(f"x{par}", w.at(f"x{par}"))
                w.wait("xt", w.at("xt", 1))
                for a in range(2):
                    last = w.eng.transpose(psT[:, par, a * P:(a + 1) * P], xg[:, par, a:D:2], ident[:, :])
                last.then_inc(sems["tr"], 1)
            w.inc("tr")
            if w.on("vector"):
                w.wait("tr", w.at("tr"))
                w.wait("h", w.at("h", 1))
                w.eng.tensor_copy(xT[:, par, :, :].rearrange("p a t -> p (a t)"), psT[:, par, 0:2 * P]).then_inc(sems["xt"], 1)
            w.inc("xt")

        def up(w, slot, ahead=0):
            par = slot % 2
            if w.on("tensor"):
                w.wait(f"w{slot}", w.at(f"w{slot}"))
                w.wait("xt", w.at("xt", ahead))
                w.wait("he", w.at("he", 1))
                for a in range(HC):
                    for c in range(2):
                        last = w.eng.matmul(psH[:, par, a, :], w1[:, slot, c, a:H:HC], xT[:, par, c, :], start=c == 0, stop=c == 1)
                last.then_inc(sems["h"], 1)
            w.inc("h")
            if w.on("scalar"):
                w.wait(f"w{slot}", w.at(f"w{slot}"))
                w.wait("h", w.at("h"))
                w.wait("o", w.at("o"))
                for a in range(HC):
                    last = w.eng.activation(hT[:, par, a, :], psH[:, par, a, :], GELU, bias=b1t[:, slot, a:a + 1])
                last.then_inc(sems["he"], 1)
            w.inc("he")

        def down(w, j, slot, later):
            par = slot % 2
            if w.on("tensor"):
                w.wait("he", w.at("he", later))
                w.wait("od", w.at("od", 1))
                for a in range(HC):
                    last = w.eng.matmul(psO[:, par, 0:D], hT[:, par, a, :], w2[:, slot, a, :], start=a == 0, stop=a == HC - 1)
                last.then_inc(sems["o"], 1)
            w.inc("o")
            if w.on("vector"):
                w.wait("o", w.at("o"))
                w.wait(f"st{par}", w.at(f"st{par}"))
                w.wait(f"w{slot}", w.at(f"w{slot}"))
                w.eng.tensor_tensor(ob[:, par, :], psO[:, par, 0:D], b2t[:, slot, :], ALU.add).then_inc(sems["od"], 1)
            w.inc("od")
            if w.on("sync"):
                row = w.fixed(j * P)
                w.waits(("od", w.at("od")))
                w.eng.dma_start(os[bass.ds(row, P), :], ob[:, par, :]).then_inc(sems[f"st{par}"], 16)
            w.inc(f"st{par}", 16)

        def tile(w, j, slot, left=SLOTS):
            par = slot % 2
            if left >= 1:
                up(w, (slot + 1) % SLOTS)
            if left >= 2:
                turn(w, par)
            if left >= 3:
                load(w, j + 3, 1 - par)
            down(w, j, slot, 1 if left else 0)
            if left >= SLOTS:
                fetch(w, j + SLOTS, slot)

        def walk(w):
            load(w, 0, 0)
            load(w, 1, 1)
            for j in range(SLOTS):
                fetch(w, j, j)
            turn(w, 0)
            load(w, 2, 0)
            turn(w, 1)
            up(w, 0, 1)
            for j in range(SLOTS):
                tile(w, j, j)
            w.loop(w.eng, NJ // SLOTS - 2, lambda i: [tile(w, SLOTS * i + SLOTS + k, k) for k in range(SLOTS)])
            for j in range(NJ - SLOTS, NJ):
                tile(w, j, j % SLOTS, NJ - 1 - j)
            if w.role == "sync":
                for n in ("st0", "st1"):
                    w.wait(n, w.at(n))

        @block.sync
        def _(eng):
            walk(Writer(nc, eng, "sync", {**sems, "w": sems["cst"]}, weights=2))

        @block.gpsimd
        def _(eng):
            make_identity(eng, ident, sems["cst"])
            eng.memset(one[:, :], 1.0).then_inc(sems["cst"], 1)
            eng.wait_ge(sems["cst"], 3)
            walk(Writer(nc, eng, "gpsimd", sems))

        @block.vector
        def _(eng):
            walk(Writer(nc, eng, "vector", sems))

        @block.scalar
        def _(eng):
            eng.preload_act_table(GELU)
            walk(Writer(nc, eng, "scalar", sems))

        @block.tensor
        def _(eng):
            eng.wait_ge(sems["cst"], 2)
            walk(Writer(nc, eng, "tensor", sems))


def add_experts(nc, X, score, pos, os):
    NT = X.shape[1]
    with ExitStack() as ctx:
        m = Room(nc, ctx, "n")
        at = m.sb("at", [P, 2], I32)
        og = m.sb("og", [P, 2, D])
        res = m.sb("res", [P, 2, D])
        bst = m.sb("bst", [P, 2, 6])
        mv = m.sb("mv", [P, 2, 2])
        rstd = m.sb("rstd", [P, 2, 2])
        mhalf = m.sb("mhalf", [P, 1])
        eps = m.sb("eps", [P, 1])
        idle = m.sb("idle", [1, 1])
        one = m.sb("one", [1, 1])
        idlep = m.sb("idlep", [1, 1])
        sems = {n: m.sem(n) for n in ("cst", "cp", "id", "g0", "g1", "sum", "dv", "var", "pl", "rstd", "y")}
        block = ctx.enter_context(nc.Block())

        def gather(w, t, par):
            if w.on("gpsimd"):
                w.wait("sum", w.at("sum"))
                w.eng.tensor_copy(at[:, par:par + 1], pos[:, bass.ds(t, 1)]).then_inc(sems["cp"], 1)
                w.wait("cp", w.at("cp", -1))
                w.wait("id", w.at("id"))
                w.eng.tensor_tensor(idlep[:, :], one[:, :], one[:, :], ALU.add).then_inc(sems["id"], 1)
                w.eng.indirect_dma_start(og[:, par, :], None, os, bass.IndirectOffsetOnAxis(ap=at[:, par:par + 1], axis=0))\
                    .then_inc(sems[f"g{par}"], 16)
            w.inc("cp")
            w.inc("id")
            w.inc(f"g{par}", 16)

        def add(w, t, par):
            if w.on("vector"):
                w.wait(f"g{par}", w.at(f"g{par}"))
                w.wait("y", w.at("y"))
                w.eng.scalar_tensor_tensor(out=res[:, par, :], in0=og[:, par, :], scalar=score[:, bass.ds(t, 1)],
                                           in1=X[:, bass.ds(t, 1), :].rearrange("p t c -> p (t c)"),
                                           op0=ALU.mult, op1=ALU.add).then_inc(sems["sum"], 1)
                w.wait("sum", w.at("sum", -1))
                w.link(w.eng.bn_stats(bst[:, par, :], res[:, par, :]), "dv")
                w.eng.memset(idle[:, :], 0.0)
                w.eng.bn_aggr(mv[:, par, :], bst[:, par, :]).then_inc(sems["var"], 1)
            else:
                w.inc("dv")
            w.inc("sum")
            w.inc("var")
            if w.on("gpsimd"):
                w.wait("var", w.at("var"))
                w.link(w.eng.tensor_tensor(rstd[:, par, 0:1], mv[:, par, 1:2], eps[:, :], ALU.add), "pl")
                w.eng.tensor_tensor(rstd[:, par, 1:2], rstd[:, par, 0:1], mhalf[:, :], ALU.pow).then_inc(sems["rstd"], 1)
            else:
                w.inc("pl")
            w.inc("rstd")

        def normed(w, t, par, later):
            if w.on("vector"):
                w.wait("rstd", w.at("rstd", later))
                w.eng.tensor_scalar(X[:, bass.ds(t, 1), :].rearrange("p t c -> p (t c)"), res[:, par, :],
                                    mv[:, par, 0:1], rstd[:, par, 1:2], ALU.subtract, ALU.mult).then_inc(sems["y"], 1)
            w.inc("y")

        def tile(w, t, par, first=False, more=True):
            add(w, t, par)
            if more:
                gather(w, t + 2, par)
            if not first:
                normed(w, t - 1, 1 - par, 1)

        def walk(w):
            gather(w, 0, 0)
            gather(w, 1, 1)
            tile(w, 0, 0, first=True)
            tile(w, 1, 1)
            w.loop(w.eng, NT // 2 - 2, lambda i: (tile(w, 2 * i + 2, 0), tile(w, 2 * i + 3, 1)))
            tile(w, NT - 2, 0, more=False)
            tile(w, NT - 1, 1, more=False)
            normed(w, NT - 1, 1, 0)

        @block.gpsimd
        def _(eng):
            eng.memset(mhalf[:, :], -0.5).then_inc(sems["cst"], 1)
            eng.memset(eps[:, :], EPS).then_inc(sems["cst"], 1)
            eng.memset(one[:, :], 1.0).then_inc(sems["cst"], 1)
            eng.wait_ge(sems["cst"], 3)
            walk(Writer(nc, eng, "gpsimd", sems))

        @block.vector
        def _(eng):
            walk(Writer(nc, eng, "vector", sems))


def two_layers(nc, a, out):
    B, TK, _ = a["ctx"].shape
    TOK = a["x"].shape[0]
    NT = TOK // P
    E = a["L0_ffn_W1"].shape[0]
    y = nc.dram_tensor("y_scratch", (TOK, D), F32, kind="Internal").ap()
    NJ = (NT + E - 1 + 3) // 4 * 4
    sorted_in, sorted_out = (nc.dram_tensor(n, (NJ * P, D), F32, kind="Internal").ap() for n in ("sorted_in", "sorted_out"))
    weights = nc.dram_tensor("weights_scratch", (B, TOK // B), F32, kind="Internal").ap()
    layer0_self_attention(nc, a["x"], a["wqT"], a["wkT"], a["wvT"], a["woT"], y)
    with nc.sbuf_tensor("X", [P, NT, D], F32) as X, nc.sbuf_tensor("xT", [P, 2, TOK], F32) as xT, \
            nc.sbuf_tensor("gates", [P, NT, E], F32) as gates, nc.sbuf_tensor("chosen", [P, NT, 1], F32) as chosen, \
            nc.sbuf_tensor("score", [P, NT], F32) as score, nc.sbuf_tensor("pos", [P, NT], I32) as pos, \
            nc.sbuf_tensor("rows", [P, NJ, 2], I32) as rows:

        load_tokens(nc, y, X, "l")
        cross_attention(nc, "c0", X, a["ctx"], *[a["L0_xattn_" + n] for n in ("Wq", "bq", "Wk", "bk", "Wv", "bv", "Wo", "bo")],
                        a["mask"])
        turn_tokens(nc, "t0", X, xT)
        expert_gates(nc, xT, a["L0_ffn_w_red"], a["L0_ffn_wg"], gates)
        route_tokens(nc, gates, score, pos, rows)
        sort_tokens(nc, X, pos, sorted_in)
        expert_mlps(nc, sorted_in, rows, *[a["L0_ffn_" + n] for n in ("W1", "b1", "W2", "b2")], sorted_out)
        add_experts(nc, X, score, pos, sorted_out)

        turn_tokens(nc, "t1", X, xT)
        layer1_self_attention(nc, X, xT, *[a["L1_attn_" + n] for n in ("W_qkv", "b_qkv", "W_out", "b_out")], B)
        cross_attention(nc, "c1", X, a["ctx"], *[a["L1_xattn_" + n] for n in ("Wq", "bq", "Wk", "bk", "Wv", "bv", "Wo", "bo")],
                        None)
        turn_tokens(nc, "t2", X, xT)
        choose_tokens(nc, xT, a["L1_ffn_w_r"], a["L1_ffn_b_r"], weights, TOK // B // 2, chosen)
        chosen_mlp(nc, X, xT, chosen, *[a["L1_ffn_" + n] for n in ("W1", "b1", "W2", "b2")], out)


def kernel(**inputs):
    import numpy as np
    import concourse.bacc as _bacc
    from concourse import mybir as _mybir
    from concourse.bass_utils import run_bass_kernel_spmd as _run

    i = {n: np.asarray(v) for n, v in inputs.items()}
    shape = i["x"].shape
    d = shape[-1]
    data = {"x": i["x"].reshape(-1, d), "ctx": i["ctx_1024"], "mask": i["mask_BxS2_bk0"].reshape(-1).view(np.int32)}
    data["wqT"], data["wkT"], data["woT"] = (i["L0_attn_" + n].T for n in ("wq", "wk", "wo"))
    data["wvT"] = i["L0_attn_wv"].T.reshape(d, 4, 2, 2, 64).transpose(0, 2, 3, 1, 4).reshape(d, -1)
    for n in ("Wq", "bq", "Wo", "bo"):
        data["L0_xattn_" + n] = i["L0_xattn_" + n]
    for k, n in enumerate("kv"):
        data["L0_xattn_W" + n] = i["L0_xattn_Wkv"][:, k * d:(k + 1) * d]
        data["L0_xattn_b" + n] = i["L0_xattn_bkv"][k * d:(k + 1) * d]
    for k, n in enumerate("qkv"):
        data["L1_xattn_W" + n] = i["L1_xattn_in_proj_weight"][:, k * d:(k + 1) * d]
        data["L1_xattn_b" + n] = i["L1_xattn_in_proj_bias"][k * d:(k + 1) * d]
    data["L1_xattn_Wo"], data["L1_xattn_bo"] = i["L1_xattn_out_proj_weight"], i["L1_xattn_out_proj_bias"]
    for n in ("w_red", "wg", "W1", "b1", "W2", "b2"):
        data["L0_ffn_" + n] = i["L0_ffn_" + n]
    for n in ("W_qkv", "b_qkv", "W_out", "b_out"):
        data["L1_attn_" + n] = i["L1_attn_" + n]
    for n in ("w_r", "b_r", "W1", "b1", "W2", "b2"):
        data["L1_ffn_" + n] = i["L1_ffn_" + n]

    nc = _bacc.Bacc("TRN2", target_bir_lowering=False, num_devices=1)
    data = {n: np.ascontiguousarray(v) for n, v in data.items()}
    args = {n: nc.dram_tensor(n, v.shape, _mybir.dt.from_np(v.dtype), kind="ExternalInput").ap() for n, v in data.items()}
    out = nc.dram_tensor("out", (shape[0] * shape[1], d), _mybir.dt.float32, kind="ExternalOutput").ap()
    two_layers(nc, args, out)
    r = _run(nc, [data], core_ids=[0])
    return r.results[0]["out"].reshape(shape)
```
